# Optimizing a Trainium2 kernel written in Bass

```python
import numpy as np
import jax
import jax.numpy as jnp

def _softmax(x, axis=-1):
    return jax.nn.softmax(x, axis=axis)

def _gelu(x):
    return jax.nn.gelu(x, approximate=True)

def _silu(x):
    return jax.nn.silu(x)

def _sigmoid(x):
    return jax.nn.sigmoid(x)

def _layernorm(x, axis=-1, eps=1e-05):
    m = jnp.mean(x, axis=axis, keepdims=True)
    v = jnp.var(x, axis=axis, keepdims=True)
    return (x - m) / jnp.sqrt(v + eps)

def _scatter_add(tgt, idx, src, axis=0):
    return tgt.at[idx].add(src)

def _segment_sum(src, seg, n):
    return jax.ops.segment_sum(src, seg, n)
kernel_name = 'mk_flamingo_gated_d2_seqx_r4_45cee2'

def setup_inputs(seed: int=0):
    np.random.seed(seed)
    _w = jnp.asarray

    def _rec_inputs():
        import jax
        import jax.numpy as jnp
        _rk = jax.random.key(seed)
        x = -0.0002928 + 1 * jax.random.normal(jax.random.fold_in(_rk, 1), (8, 256, 256), jnp.float32)
        _lenS = 256 - jax.random.randint(jax.random.fold_in(_rk, 7), (8,), 0, max(1, 256 // 4) + 1, jnp.int32)
        _lenS2 = 77 - jax.random.randint(jax.random.fold_in(_rk, 8), (8,), 0, max(1, 77 // 4) + 1, jnp.int32)
        _ctx_1024P = jax.random.normal(jax.random.fold_in(_rk, 11), (8, 16, 256), jnp.float32)
        _ctx_1024c = jax.random.dirichlet(jax.random.fold_in(_rk, 511), 0.3 * jnp.ones((16,), jnp.float32), (8, 77))
        _ctx_1024t = jnp.einsum('bsk,bkd->bsd', _ctx_1024c, _ctx_1024P)
        _ctx_1024t = _ctx_1024t * jax.lax.rsqrt(jnp.mean(jnp.square(_ctx_1024t)) + 1e-12) * 0.953939
        ctx_1024 = -1.39393e-06 + 0.999914 * (_ctx_1024t + 0.3 * jax.random.normal(jax.random.fold_in(_rk, 611), (8, 77, 256), jnp.float32))
        _g = jax.random.normal(jax.random.fold_in(_rk, 9001), (2, 2), jnp.float32)
        _g = jnp.sign(_g) * jnp.maximum(jnp.abs(_g), 1.0) + (_g == 0) * 1.0
        g_xattn = _g[0]
        g_ffn = _g[1]
        return (x, ctx_1024, g_xattn, g_ffn)
    x, ctx_1024, g_xattn, g_ffn = _rec_inputs()

    def _L0_xattn_setup():
        import jax, jax.numpy as jnp
        import numpy as np
        D_MODEL = 256
        N_HEAD = 16
        HEAD_DIM = D_MODEL // N_HEAD

        def _split_heads(x):
            B, S, _ = x.shape
            return x.reshape(B, S, N_HEAD, HEAD_DIM).transpose(0, 2, 1, 3)
        key = jax.random.key(seed)
        ks = jax.random.split(key, 11)
        B, S = (2, 512)
        scale = 1.0 / np.sqrt(D_MODEL)
        inp = {'q': jax.random.normal(ks[0], (B, S, D_MODEL), dtype=jnp.float32), 'k': jax.random.normal(ks[1], (B, S, D_MODEL), dtype=jnp.float32), 'v': jax.random.normal(ks[2], (B, S, D_MODEL), dtype=jnp.float32), 'Wq': jax.random.normal(ks[3], (D_MODEL, D_MODEL), dtype=jnp.float32) * scale, 'bq': jnp.zeros((D_MODEL,), dtype=jnp.float32), 'Wk': jax.random.normal(ks[4], (D_MODEL, D_MODEL), dtype=jnp.float32) * scale, 'bk': jnp.zeros((D_MODEL,), dtype=jnp.float32), 'Wv': jax.random.normal(ks[5], (D_MODEL, D_MODEL), dtype=jnp.float32) * scale, 'bv': jnp.zeros((D_MODEL,), dtype=jnp.float32), 'Wo': jax.random.normal(ks[6], (D_MODEL, D_MODEL), dtype=jnp.float32) * scale, 'bo': jnp.zeros((D_MODEL,), dtype=jnp.float32)}
        return inp
    _L0_xattn_all = _L0_xattn_setup()
    _L0_xattn_in = {k: v for k, v in _L0_xattn_all.items() if k in ('Wq', 'bq', 'Wk', 'bk', 'Wv', 'bv', 'Wo', 'bo')}
    del _L0_xattn_all

    def _L0_ffn_setup():
        import jax, jax.numpy as jnp
        import numpy as np
        import math
        D = 256
        H = 16
        E = 8
        TOPK = 2
        LAT = D // 2
        KPH = LAT // H
        HD = D // H

        def _forward(hs, q_w, q_b, k_w, k_b, v_w, v_b, o_w, o_b, router_w, router_b, w1, b1, w2, b2):
            B, S, _ = hs.shape
            Q = (hs @ q_w + q_b).reshape(B, S, H, HD).transpose(0, 2, 1, 3)
            K = (hs @ k_w + k_b).reshape(B, S, H, KPH).transpose(0, 2, 1, 3)
            V = (hs @ v_w + v_b).reshape(B, S, H, KPH).transpose(0, 2, 1, 3)
            scores = jnp.einsum('bhsk,bhtk->bhst', Q[..., :KPH], K) / math.sqrt(KPH)
            attn = jax.nn.softmax(scores, axis=-1)
            ao = jnp.einsum('bhst,bhtv->bhsv', attn, V)
            ao = ao.transpose(0, 2, 1, 3).reshape(B, S, H * KPH)
            ao = jnp.concatenate([ao, jnp.zeros((B, S, D - LAT), ao.dtype)], axis=-1)
            mla_out = ao @ o_w + o_b
            probs = jax.nn.softmax(mla_out @ router_w + router_b, axis=-1)
            topw, topi = jax.lax.top_k(probs, TOPK)
            topw = topw / (topw.sum(-1, keepdims=True) + 1e-08)
            combine = jnp.sum(jax.nn.one_hot(topi, E, dtype=probs.dtype) * topw[..., None], axis=-2)
            h1 = jnp.einsum('bsd,edf->ebsf', mla_out, w1) + b1[:, None, None, :]
            h1 = jax.nn.gelu(h1, approximate=False)
            h2 = jnp.einsum('ebsf,efd->ebsd', h1, w2) + b2[:, None, None, :]
            moe_out = jnp.einsum('bse,ebsd->bsd', combine, h2)
            return hs + 0.3 * moe_out
        key = jax.random.key(seed)
        ks = jax.random.split(key, 16)
        s = 0.02
        inp = {'hidden_states': jax.random.normal(ks[0], (2, 512, D), jnp.float32), 'q_w': jax.random.normal(ks[1], (D, D), jnp.float32) * s, 'q_b': jnp.zeros((D,), jnp.float32), 'k_w': jax.random.normal(ks[2], (D, LAT), jnp.float32) * s, 'k_b': jnp.zeros((LAT,), jnp.float32), 'v_w': jax.random.normal(ks[3], (D, LAT), jnp.float32) * s, 'v_b': jnp.zeros((LAT,), jnp.float32), 'o_w': jax.random.normal(ks[4], (D, D), jnp.float32) * s, 'o_b': jnp.zeros((D,), jnp.float32), 'router_w': jax.random.normal(ks[5], (D, E), jnp.float32) * s, 'router_b': jnp.zeros((E,), jnp.float32), 'w1': jax.random.normal(ks[6], (E, D, 2 * D), jnp.float32) * s, 'b1': jnp.zeros((E, 2 * D), jnp.float32), 'w2': jax.random.normal(ks[7], (E, 2 * D, D), jnp.float32) * s, 'b2': jnp.zeros((E, D), jnp.float32)}
        return inp
    _L0_ffn_all = _L0_ffn_setup()
    _L0_ffn_in = {k: v for k, v in _L0_ffn_all.items() if k in ('q_w', 'q_b', 'k_w', 'k_b', 'v_w', 'v_b', 'o_w', 'o_b', 'router_w', 'router_b', 'w1', 'b1', 'w2', 'b2')}
    del _L0_ffn_all

    def _L1_xattn_setup():
        import jax, jax.numpy as jnp
        import numpy as np
        DIM = 256
        HEADS = 16
        DIM_HEAD = 64
        INNER = HEADS * DIM_HEAD
        MLP = 1024
        EPS = 1e-05

        def _layernorm(x, g, b):
            mu = jnp.mean(x, axis=-1, keepdims=True)
            var = jnp.mean(jnp.square(x - mu), axis=-1, keepdims=True)
            return (x - mu) * jax.lax.rsqrt(var + EPS) * g + b

        def _l2norm(x):
            n = jnp.sqrt(jnp.sum(jnp.square(x), axis=-1, keepdims=True))
            return x / jnp.maximum(n, 1e-12)

        def _split_heads(x, B, N):
            return x.reshape(B, N, HEADS, DIM_HEAD).transpose(0, 2, 1, 3)
        key = jax.random.key(seed)
        ks = jax.random.split(key, 16)
        B, N = (4, 512)
        s = 0.02
        return {'Q': jax.random.normal(ks[0], (B, N, DIM), jnp.float32), 'K': jax.random.normal(ks[1], (B, N, DIM), jnp.float32), 'V': jax.random.normal(ks[2], (B, N, DIM), jnp.float32), 'wq': jax.random.normal(ks[3], (DIM, INNER), jnp.float32) * s, 'wk': jax.random.normal(ks[4], (DIM, INNER), jnp.float32) * s, 'wv': jax.random.normal(ks[5], (DIM, INNER), jnp.float32) * s, 'wo': jax.random.normal(ks[6], (INNER, DIM), jnp.float32) * s, 'bo': jnp.zeros((DIM,), jnp.float32), 'w1': jax.random.normal(ks[7], (DIM, MLP), jnp.float32) * s, 'b1': jnp.zeros((MLP,), jnp.float32), 'w2': jax.random.normal(ks[8], (MLP, DIM), jnp.float32) * s, 'b2': jnp.zeros((DIM,), jnp.float32), 'ln1_g': jnp.ones((DIM,), jnp.float32), 'ln1_b': jnp.zeros((DIM,), jnp.float32), 'ln2_g': jnp.ones((DIM,), jnp.float32), 'ln2_b': jnp.zeros((DIM,), jnp.float32)}
    _L1_xattn_all = _L1_xattn_setup()
    _L1_xattn_in = {k: v for k, v in _L1_xattn_all.items() if k in ('wq', 'wk', 'wv', 'wo', 'bo', 'w1', 'b1', 'w2', 'b2', 'ln1_g', 'ln1_b', 'ln2_g', 'ln2_b')}
    del _L1_xattn_all

    def _L1_ffn_setup():
        import jax, jax.numpy as jnp
        import numpy as np
        EMBED_DIM = 256
        HIDDEN = 4 * EMBED_DIM
        BATCH, SEQ = (4, 1024)
        EPS = 1e-05

        def _quant_weight(w):
            s = jnp.clip(jnp.mean(jnp.abs(w)), EPS, None)
            wq = jnp.clip(jnp.round(w / s), -1.0, 1.0) * s
            return w + jax.lax.stop_gradient(wq - w)

        def _quant_act(x):
            scale = 127.0 / jnp.clip(jnp.max(jnp.abs(x), axis=-1, keepdims=True), EPS, None)
            xq = jnp.clip(jnp.round(x * scale), -128.0, 127.0) / scale
            return x + jax.lax.stop_gradient(xq - x)

        def _bitlinear(x, w):
            return jnp.einsum('bsi,oi->bso', _quant_act(x), _quant_weight(w))
        key = jax.random.key(seed)
        k1, k2, k3 = jax.random.split(key, 3)
        x = jax.random.normal(k1, (BATCH, SEQ, EMBED_DIM), dtype=jnp.float32)
        w1 = jax.random.normal(k2, (HIDDEN, EMBED_DIM), dtype=jnp.float32) * (1.0 / np.sqrt(EMBED_DIM))
        w2 = jax.random.normal(k3, (EMBED_DIM, HIDDEN), dtype=jnp.float32) * (1.0 / np.sqrt(HIDDEN))
        return {'x': x, 'w1': w1, 'w2': w2}
    _L1_ffn_all = _L1_ffn_setup()
    _L1_ffn_in = {k: v for k, v in _L1_ffn_all.items() if k in ('w1', 'w2')}
    del _L1_ffn_all
    return {'x': x, 'ctx_1024': ctx_1024, 'g_xattn': g_xattn, 'g_ffn': g_ffn, 'L0_xattn_Wq': _L0_xattn_in['Wq'], 'L0_xattn_bq': _L0_xattn_in['bq'], 'L0_xattn_Wk': _L0_xattn_in['Wk'], 'L0_xattn_bk': _L0_xattn_in['bk'], 'L0_xattn_Wv': _L0_xattn_in['Wv'], 'L0_xattn_bv': _L0_xattn_in['bv'], 'L0_xattn_Wo': _L0_xattn_in['Wo'], 'L0_xattn_bo': _L0_xattn_in['bo'], 'L0_ffn_q_w': _L0_ffn_in['q_w'], 'L0_ffn_q_b': _L0_ffn_in['q_b'], 'L0_ffn_k_w': _L0_ffn_in['k_w'], 'L0_ffn_k_b': _L0_ffn_in['k_b'], 'L0_ffn_v_w': _L0_ffn_in['v_w'], 'L0_ffn_v_b': _L0_ffn_in['v_b'], 'L0_ffn_o_w': _L0_ffn_in['o_w'], 'L0_ffn_o_b': _L0_ffn_in['o_b'], 'L0_ffn_router_w': _L0_ffn_in['router_w'], 'L0_ffn_router_b': _L0_ffn_in['router_b'], 'L0_ffn_w1': _L0_ffn_in['w1'], 'L0_ffn_b1': _L0_ffn_in['b1'], 'L0_ffn_w2': _L0_ffn_in['w2'], 'L0_ffn_b2': _L0_ffn_in['b2'], 'L1_xattn_wq': _L1_xattn_in['wq'], 'L1_xattn_wk': _L1_xattn_in['wk'], 'L1_xattn_wv': _L1_xattn_in['wv'], 'L1_xattn_wo': _L1_xattn_in['wo'], 'L1_xattn_bo': _L1_xattn_in['bo'], 'L1_xattn_w1': _L1_xattn_in['w1'], 'L1_xattn_b1': _L1_xattn_in['b1'], 'L1_xattn_w2': _L1_xattn_in['w2'], 'L1_xattn_b2': _L1_xattn_in['b2'], 'L1_xattn_ln1_g': _L1_xattn_in['ln1_g'], 'L1_xattn_ln1_b': _L1_xattn_in['ln1_b'], 'L1_xattn_ln2_g': _L1_xattn_in['ln2_g'], 'L1_xattn_ln2_b': _L1_xattn_in['ln2_b'], 'L1_ffn_w1': _L1_ffn_in['w1'], 'L1_ffn_w2': _L1_ffn_in['w2']}

def reference(x, ctx_1024, g_xattn, g_ffn, L0_xattn_Wq, L0_xattn_bq, L0_xattn_Wk, L0_xattn_bk, L0_xattn_Wv, L0_xattn_bv, L0_xattn_Wo, L0_xattn_bo, L0_ffn_q_w, L0_ffn_q_b, L0_ffn_k_w, L0_ffn_k_b, L0_ffn_v_w, L0_ffn_v_b, L0_ffn_o_w, L0_ffn_o_b, L0_ffn_router_w, L0_ffn_router_b, L0_ffn_w1, L0_ffn_b1, L0_ffn_w2, L0_ffn_b2, L1_xattn_wq, L1_xattn_wk, L1_xattn_wv, L1_xattn_wo, L1_xattn_bo, L1_xattn_w1, L1_xattn_b1, L1_xattn_w2, L1_xattn_b2, L1_xattn_ln1_g, L1_xattn_ln1_b, L1_xattn_ln2_g, L1_xattn_ln2_b, L1_ffn_w1, L1_ffn_w2):
    import jax
    import jax.numpy as jnp

    def _L0_xattn_ref(q, k, v, Wq, bq, Wk, bk, Wv, bv, Wo, bo):
        import jax, jax.numpy as jnp
        import numpy as np
        D_MODEL = 256
        N_HEAD = 16
        HEAD_DIM = D_MODEL // N_HEAD

        def _split_heads(x):
            B, S, _ = x.shape
            return x.reshape(B, S, N_HEAD, HEAD_DIM).transpose(0, 2, 1, 3)
        B, S, _ = q.shape
        qh = _split_heads(q @ Wq + bq)
        kh = _split_heads(k @ Wk + bk)
        vh = _split_heads(v @ Wv + bv)
        inv_sqrt_d = jnp.asarray(1.0 / np.sqrt(HEAD_DIM), dtype=q.dtype)
        scores = jnp.einsum('bhqd,bhkd->bhqk', qh, kh) * inv_sqrt_d
        attn = jax.nn.softmax(scores, axis=-1)
        out = jnp.einsum('bhqk,bhkd->bhqd', attn, vh)
        out = out.transpose(0, 2, 1, 3).reshape(B, S, D_MODEL)
        return out @ Wo + bo

    def _L0_ffn_ref(hidden_states, q_w, q_b, k_w, k_b, v_w, v_b, o_w, o_b, router_w, router_b, w1, b1, w2, b2):
        import jax, jax.numpy as jnp
        import numpy as np
        import math
        D = 256
        H = 16
        E = 8
        TOPK = 2
        LAT = D // 2
        KPH = LAT // H
        HD = D // H

        def _forward(hs, q_w, q_b, k_w, k_b, v_w, v_b, o_w, o_b, router_w, router_b, w1, b1, w2, b2):
            B, S, _ = hs.shape
            Q = (hs @ q_w + q_b).reshape(B, S, H, HD).transpose(0, 2, 1, 3)
            K = (hs @ k_w + k_b).reshape(B, S, H, KPH).transpose(0, 2, 1, 3)
            V = (hs @ v_w + v_b).reshape(B, S, H, KPH).transpose(0, 2, 1, 3)
            scores = jnp.einsum('bhsk,bhtk->bhst', Q[..., :KPH], K) / math.sqrt(KPH)
            attn = jax.nn.softmax(scores, axis=-1)
            ao = jnp.einsum('bhst,bhtv->bhsv', attn, V)
            ao = ao.transpose(0, 2, 1, 3).reshape(B, S, H * KPH)
            ao = jnp.concatenate([ao, jnp.zeros((B, S, D - LAT), ao.dtype)], axis=-1)
            mla_out = ao @ o_w + o_b
            probs = jax.nn.softmax(mla_out @ router_w + router_b, axis=-1)
            topw, topi = jax.lax.top_k(probs, TOPK)
            topw = topw / (topw.sum(-1, keepdims=True) + 1e-08)
            combine = jnp.sum(jax.nn.one_hot(topi, E, dtype=probs.dtype) * topw[..., None], axis=-2)
            h1 = jnp.einsum('bsd,edf->ebsf', mla_out, w1) + b1[:, None, None, :]
            h1 = jax.nn.gelu(h1, approximate=False)
            h2 = jnp.einsum('ebsf,efd->ebsd', h1, w2) + b2[:, None, None, :]
            moe_out = jnp.einsum('bse,ebsd->bsd', combine, h2)
            return hs + 0.3 * moe_out
        return _forward(hidden_states, q_w, q_b, k_w, k_b, v_w, v_b, o_w, o_b, router_w, router_b, w1, b1, w2, b2)

    def _L1_xattn_ref(Q, K, V, wq, wk, wv, wo, bo, w1, b1, w2, b2, ln1_g, ln1_b, ln2_g, ln2_b):
        import jax, jax.numpy as jnp
        import numpy as np
        DIM = 256
        HEADS = 16
        DIM_HEAD = 64
        INNER = HEADS * DIM_HEAD
        MLP = 1024
        EPS = 1e-05

        def _layernorm(x, g, b):
            mu = jnp.mean(x, axis=-1, keepdims=True)
            var = jnp.mean(jnp.square(x - mu), axis=-1, keepdims=True)
            return (x - mu) * jax.lax.rsqrt(var + EPS) * g + b

        def _l2norm(x):
            n = jnp.sqrt(jnp.sum(jnp.square(x), axis=-1, keepdims=True))
            return x / jnp.maximum(n, 1e-12)

        def _split_heads(x, B, N):
            return x.reshape(B, N, HEADS, DIM_HEAD).transpose(0, 2, 1, 3)
        B, Nq, _ = Q.shape
        Nk = K.shape[1]
        Qn = _layernorm(Q, ln1_g, ln1_b)
        Kn = _layernorm(K, ln1_g, ln1_b)
        Vn = _layernorm(V, ln1_g, ln1_b)
        q = _split_heads(Qn @ wq, B, Nq)
        k = _split_heads(Kn @ wk, B, Nk)
        v = _split_heads(Vn @ wv, B, Nk)
        qn = _l2norm(q)
        kn = _l2norm(k)
        attn = jnp.einsum('bhqd,bhkd->bhqk', qn, kn)
        out = jnp.einsum('bhqk,bhkd->bhqd', attn, v)
        out = out.transpose(0, 2, 1, 3).reshape(B, Nq, INNER)
        x = Q + out @ wo + bo
        xn = _layernorm(x, ln2_g, ln2_b)
        h = jax.nn.gelu(xn @ w1 + b1, approximate=False)
        return x + h @ w2 + b2

    def _L1_ffn_ref(x, w1, w2):
        import jax, jax.numpy as jnp
        import numpy as np
        EMBED_DIM = 256
        HIDDEN = 4 * EMBED_DIM
        BATCH, SEQ = (4, 1024)
        EPS = 1e-05

        def _quant_weight(w):
            s = jnp.clip(jnp.mean(jnp.abs(w)), EPS, None)
            wq = jnp.clip(jnp.round(w / s), -1.0, 1.0) * s
            return w + jax.lax.stop_gradient(wq - w)

        def _quant_act(x):
            scale = 127.0 / jnp.clip(jnp.max(jnp.abs(x), axis=-1, keepdims=True), EPS, None)
            xq = jnp.clip(jnp.round(x * scale), -128.0, 127.0) / scale
            return x + jax.lax.stop_gradient(xq - x)

        def _bitlinear(x, w):
            return jnp.einsum('bsi,oi->bso', _quant_act(x), _quant_weight(w))
        h = jax.nn.gelu(_bitlinear(x, w1), approximate=False)
        return _bitlinear(h, w2)
    x = x + jnp.tanh(g_xattn[0]) * _L0_xattn_ref(_layernorm(x, axis=-1), ctx_1024, ctx_1024, L0_xattn_Wq, L0_xattn_bq, L0_xattn_Wk, L0_xattn_bk, L0_xattn_Wv, L0_xattn_bv, L0_xattn_Wo, L0_xattn_bo)
    x = x + jnp.tanh(g_ffn[0]) * _L0_ffn_ref(_layernorm(x, axis=-1), L0_ffn_q_w, L0_ffn_q_b, L0_ffn_k_w, L0_ffn_k_b, L0_ffn_v_w, L0_ffn_v_b, L0_ffn_o_w, L0_ffn_o_b, L0_ffn_router_w, L0_ffn_router_b, L0_ffn_w1, L0_ffn_b1, L0_ffn_w2, L0_ffn_b2)
    x = x + jnp.tanh(g_xattn[1]) * _L1_xattn_ref(_layernorm(x, axis=-1), ctx_1024, ctx_1024, L1_xattn_wq, L1_xattn_wk, L1_xattn_wv, L1_xattn_wo, L1_xattn_bo, L1_xattn_w1, L1_xattn_b1, L1_xattn_w2, L1_xattn_b2, L1_xattn_ln1_g, L1_xattn_ln1_b, L1_xattn_ln2_g, L1_xattn_ln2_b)
    x = x + jnp.tanh(g_ffn[1]) * _L1_ffn_ref(_layernorm(x, axis=-1), L1_ffn_w1, L1_ffn_w2)
    return x

_drawn_inputs = setup_inputs


def setup_inputs(seed=0):
    import zlib

    import numpy as np

    out = dict(_drawn_inputs(seed))
    spreads = {'g_ffn': (-1.0, 0.6),
     'L0_xattn_bq': (0.0, 0.441),
     'L0_xattn_bk': (0.0, 2.0),
     'L0_xattn_bv': (0.0, 0.1),
     'L0_xattn_bo': (0.0, 0.1),
     'L0_ffn_q_b': (0.0, 0.8),
     'L0_ffn_k_b': (0.0, 2.0),
     'L0_ffn_v_b': (0.0, 0.532),
     'L0_ffn_o_b': (0.0, 0.1),
     'L0_ffn_router_b': (0.0, 0.1),
     'L0_ffn_b1': (0.0, 0.622),
     'L0_ffn_b2': (0.0, 0.483),
     'L1_xattn_bo': (0.0, 0.1),
     'L1_xattn_b1': (0.0, 0.1),
     'L1_xattn_b2': (0.0, 0.1),
     'L1_xattn_ln1_g': (1.0, 0.2),
     'L1_xattn_ln1_b': (0.0, 0.1),
     'L1_xattn_ln2_g': (1.0, 0.6),
     'L1_xattn_ln2_b': (0.0, 0.61)}
    factors = {'L0_ffn_q_w': 8.0,
     'L0_ffn_k_w': 8.0,
     'L0_ffn_v_w': 5.267,
     'L0_ffn_o_w': 5.289,
     'L0_ffn_w1': 8.0,
     'L0_ffn_w2': 4.527}
    for name, (base, spread) in spreads.items():
        noise = np.random.default_rng([zlib.crc32(name.encode()), seed]).standard_normal(out[name].shape)
        drawn = base * np.exp(spread * noise) if base else spread * noise
        out[name] = jnp.asarray(drawn.astype(out[name].dtype))
    for name, factor in factors.items():
        out[name] = (out[name] * factor).astype(out[name].dtype)
    return out
```

```python
import concourse.bass as bass
from concourse import mybir
from contextlib import ExitStack

F32 = mybir.dt.float32
BF16 = mybir.dt.bfloat16
I32 = mybir.dt.int32
U32 = mybir.dt.uint32
ALU = mybir.AluOpType
ACT = mybir.ActivationFunctionType
X = mybir.AxisListType.X

P = 128
B, S, D = 8, 256, 256
SC = 77
H = 16
TPB = S // P
NT = B * TPB
KD = D // P
GR = 4
CH = H // GR
E, F0 = 8, 512
TOPK = 2
INNER = 1024
HD1 = INNER // H
FF = 1024
SLOT_TILES = NT * TOPK + E
EPS = 1e-5
ROUND = 1.5 * 2.0 ** 23


def program(nc, t, out):
    ctx = ExitStack()
    with ctx:
        def sb(name, shape, dt=F32):
            return ctx.enter_context(nc.sbuf_tensor(name, shape, dt))

        def sem(name):
            return ctx.enter_context(nc.semaphore(name))

        x_slots = nc.dram_tensor("x_slots", [SLOT_TILES * P, D], F32, kind="Internal").ap()
        y_slots = nc.dram_tensor("y_slots", [SLOT_TILES * P, D], F32, kind="Internal").ap()

        ps = ctx.enter_context(nc.psum_tensor("ps", [P, 8, 512], F32))

        def banks(b, n, shape):
            flat = ps[:, b:b + n, :].rearrange("p b n -> p (b n)")
            return flat

        x = sb("x", [P, NT, D])
        ident = sb("ident", [P, P])
        ident16 = sb("ident16", [P, P], BF16)
        ones = sb("ones", [P, P])
        before = sb("before", [P, P])
        gates = sb("gates", [P, 4])
        minus_half = sb("minus_half", [P, H])
        stats = sb("stats", [P, 3, 6])
        mv = sb("mv", [P, 3, 2])
        var = sb("var", [P, 3])
        rstd = sb("rstd", [P, 3])
        route_i = sb("route_i", [P, NT, TOPK], U32)
        route_w = sb("route_w", [P, NT, TOPK])

        layers = {}

        s_x = sem("s_x")
        s_gate = sem("s_gate")
        s_const = sem("s_const")
        s_ones = sem("s_ones")
        with nc.Block() as block:
            @block.sync
            def _(sp):
                sp.dma_start(x[:, :, :], t["x"].rearrange("b (t p) d -> p (b t) d", p=P)).then_inc(s_x, 16)
                for i, g in enumerate(("g_xattn", "g_ffn")):
                    for j in range(2):
                        sp.dma_start(gates[:, 2 * j + i:2 * j + i + 1],
                                     t[g][j:j + 1].partition_broadcast(P)).then_inc(s_gate, 16)
                sp.wait_ge(s_x, 16)

            @block.gpsimd
            def _(pool):
                pool.memset(ident[:, :], 0.0)
                pool.memset(ident16[:, :], 0.0)
                pool.memset(ones[:, :], 1.0)
                pool.memset(before[:, :], 1.0)
                pool.memset(minus_half[:, :], -0.5)
                pool.drain()
                pool.affine_select(out=ident[:, :], in_=ident[:, :], compare_op=ALU.not_equal, fill=1.0,
                                   base=0, pattern=[[-1, P]], channel_multiplier=1)
                pool.affine_select(out=ident16[:, :], in_=ident16[:, :], compare_op=ALU.not_equal, fill=1.0,
                                   base=0, pattern=[[-1, P]], channel_multiplier=1)
                pool.affine_select(out=before[:, :], in_=before[:, :], compare_op=ALU.is_gt, fill=0.0,
                                   base=0, pattern=[[1, P]], channel_multiplier=-1)

            @block.scalar
            def _(act):
                act.wait_ge(s_gate, 64)
                act.activation(gates[:, :], gates[:, :], ACT.Tanh)

        def softmax_attention(tag, hd, NK, KC, cross, rest):
            VD = H * hd
            OK = VD // P
            scale = float(hd) ** -0.5
            R = CH * KC // 2
            st = ExitStack()

            def tb(name, shape, dt=F32):
                return st.enter_context(nc.sbuf_tensor(tag + name, shape, dt))

            def ts(name):
                return sem(tag + name)

            wq = tb("wq", [P, KD, CH * P])
            wk = tb("wk", [P, KD, CH * P])
            wv = tb("wv", [P, KD, VD])
            wo = tb("wo", [P, OK, D])
            bq = tb("bq", [P, CH])
            bk = tb("bk", [P, CH])
            bv = tb("bv", [P, VD])
            bo = tb("bo", [P, D])
            xn = tb("xn", [P, TPB, D]) if cross else None
            xnT = tb("xnT", [P, KD, S])
            src = tb("src", [P, D]) if cross else None
            srcT = tb("srcT", [P, KD, NK]) if cross else xnT
            q = tb("q", [P, CH, S])
            k = tb("k", [P, CH, NK * KC])
            v = tb("v", [P, KC, H, hd + 1])
            negmax = tb("negmax", [P, TPB, CH, P])
            pt = tb("pt", [P, 2, GR, 2, S])
            rsum = tb("rsum", [P, TPB, H])
            ao = tb("ao", [P, TPB, VD])
            aoT = tb("aoT", [P, OK, S])
            tmp = tb("tmp", [P, TPB, D])
            if not cross:
                mo, hln, rw, rb, moT, logits, zeros = rest
            s_w = ts("s_w")
            s_src = ts("s_src")
            s_var = ts("s_var")
            s_rstd = ts("s_rstd")
            s_xn = ts("s_xn")
            s_xT = ts("s_xT")
            s_xTe = ts("s_xTe")
            s_srcT = ts("s_srcT")
            s_srcTe = ts("s_srcTe")
            s_q = ts("s_q")
            s_qe = ts("s_qe")
            s_k = ts("s_k")
            s_ke = ts("s_ke")
            s_v = ts("s_v")
            s_ve = ts("s_ve")
            s_max = ts("s_max")
            s_maxe = ts("s_maxe")
            s_mT = ts("s_mT")
            s_q2 = ts("s_q2")
            s_sc = ts("s_sc")
            s_exp = ts("s_exp")
            s_pv = ts("s_pv")
            s_ao = ts("s_ao")
            s_aoT = ts("s_aoT")
            s_aoTe = ts("s_aoTe")
            s_o = ts("s_o")
            s_oe = ts("s_oe")
            s_moT = ts("s_moT")
            s_moTe = ts("s_moTe")
            s_lg = ts("s_lg")
            s_lge = ts("s_lge")
            s_zero = ts("s_zero")

            def flat(b, n, w, parts=P):
                return ps[0:parts, b:b + n, :].rearrange("p b n -> p (b n)")[:, 0:w]

            xT_ps = flat(0, 1, KD * S).rearrange("p (k s) -> p k s", k=KD)
            srcT_ps = flat(1, 1, KD * NK).rearrange("p (k s) -> p k s", k=KD)
            q_ps = flat(2, 2, CH * S).rearrange("p (c s) -> p c s", c=CH)
            k_ps = flat(0, 2, CH * NK * KC).rearrange("p (c s) -> p c s", c=CH)
            v_ps = flat(4, 1, KC * VD).rearrange("p (k n) -> p k n", k=KC)
            mT_ps = flat(0, 2, CH * S).rearrange("p (c s) -> p c s", c=CH)
            pv_ps = ps[:, 0:TPB, 0:H * (hd + 1)].rearrange("p t (h e) -> p t h e", h=H)
            aoT_ps = flat(2, 1, OK * S).rearrange("p (k s) -> p k s", k=OK)
            o_ps = flat(3, 1, TPB * D).rearrange("p (t d) -> p t d", t=TPB)
            moT_ps = flat(0, 1, KD * S).rearrange("p (k s) -> p k s", k=KD)
            lg_ps = ps[:, 1, 0:TPB * E].rearrange("p (t e) -> p t e", t=TPB)

            def max_ps(m):
                b = 4 * (m % 2)
                return ps[:, b:b + GR, 0:2 * NK * KC].rearrange("p g (c n) -> p g c n", c=2)

            def slot(r, j):
                return (2 * r + j, 0) if KC == 1 else (r, j)

            with st, nc.Block() as block:
                @block.sync
                def _(sp):
                    names = [(wq, tag + "wq"), (wk, tag + "wk"), (wv, tag + "wv"), (wo, tag + "wo")]
                    for dst, n in names:
                        sp.dma_start(dst[:, :, :], t[n].rearrange("(k p) n -> p k n", p=P)).then_inc(s_w, 16)
                    for dst, n in ((bq, tag + "bq"), (bk, tag + "bk")):
                        sp.dma_start(dst[:, :], t[n]).then_inc(s_w, 16)
                    for dst, n in ((bv, tag + "bv"), (bo, tag + "bo")):
                        sp.dma_start(dst[:, :], t[n].partition_broadcast(P)).then_inc(s_w, 16)
                    if cross:
                        sp.sem_inc(s_srcTe, 1)
                        with sp.Fori(0, B) as i:
                            sp.wait_ge(s_srcTe, i + 1)
                            sp.dma_start(src[0:SC, :], t["ctx"][bass.ds(i, 1)].rearrange("a s d -> (a s) d"))\
                                .then_inc(s_src, 16)
                    else:
                        sp.dma_start(rw[:, :, :], t["router_w"].rearrange("(k p) n -> p k n", p=P)).then_inc(s_w, 16)
                        sp.dma_start(rb[:, :], t["router_b"].partition_broadcast(P)).then_inc(s_w, 16)
                        sp.wait_ge(s_zero, 1)
                        with sp.Fori(0, SLOT_TILES // 8) as i:
                            sp.dma_start(x_slots.rearrange("(i a p) d -> i p a d", a=8, p=P)[bass.ds(i, 1)]
                                         .rearrange("i p a d -> (i p) a d"),
                                         zeros[:, :].unsqueeze(1).to_broadcast([P, 8, D])).then_inc(s_src, 16)
                        sp.wait_ge(s_src, 16 * (SLOT_TILES // 8))

                @block.gpsimd
                def _(pool):
                    if not cross:
                        pool.memset(zeros[:, :], 0.0).then_inc(s_zero, 1)
                    with pool.Fori(0, B) as i:
                        pool.wait_ge(s_var, i + 1)
                        pool.tensor_tensor(rstd[:, 0:TPB], var[:, 0:TPB], minus_half[:, 0:TPB], ALU.pow)\
                            .then_inc(s_rstd, 1)

                @block.vector
                def _(dve):
                    dve.memset(v[:, :, :, :], 1.0)
                    dve.memset(negmax[:, :, :, :], 0.0)
                    dve.wait_ge(s_w, 16 * (8 if cross else 10))
                    with dve.Fori(0, B) as i:
                        for tt in range(TPB):
                            dve.bn_stats(stats[:, tt, :], x[:, bass.ds(TPB * i + tt, 1), :])
                        dve.drain()
                        for tt in range(TPB):
                            dve.bn_aggr(mv[:, tt, :], stats[:, tt, :])
                        dve.drain()
                        dve.tensor_scalar(var[:, 0:TPB], mv[:, 0:TPB, 1], EPS, None, ALU.add).then_inc(s_var, 1)
                        dve.wait_ge(s_rstd, i + 1)
                        for tt in range(TPB):
                            dst = xn[:, tt:tt + 1, :] if cross else hln[:, bass.ds(TPB * i + tt, 1), :]
                            ins = dve.tensor_scalar(dst, x[:, bass.ds(TPB * i + tt, 1), :],
                                                    mv[:, tt, 0:1], rstd[:, tt:tt + 1], ALU.subtract, ALU.mult)
                            if not cross:
                                dve.drain()
                                ins = dve.tensor_copy(tmp[:, tt:tt + 1, :], dst)
                            ins.then_inc(s_xn, 1)
                        dve.wait_ge(s_k, i + 1)
                        dve.tensor_tensor(k[:, :, :], k_ps, bk[:, :].unsqueeze(2).to_broadcast([P, CH, NK * KC]),
                                          ALU.add).then_inc(s_ke, 1)
                        dve.wait_ge(s_v, i + 1)
                        for kc in range(KC):
                            ins = dve.tensor_tensor(v[0:NK, kc, :, 0:hd],
                                                    v_ps[0:NK, kc, :].rearrange("p (h e) -> p h e", h=H),
                                                    bv[0:NK, :].rearrange("p (h e) -> p h e", h=H), ALU.add)
                        ins.then_inc(s_ve, 1)
                        for m in range(4):
                            tt, cp = m // 2, m % 2
                            dve.wait_ge(s_max, 4 * i + m + 1)
                            dst = negmax[:, tt, 2 * cp:2 * cp + 2, :].rearrange(
                                "p c (g r) -> p g c r", g=GR)[:, :, :, hd]
                            dve.tensor_reduce(dst, max_ps(m), X, ALU.max, negate=True).then_inc(s_maxe, 1)
                        dve.wait_ge(s_mT, i + 1)
                        dve.wait_ge(s_qe, i + 1)
                        dve.tensor_tensor(q[:, :, :], q[:, :, :], mT_ps, ALU.add).then_inc(s_q2, 1)
                        dve.wait_ge(s_pv, i + 1)
                        dve.reciprocal(rsum[:, :, :], pv_ps[:, :, :, hd])
                        dve.drain()
                        for tt in range(TPB):
                            ins = dve.tensor_tensor(ao[:, tt, :].rearrange("p (h e) -> p h e", h=H),
                                                    pv_ps[:, tt, :, 0:hd],
                                                    rsum[:, tt, :].unsqueeze(2).to_broadcast([P, H, hd]), ALU.mult)
                        ins.then_inc(s_ao, 1)
                        dve.wait_ge(s_o, i + 1)
                        xb = x[:, bass.ds(TPB * i, TPB), :]
                        bob = bo[:, :].unsqueeze(1).to_broadcast([P, TPB, D])
                        if cross:
                            dve.tensor_tensor(tmp[:, :, :], o_ps, bob, ALU.add)
                            dve.drain()
                            dve.scalar_tensor_tensor(xb, tmp[:, :, :], gates[:, 0:1], xb, ALU.mult, ALU.add)\
                                .then_inc(s_oe, 1)
                            dve.drain()
                        else:
                            dve.tensor_tensor(tmp[:, :, :], o_ps, bob, ALU.add).then_inc(s_oe, 1)
                            dve.drain()
                            dve.tensor_copy(mo[:, bass.ds(TPB * i, TPB), :], tmp[:, :, :])
                            dve.wait_ge(s_lg, i + 1)
                            dve.tensor_tensor(logits[:, bass.ds(TPB * i, TPB), :], lg_ps,
                                              rb[:, :].unsqueeze(1).to_broadcast([P, TPB, E]), ALU.add)\
                                .then_inc(s_lge, 1)
                            dve.drain()

                @block.scalar
                def _(act):
                    act.wait_ge(s_w, 16 * (8 if cross else 10))
                    with act.Fori(0, B) as i:
                        act.wait_ge(s_xT, i + 1)
                        act.activation(xnT[:, :, :], xT_ps, ACT.Copy).then_inc(s_xTe, 1)
                        if cross:
                            act.wait_ge(s_srcT, i + 1)
                            act.activation(srcT[:, :, :], srcT_ps, ACT.Copy).then_inc(s_srcTe, 1)
                        act.wait_ge(s_q, i + 1)
                        for c in range(CH):
                            ins = act.activation(q[:, c, :], q_ps[:, c, :], ACT.Identity, bias=bq[:, c:c + 1])
                        ins.then_inc(s_qe, 1)
                        for r in range(R):
                            act.wait_ge(s_sc, R * i + r + 1)
                            act.activation(pt[0:NK, r % 2, :, :, :].rearrange("p g j s -> p (g j s)"),
                                           ps[0:NK, 4:8, :].rearrange("p g n -> p (g n)"),
                                           ACT.Exp, scale=scale).then_inc(s_exp, 1)
                        act.wait_ge(s_aoT, i + 1)
                        act.activation(aoT[:, :, :], aoT_ps, ACT.Copy).then_inc(s_aoTe, 1)
                        if not cross:
                            act.wait_ge(s_moT, i + 1)
                            act.activation(moT[:, :, :], moT_ps, ACT.Copy).then_inc(s_moTe, 1)

                @block.tensor
                def _(pe):
                    pe.wait_ge(s_w, 16 * (8 if cross else 10))
                    toks = xn if cross else tmp

                    def pv(i, r):
                        pe.wait_ge(s_exp, R * i + r + 1)
                        for j in range(2):
                            c, kc = slot(r, j)
                            for g in range(GR):
                                h = c * GR + g
                                for tt in range(TPB):
                                    if KC == 2:
                                        if j == 1:
                                            continue
                                        for kk in range(2):
                                            ins = pe.matmul(pv_ps[:, tt, h, :],
                                                            pt[0:NK, r % 2, g, kk, tt * P:(tt + 1) * P],
                                                            v[0:NK, kk, h, :], start=(kk == 0), stop=(kk == 1))
                                    else:
                                        ins = pe.matmul(pv_ps[:, tt, h, :],
                                                        pt[0:NK, r % 2, g, j, tt * P:(tt + 1) * P],
                                                        v[0:NK, 0, h, :], start=True, stop=True)
                        return ins

                    with pe.Fori(0, B) as i:
                        pe.wait_ge(s_xn, TPB * i + TPB)
                        for tt in range(TPB):
                            for kd in range(KD):
                                ins = pe.transpose(xT_ps[:, kd, tt * P:(tt + 1) * P],
                                                   toks[:, tt, kd * P:(kd + 1) * P], ident[:, :])
                        ins.then_inc(s_xT, 1)
                        if cross:
                            pe.wait_ge(s_src, 16 * i + 16)
                            for kd in range(KD):
                                ins = pe.transpose(srcT_ps[:, kd, :], src[0:SC, kd * P:(kd + 1) * P],
                                                   ident[0:SC, 0:SC])
                            ins.then_inc(s_srcT, 1)
                        pe.wait_ge(s_xTe, i + 1)
                        for c in range(CH):
                            for kd in range(KD):
                                ins = pe.matmul(q_ps[:, c, :], wq[:, kd, c * P:(c + 1) * P], xnT[:, kd, :],
                                                start=(kd == 0), stop=(kd == KD - 1))
                        ins.then_inc(s_q, 1)
                        if cross:
                            pe.wait_ge(s_srcTe, i + 2)
                        for c in range(CH):
                            for kd in range(KD):
                                ins = pe.matmul(k_ps[:, c, :], wk[:, kd, c * P:(c + 1) * P], srcT[:, kd, :],
                                                start=(kd == 0), stop=(kd == KD - 1))
                        ins.then_inc(s_k, 1)
                        for kc in range(KC):
                            for kd in range(KD):
                                ins = pe.matmul(v_ps[0:NK, kc, :], srcT[:, kd, kc * NK:(kc + 1) * NK],
                                                wv[:, kd, :], start=(kd == 0), stop=(kd == KD - 1))
                        ins.then_inc(s_v, 1)
                        pe.wait_ge(s_qe, i + 1)
                        pe.wait_ge(s_ke, i + 1)
                        for m in range(4):
                            tt, cp = m // 2, m % 2
                            if m == 1:
                                pe.wait_ge(s_ve, i + 1)
                            if m >= 2:
                                pe.wait_ge(s_maxe, 4 * i + m - 1)
                            for cc in range(2):
                                for g in range(GR):
                                    c, rows = 2 * cp + cc, slice(32 * g, 32 * g + hd)
                                    ins = pe.matmul(max_ps(m)[:, g, cc, :], q[rows, c, tt * P:(tt + 1) * P],
                                                    k[rows, c, :], start=True, stop=True)
                            ins.then_inc(s_max, 1)
                        pe.wait_ge(s_maxe, 4 * i + 4)
                        for tt in range(TPB):
                            for c in range(CH):
                                ins = pe.transpose(mT_ps[:, c, tt * P:(tt + 1) * P], negmax[:, tt, c, :],
                                                   ident[:, :])
                        ins.then_inc(s_mT, 1)
                        pe.wait_ge(s_q2, i + 1)
                        for r in range(R):
                            if r:
                                pe.wait_ge(s_exp, R * i + r)
                            for j in range(2):
                                c, kc = slot(r, j)
                                for g in range(GR):
                                    rows = slice(32 * g, 32 * g + hd + 1)
                                    ins = pe.matmul(ps[0:NK, 4 + g, j * S:(j + 1) * S],
                                                    k[rows, c, kc * NK:(kc + 1) * NK], q[rows, c, :],
                                                    start=True, stop=True)
                            ins.then_inc(s_sc, 1)
                            if r:
                                pv(i, r - 1)
                        pv(i, R - 1).then_inc(s_pv, 1)
                        pe.wait_ge(s_ao, i + 1)
                        for tt in range(TPB):
                            for kd in range(OK):
                                ins = pe.transpose(aoT_ps[:, kd, tt * P:(tt + 1) * P],
                                                   ao[:, tt, kd * P:(kd + 1) * P], ident[:, :])
                        ins.then_inc(s_aoT, 1)
                        pe.wait_ge(s_aoTe, i + 1)
                        for tt in range(TPB):
                            for kd in range(OK):
                                ins = pe.matmul(o_ps[:, tt, :], aoT[:, kd, tt * P:(tt + 1) * P], wo[:, kd, :],
                                                start=(kd == 0), stop=(kd == OK - 1))
                        ins.then_inc(s_o, 1)
                        if not cross:
                            pe.wait_ge(s_oe, i + 1)
                            for tt in range(TPB):
                                for kd in range(KD):
                                    ins = pe.transpose(moT_ps[:, kd, tt * P:(tt + 1) * P],
                                                       tmp[:, tt, kd * P:(kd + 1) * P], ident[:, :])
                            ins.then_inc(s_moT, 1)
                            pe.wait_ge(s_moTe, i + 1)
                            for tt in range(TPB):
                                for kd in range(KD):
                                    ins = pe.matmul(lg_ps[:, tt, :], moT[:, kd, tt * P:(tt + 1) * P],
                                                    rw[:, kd, :], start=(kd == 0), stop=(kd == KD - 1))
                            ins.then_inc(s_lg, 1)
                        pe.wait_ge(s_oe, i + 1)

        softmax_attention("a_", D // H, SC, 1, True, None)

        moe = ExitStack()
        with moe:
            def mb(name, shape, dt=F32):
                return moe.enter_context(nc.sbuf_tensor(name, shape, dt))

            hln = mb("hln", [P, NT, D])
            expert_of = mb("expert_of", [1, SLOT_TILES], I32)
            with nc.sbuf_tensor("mo", [P, NT, D], F32) as mo, nc.sbuf_tensor("logits", [P, NT, E], F32) as logits:
                with nc.sbuf_tensor("rw", [P, KD, E], F32) as rw, nc.sbuf_tensor("rb", [P, E], F32) as rb, \
                        nc.sbuf_tensor("moT", [P, KD, S], F32) as moT, nc.sbuf_tensor("zeros", [P, D], F32) as zeros:
                    softmax_attention("b_", D // 2 // H, P, TPB, False, (mo, hln, rw, rb, moT, logits, zeros))
                route(nc, sem, ps, ones, before, mo, logits, route_i, route_w, expert_of, x_slots)
            experts(nc, sem, ps, t, ident, expert_of, x_slots, y_slots)
            cosine_layer(nc, sem, ps, t, x, hln, ident, minus_half, gates, stats, mv, var, rstd,
                         route_i, route_w, y_slots)
        ternary_layer(nc, sem, ps, t, x, ident, ident16, ones, minus_half, gates, stats, mv, var, rstd, out)


def route(nc, sem, ps, ones, before, mo, logits, route_i, route_w, expert_of, x_slots):
    st = ExitStack()

    def tb(name, shape, dt=F32):
        return st.enter_context(nc.sbuf_tensor("r_" + name, shape, dt))

    prob = tb("prob", [P, NT, E])
    red = tb("red", [P, NT])
    rec = tb("rec", [P, NT])
    top = tb("top", [P, NT, 8])
    topi = tb("topi", [P, NT, 8], U32)
    topf = tb("topf", [P, NT, TOPK])
    iota_e = tb("iota_e", [P, E])
    iota_s = tb("iota_s", [1, SLOT_TILES])
    one_hot = tb("one_hot", [P, TOPK, NT, E])
    both = tb("both", [P, NT, E])
    total = tb("total", [P, E, NT])
    upto = tb("upto", [P, E, NT])
    tiles = tb("tiles", [P, E])
    tend = tb("tend", [P, E])
    base = tb("base", [P, E])
    place = tb("place", [P, NT, E])
    pick = tb("pick", [P, TOPK, NT, E])
    pos = tb("pos", [P, TOPK, NT])
    passed = tb("passed", [1, SLOT_TILES, E])
    npass = tb("npass", [1, SLOT_TILES])
    idx = tb("idx", [P, TOPK], U32)
    s_iota = sem("r_iota")
    s_max = sem("r_max")
    s_exp = sem("r_exp")
    s_one = sem("r_one")
    s_cnt = sem("r_cnt")
    s_pos = sem("r_pos")
    s_idx = sem("r_idx")
    s_sent = sem("r_sent")
    rank_ps = ps[:, 0, 0:NT * E].rearrange("p (t e) -> p t e", t=NT)
    total_ps = ps[:, 1, 0:NT * E].rearrange("p (t e) -> p e t", t=NT)
    ones_nt = ones[:, 0:NT]

    def over_experts(a):
        return a.unsqueeze(2).to_broadcast([P, NT, E])

    with st, nc.Block() as block:
        @block.gpsimd
        def _(pool):
            pool.iota(iota_e[:, :], [[1, E]], base=0, channel_multiplier=0, allow_small_or_imprecise_dtypes=True)
            pool.iota(iota_s[:, :], [[1, SLOT_TILES]], base=0, channel_multiplier=0,
                      allow_small_or_imprecise_dtypes=True).then_inc(s_iota, 1)
            pool.wait_ge(s_pos, 1)
            for tt in range(NT):
                for j in range(TOPK):
                    pool.indirect_dma_start(x_slots[:, :], bass.IndirectOffsetOnAxis(route_i[:, tt, j:j + 1], axis=0),
                                            mo[:, tt, :], None).then_inc(s_sent, 16)
            pool.wait_ge(s_sent, 16 * NT * TOPK)

        @block.scalar
        def _(act):
            act.wait_ge(s_max, 1)
            act.activation(prob[:, :, :], prob[:, :, :], ACT.Exp).then_inc(s_exp, 1)

        @block.tensor
        def _(pe):
            pe.wait_ge(s_one, 1)
            rhs = both[:, :, :].rearrange("p t e -> p (t e)")
            pe.matmul(ps[:, 0, 0:NT * E], before[:, :], rhs, start=True, stop=True)
            pe.matmul(ps[:, 1, 0:NT * E], ones[:, :], rhs, start=True, stop=True).then_inc(s_cnt, 1)

        @block.vector
        def _(dve):
            dve.tensor_reduce(red[:, :], logits[:, :, :], X, ALU.max)
            dve.drain()
            dve.tensor_tensor(prob[:, :, :], logits[:, :, :], over_experts(red[:, :]), ALU.subtract).then_inc(s_max, 1)
            dve.wait_ge(s_exp, 1)
            dve.tensor_reduce(red[:, :], prob[:, :, :], X, ALU.add)
            dve.drain()
            dve.reciprocal(rec[:, :], red[:, :])
            dve.drain()
            dve.tensor_tensor(prob[:, :, :], prob[:, :, :], over_experts(rec[:, :]), ALU.mult)
            dve.drain()
            for tt in range(NT):
                dve.max(top[:, tt, :], prob[:, tt, :])
            dve.drain()
            for tt in range(NT):
                dve.max_index(topi[:, tt, :], top[:, tt, :], prob[:, tt, :])
            dve.drain()
            dve.tensor_reduce(red[:, :], top[:, :, 0:TOPK], X, ALU.add)
            dve.tensor_copy(topf[:, :, :], topi[:, :, 0:TOPK])
            dve.drain()
            dve.tensor_scalar(red[:, :], red[:, :], 1e-8, None, ALU.add)
            dve.wait_ge(s_iota, 1)
            for j in range(TOPK):
                dve.tensor_tensor(one_hot[:, j, :, :], over_experts(topf[:, :, j]),
                                  iota_e[:, :].unsqueeze(1).to_broadcast([P, NT, E]), ALU.is_equal)
            dve.drain()
            dve.reciprocal(rec[:, :], red[:, :])
            dve.tensor_tensor(both[:, :, :], one_hot[:, 0, :, :], one_hot[:, 1, :, :], ALU.add).then_inc(s_one, 1)
            dve.drain()
            dve.tensor_tensor(route_w[:, :, :], top[:, :, 0:TOPK],
                              rec[:, :].unsqueeze(2).to_broadcast([P, NT, TOPK]), ALU.mult)
            dve.wait_ge(s_cnt, 1)
            dve.tensor_copy(total[:, :, :], total_ps)
            dve.drain()
            for e in range(E):
                dve.tensor_tensor_scan(upto[:, e, :], ones_nt, total[:, e, :], 0.0, ALU.mult, ALU.add)
            dve.drain()
            dve.tensor_scalar(tiles[:, :], upto[:, :, NT - 1], 127.0, 1.0 / P, ALU.add, ALU.mult)
            dve.drain()
            dve.tensor_scalar(tiles[:, :], tiles[:, :], -127.0 / 256, ROUND, ALU.add, ALU.add)
            dve.drain()
            dve.tensor_scalar(tiles[:, :], tiles[:, :], -ROUND, None, ALU.add)
            dve.drain()
            dve.tensor_tensor_scan(tend[:, :], ones[:, 0:E], tiles[:, :], 0.0, ALU.mult, ALU.add)
            dve.drain()
            dve.tensor_tensor(base[:, :], tend[:, :], tiles[:, :], ALU.subtract)
            dve.tensor_tensor(upto[:, :, :], upto[:, :, :], total[:, :, :], ALU.subtract)
            dve.tensor_tensor(passed[:, :, :], iota_s[:, :].unsqueeze(2).to_broadcast([1, SLOT_TILES, E]),
                              tend[0:1, :].unsqueeze(1).to_broadcast([1, SLOT_TILES, E]), ALU.is_ge)
            dve.drain()
            dve.tensor_tensor(place[:, :, :], rank_ps, upto[:, :, :].rearrange("p e t -> p t e"), ALU.add)
            dve.tensor_reduce(npass[:, :], passed[:, :, :], X, ALU.add)
            dve.tensor_scalar(base[:, :], base[:, :], float(P), None, ALU.mult)
            dve.drain()
            dve.tensor_scalar(npass[:, :], npass[:, :], float(E - 1), None, ALU.min)
            dve.tensor_tensor(place[:, :, :], place[:, :, :], base[:, :].unsqueeze(1).to_broadcast([P, NT, E]),
                              ALU.add)
            dve.drain()
            dve.tensor_copy(expert_of[:, :], npass[:, :])
            for j in range(TOPK):
                dve.tensor_tensor(pick[:, j, :, :], one_hot[:, j, :, :], place[:, :, :], ALU.mult)
            dve.drain()
            for j in range(TOPK):
                dve.tensor_reduce(pos[:, j, :], pick[:, j, :, :], X, ALU.add)
            dve.drain()
            dve.tensor_copy(route_i[:, :, :], pos[:, :, :].rearrange("p j t -> p t j")).then_inc(s_pos, 1)


def experts(nc, sem, ps, t, ident, expert_of, x_slots, y_slots):
    st = ExitStack()

    def tb(name, shape, dt=F32):
        return st.enter_context(nc.sbuf_tensor("e_" + name, shape, dt))

    FK = F0 // P
    w1 = tb("w1", [P, E, KD, F0])
    w2 = tb("w2", [P, E, FK, D])
    b1 = tb("b1", [P, E, F0])
    b2 = tb("b2", [P, E, D])
    xs = tb("xs", [P, 2, D])
    xsT = tb("xsT", [P, 2, KD, P])
    h = tb("h", [P, 2, F0])
    hT = tb("hT", [P, 2, FK, P])
    ys = tb("ys", [P, 2, D])
    s_w = sem("e_w")
    s_in = [sem("e_in0"), sem("e_in1")]
    s_xT = sem("e_xT")
    s_xTe = sem("e_xTe")
    s_h = sem("e_h")
    s_he = sem("e_he")
    s_hT = sem("e_hT")
    s_hTe = sem("e_hTe")
    s_y = sem("e_y")
    s_ye = sem("e_ye")
    s_out = [sem("e_out0"), sem("e_out1")]
    xT_ps = [ps[:, u, 0:KD * P].rearrange("p (k s) -> p k s", k=KD) for u in range(2)]
    h_ps = [ps[:, 2 + u, :] for u in range(2)]
    hT_ps = [ps[:, 4 + u, :].rearrange("p (k s) -> p k s", k=FK) for u in range(2)]
    y_ps = [ps[:, 6 + u, 0:D] for u in range(2)]
    xv = x_slots.rearrange("(i p) d -> i p d", p=P)
    yv = y_slots.rearrange("(i p) d -> i p d", p=P)
    N = SLOT_TILES // 2

    with st, nc.Block() as block:
        @block.sync
        def _(sp):
            sp.dma_start(w1[:, :, :, :], t["moe_w1"].rearrange("e (k p) f -> p e k f", p=P)).then_inc(s_w, 16)
            sp.dma_start(b1[:, :, :].rearrange("p e f -> p (e f)"),
                         t["moe_b1"].rearrange("e f -> (e f)").partition_broadcast(P)).then_inc(s_w, 16)
            sp.dma_start(w2[:, :, :, :], t["moe_w2"].rearrange("e (k p) f -> p e k f", p=P)).then_inc(s_w, 16)
            sp.dma_start(b2[:, :, :].rearrange("p e f -> p (e f)"),
                         t["moe_b2"].rearrange("e f -> (e f)").partition_broadcast(P)).then_inc(s_w, 16)
            sp.sem_inc(s_ye, 2)
            sp.sem_inc(s_out[0], 16)
            sp.sem_inc(s_out[1], 16)
            with sp.Fori(0, N) as i:
                for u in range(2):
                    sp.wait_ge(s_ye, 2 * i + u + 3)
                    sp.dma_start(yv[bass.ds(2 * i + u, 1)].rearrange("a p d -> (a p) d"), ys[:, u, :])\
                        .then_inc(s_out[u], 16)
            for u in range(2):
                sp.wait_ge(s_out[u], 16 * (N + 1))

        @block.gpsimd
        def _(pool):
            pool.sem_inc(s_xT, 2)
            with pool.Fori(0, N) as i:
                for u in range(2):
                    pool.wait_ge(s_xT, 2 * i + u + 1)
                    pool.dma_start(xs[:, u, :], xv[bass.ds(2 * i + u, 1)].rearrange("a p d -> (a p) d"))\
                        .then_inc(s_in[u], 16)

        @block.tensor
        def _(pe):
            pe.wait_ge(s_w, 64)
            with pe.Fori(0, N) as i:
                e = [pe.value_load(expert_of[0:1, bass.ds(2 * i + u, 1)], min_val=0, max_val=E - 1) for u in range(2)]
                for u in range(2):
                    pe.wait_ge(s_in[u], 16 * i + 16)
                    for kd in range(KD):
                        ins = pe.transpose(xT_ps[u][:, kd, :], xs[:, u, kd * P:(kd + 1) * P], ident[:, :])
                    ins.then_inc(s_xT, 1)
                for u in range(2):
                    pe.wait_ge(s_xTe, 2 * i + u + 1)
                    for kd in range(KD):
                        ins = pe.matmul(h_ps[u], xsT[:, u, kd, :], w1[:, bass.ds(e[u], 1), kd, :],
                                        start=(kd == 0), stop=(kd == KD - 1))
                    ins.then_inc(s_h, 1)
                for u in range(2):
                    pe.wait_ge(s_he, 2 * i + u + 1)
                    for kd in range(FK):
                        ins = pe.transpose(hT_ps[u][:, kd, :], h[:, u, kd * P:(kd + 1) * P], ident[:, :])
                    ins.then_inc(s_hT, 1)
                for u in range(2):
                    pe.wait_ge(s_hTe, 2 * i + u + 1)
                    for kd in range(FK):
                        ins = pe.matmul(y_ps[u], hT[:, u, kd, :], w2[:, bass.ds(e[u], 1), kd, :],
                                        start=(kd == 0), stop=(kd == FK - 1))
                    ins.then_inc(s_y, 1)

        @block.scalar
        def _(act):
            with act.Fori(0, N) as i:
                for u in range(2):
                    act.wait_ge(s_xT, 2 * i + u + 3)
                    act.activation(xsT[:, u, :, :], xT_ps[u], ACT.Copy).then_inc(s_xTe, 1)
                for u in range(2):
                    act.wait_ge(s_hT, 2 * i + u + 1)
                    act.activation(hT[:, u, :, :], hT_ps[u], ACT.Gelu).then_inc(s_hTe, 1)

        @block.vector
        def _(dve):
            dve.wait_ge(s_w, 64)
            with dve.Fori(0, N) as i:
                e = [dve.value_load(expert_of[0:1, bass.ds(2 * i + u, 1)], min_val=0, max_val=E - 1) for u in range(2)]
                for u in range(2):
                    dve.wait_ge(s_h, 2 * i + u + 1)
                    dve.tensor_tensor(h[:, u, :], h_ps[u], b1[:, bass.ds(e[u], 1), :]
                                      .rearrange("p a f -> p (a f)"), ALU.add).then_inc(s_he, 1)
                for u in range(2):
                    dve.wait_ge(s_y, 2 * i + u + 1)
                    dve.wait_ge(s_out[u], 16 * i + 16)
                    dve.tensor_tensor(ys[:, u, :], y_ps[u], b2[:, bass.ds(e[u], 1), :]
                                      .rearrange("p a f -> p (a f)"), ALU.add).then_inc(s_ye, 1)


def cosine_layer(nc, sem, ps, t, x, hln, ident, minus_half, gates, stats, mv, var, rstd, route_i, route_w, y_slots):
    st = ExitStack()

    def tb(name, shape, dt=F32):
        return st.enter_context(nc.sbuf_tensor("c_" + name, shape, dt))

    IK = INNER // P
    FK = FF // P
    wq = tb("wq", [P, KD, INNER])
    wk = tb("wk", [P, KD, INNER])
    wv = tb("wv", [P, KD, INNER])
    wo = tb("wo", [P, IK, D])
    w1 = tb("w1", [P, KD, FF])
    w2 = tb("w2", [P, FK, D])
    b1 = tb("b1", [P, FK])
    lnw = tb("lnw", [P, 4, KD])
    bo = tb("bo", [P, D])
    b2 = tb("b2", [P, D])
    idx = tb("idx", [P, TPB * TOPK], U32)
    yg = tb("yg", [P, TPB, TOPK, D])
    rw = tb("rw", [P, TPB, TOPK])
    mix = tb("mix", [P, TPB, D])
    xq = tb("xq", [P, TPB, D])
    xh = tb("xh", [P, TPB, D])
    xT = tb("xT", [P, KD, S])
    cx = tb("cx", [P, D])
    cT = tb("cT", [P, KD, SC])
    big = tb("big", [P, INNER])
    qn = tb("qn", [P, INNER])
    kn = tb("kn", [P, INNER])
    vv = tb("vv", [P, INNER])
    ss = tb("ss", [P, 3, H])
    rn = tb("rn", [P, 3, H])
    mT = tb("mT", [P, IK, P])
    gm = tb("gm", [P, IK, D])
    qT = tb("qT", [P, TPB, IK, P])
    hT = tb("hT", [P, FK, S])
    one = tb("one", [P, H])
    names = "w ctx gath idx var rstd xn xT xTe cn cT cTe k ks kss kr kn v ve M Me G Ge q qs qss qr qn qT qTe o oe " \
            "x2 x2T x2Te h he y ye".split()
    s = {n: sem("c_s_" + n) for n in names}

    xT_ps = ps[:, 0, :].rearrange("p (k s) -> p k s", k=KD)
    cT_ps = ps[:, 1, 0:KD * SC].rearrange("p (k s) -> p k s", k=KD)
    lo = ps[:, 2:4, :].rearrange("p b n -> p (b n)")
    hi = ps[:, 4:6, :].rearrange("p b n -> p (b n)")
    g_ps = ps[:, 4:8, :].rearrange("p b (c n) -> p (b c) n", c=2)
    o_ps = ps[:, 1, :].rearrange("p (t d) -> p t d", t=TPB)

    def heads(a):
        return a.rearrange("p (h e) -> p h e", h=H)

    with st, nc.Block() as block:
        @block.sync
        def _(sp):
            for dst, n in ((wk, "l1_wk"), (wv, "l1_wv"), (wo, "l1_wo"), (wq, "l1_wq"), (w1, "l1_w1"), (w2, "l1_w2")):
                sp.dma_start(dst[:, :, :], t[n].rearrange("(k p) n -> p k n", p=P)).then_inc(s["w"], 16)
            sp.dma_start(b1[:, :], t["l1_b1"]).then_inc(s["w"], 16)
            sp.dma_start(lnw[:, :, :], t["l1_ln"]).then_inc(s["w"], 16)
            sp.dma_start(bo[:, :], t["l1_bo"].partition_broadcast(P)).then_inc(s["w"], 16)
            sp.dma_start(b2[:, :], t["l1_b2"].partition_broadcast(P)).then_inc(s["w"], 16)
            sp.sem_inc(s["cTe"], 1)
            with sp.Fori(0, B) as i:
                sp.wait_ge(s["cTe"], i + 1)
                sp.dma_start(cx[0:SC, :], t["ctx"][bass.ds(i, 1)].rearrange("a s d -> (a s) d")).then_inc(s["ctx"], 16)

        @block.gpsimd
        def _(pool):
            with pool.Fori(0, B) as i:
                pool.tensor_copy(idx[:, :], route_i[:, bass.ds(TPB * i, TPB), :].rearrange("p t j -> p (t j)"))
                pool.drain()
                for tt in range(TPB):
                    for j in range(TOPK):
                        n = tt * TOPK + j
                        pool.indirect_dma_start(yg[:, tt, j, :], None, y_slots[:, :],
                                                bass.IndirectOffsetOnAxis(idx[:, n:n + 1], axis=0))\
                            .then_inc(s["gath"], 16)
                pool.wait_ge(s["gath"], 64 * i + 64)
                for n in range(3):
                    pool.wait_ge(s["var"], 4 * i + n + 1)
                    cols = slice(2, 3) if n == 0 else slice(0, TPB)
                    pool.tensor_tensor(rstd[:, cols], var[:, cols], minus_half[:, cols], ALU.pow).then_inc(s["rstd"], 1)
                pool.wait_ge(s["kss"], i + 1)
                pool.tensor_tensor(rn[0:SC, 2, :], ss[0:SC, 2, :], minus_half[0:SC, :], ALU.pow).then_inc(s["kr"], 1)
                for tt in range(TPB):
                    pool.wait_ge(s["qss"], TPB * i + tt + 1)
                    pool.tensor_tensor(rn[:, tt, :], ss[:, tt, :], minus_half[:, :], ALU.pow).then_inc(s["qr"], 1)
                pool.wait_ge(s["var"], 4 * i + 4)
                pool.tensor_tensor(rstd[:, 0:TPB], var[:, 0:TPB], minus_half[:, 0:TPB], ALU.pow)\
                    .then_inc(s["rstd"], 1)

        @block.vector
        def _(dve):
            dve.memset(mT[:, :, :], 0.0)
            dve.memset(var[:, :], 1.0)
            dve.wait_ge(s["w"], 160)

            def norm_stats(src, n, first):
                for tt in range(n):
                    dve.bn_stats(stats[:, first + tt, :], src(tt))
                dve.drain()
                for tt in range(n):
                    dve.bn_aggr(mv[:, first + tt, :], stats[:, first + tt, :])
                dve.drain()
                dve.tensor_scalar(var[:, first:first + n], mv[:, first:first + n, 1], EPS, None, ALU.add)\
                    .then_inc(s["var"], 1)

            with dve.Fori(0, B) as i:
                dve.wait_ge(s["ctx"], 16 * i + 16)
                dve.bn_stats(stats[0:SC, 2, :], cx[0:SC, :])
                dve.drain()
                dve.bn_aggr(mv[0:SC, 2, :], stats[0:SC, 2, :])
                dve.drain()
                dve.tensor_scalar(var[0:SC, 2:3], mv[0:SC, 2, 1:2], EPS, None, ALU.add).then_inc(s["var"], 1)
                dve.wait_ge(s["rstd"], 4 * i + 1)
                dve.tensor_scalar(cx[0:SC, :], cx[0:SC, :], mv[0:SC, 2, 0:1], rstd[0:SC, 2:3],
                                  ALU.subtract, ALU.mult).then_inc(s["cn"], 1)
                dve.wait_ge(s["gath"], 64 * i + 64)
                for tt in range(TPB):
                    dve.tensor_scalar(mix[:, tt, :], yg[:, tt, 0, :],
                                      route_w[:, bass.ds(TPB * i + tt, 1), 0], None, ALU.mult)
                dve.drain()
                for tt in range(TPB):
                    dve.scalar_tensor_tensor(mix[:, tt, :], yg[:, tt, 1, :],
                                             route_w[:, bass.ds(TPB * i + tt, 1), 1], mix[:, tt, :], ALU.mult, ALU.add)
                dve.drain()
                dve.scalar_tensor_tensor(mix[:, :, :], mix[:, :, :], 0.3, hln[:, bass.ds(TPB * i, TPB), :],
                                         ALU.mult, ALU.add)
                dve.drain()
                xb = x[:, bass.ds(TPB * i, TPB), :]
                dve.scalar_tensor_tensor(xb, mix[:, :, :], gates[:, 1:2], xb, ALU.mult, ALU.add)
                dve.drain()
                norm_stats(lambda tt: x[:, bass.ds(TPB * i + tt, 1), :], TPB, 0)
                dve.wait_ge(s["rstd"], 4 * i + 2)
                for tt in range(TPB):
                    dve.tensor_scalar(xq[:, tt:tt + 1, :], x[:, bass.ds(TPB * i + tt, 1), :], mv[:, tt, 0:1],
                                      rstd[:, tt:tt + 1], ALU.subtract, ALU.mult)
                dve.drain()
                norm_stats(lambda tt: xq[:, tt, :], TPB, 0)
                dve.wait_ge(s["rstd"], 4 * i + 3)
                for tt in range(TPB):
                    ins = dve.tensor_scalar(xh[:, tt, :], xq[:, tt, :], mv[:, tt, 0:1],
                                            rstd[:, tt:tt + 1], ALU.subtract, ALU.mult)
                ins.then_inc(s["xn"], 1)
                dve.wait_ge(s["cT"], i + 1)
                for kd in range(KD):
                    ins = dve.tensor_scalar(cT[:, kd, :], cT_ps[:, kd, :], lnw[:, 0, kd:kd + 1], lnw[:, 1, kd:kd + 1],
                                            ALU.mult, ALU.add)
                ins.then_inc(s["cTe"], 1)
                dve.wait_ge(s["xT"], i + 1)
                for kd in range(KD):
                    ins = dve.tensor_scalar(xT[:, kd, :], xT_ps[:, kd, :], lnw[:, 0, kd:kd + 1], lnw[:, 1, kd:kd + 1],
                                            ALU.mult, ALU.add)
                ins.then_inc(s["xTe"], 1)
                dve.wait_ge(s["ks"], i + 1)
                dve.tensor_reduce(ss[0:SC, 2, :], heads(big[0:SC, :]), X, ALU.add)
                dve.drain()
                dve.tensor_scalar(ss[0:SC, 2, :], ss[0:SC, 2, :], 1e-24, None, ALU.max).then_inc(s["kss"], 1)
                dve.wait_ge(s["kr"], i + 1)
                dve.tensor_tensor(heads(kn[0:SC, :]), heads(lo[0:SC, :]),
                                  rn[0:SC, 2, :].unsqueeze(2).to_broadcast([SC, H, HD1]), ALU.mult)\
                    .then_inc(s["kn"], 1)
                dve.wait_ge(s["M"], i + 1)
                for u in range(2):
                    rows = slice(64 * u, 64 * u + 64)
                    ins = dve.tensor_copy(mT[rows, :, rows], lo[rows, :].rearrange("p (c n) -> p c n", c=IK)[:, :, rows])
                ins.then_inc(s["Me"], 1)
                for tt in range(TPB):
                    dve.wait_ge(s["qs"], TPB * i + tt + 1)
                    dve.tensor_reduce(ss[:, tt, :], heads(big[:, :]), X, ALU.add)
                    dve.drain()
                    dve.tensor_scalar(ss[:, tt, :], ss[:, tt, :], 1e-24, None, ALU.max).then_inc(s["qss"], 1)
                    dve.wait_ge(s["qr"], TPB * i + tt + 1)
                    dve.tensor_tensor(heads(qn[:, :]), heads(lo),
                                      rn[:, tt, :].unsqueeze(2).to_broadcast([P, H, HD1]), ALU.mult)\
                        .then_inc(s["qn"], 1)
                dve.wait_ge(s["o"], i + 1)
                dve.tensor_tensor(xq[:, :, :], xq[:, :, :], bo[:, :].unsqueeze(1).to_broadcast([P, TPB, D]), ALU.add)
                dve.drain()
                dve.tensor_tensor(xq[:, :, :], xq[:, :, :], o_ps, ALU.add).then_inc(s["oe"], 1)
                dve.drain()
                norm_stats(lambda tt: xq[:, tt, :], TPB, 0)
                dve.wait_ge(s["rstd"], 4 * i + 4)
                for tt in range(TPB):
                    ins = dve.tensor_scalar(xh[:, tt, :], xq[:, tt, :], mv[:, tt, 0:1],
                                            rstd[:, tt:tt + 1], ALU.subtract, ALU.mult)
                ins.then_inc(s["x2"], 1)
                dve.wait_ge(s["x2T"], i + 1)
                for kd in range(KD):
                    ins = dve.tensor_scalar(xT[:, kd, :], xT_ps[:, kd, :], lnw[:, 2, kd:kd + 1], lnw[:, 3, kd:kd + 1],
                                            ALU.mult, ALU.add)
                ins.then_inc(s["x2Te"], 1)
                dve.tensor_tensor(xq[:, :, :], xq[:, :, :], b2[:, :].unsqueeze(1).to_broadcast([P, TPB, D]), ALU.add)
                dve.drain()
                dve.wait_ge(s["y"], i + 1)
                dve.tensor_tensor(xq[:, :, :], xq[:, :, :], o_ps, ALU.add).then_inc(s["ye"], 1)
                dve.drain()
                dve.scalar_tensor_tensor(xb, xq[:, :, :], gates[:, 2:3], xb, ALU.mult, ALU.add)
                dve.drain()

        @block.scalar
        def _(act):
            act.wait_ge(s["w"], 160)
            with act.Fori(0, B) as i:
                act.wait_ge(s["k"], i + 1)
                act.activation(big[0:SC, :], lo[0:SC, :], ACT.Square).then_inc(s["ks"], 1)
                act.wait_ge(s["v"], i + 1)
                act.activation(vv[0:SC, :], hi[0:SC, :], ACT.Copy).then_inc(s["ve"], 1)
                act.wait_ge(s["G"], i + 1)
                act.activation(gm[:, :, :], g_ps, ACT.Copy).then_inc(s["Ge"], 1)
                act.wait_ge(s["kss"], i + 1)
                for tt in range(TPB):
                    act.wait_ge(s["q"], TPB * i + tt + 1)
                    if tt:
                        act.wait_ge(s["qss"], TPB * i + tt)
                    act.activation(big[:, :], lo, ACT.Square).then_inc(s["qs"], 1)
                    act.wait_ge(s["qT"], TPB * i + tt + 1)
                    act.activation(qT[:, tt, :, :].rearrange("p c n -> p (c n)"), hi, ACT.Copy).then_inc(s["qTe"], 1)
                act.wait_ge(s["h"], i + 1)
                for c in range(FK):
                    ins = act.activation(hT[:, c, :], ps[:, 4 + c // 2, (c % 2) * S:(c % 2 + 1) * S], ACT.Gelu,
                                         bias=b1[:, c:c + 1])
                ins.then_inc(s["he"], 1)

        @block.tensor
        def _(pe):
            pe.wait_ge(s["w"], 160)

            def transposes(dst):
                for tt in range(TPB):
                    for kd in range(KD):
                        ins = pe.transpose(dst[:, kd, tt * P:(tt + 1) * P], xh[:, tt, kd * P:(kd + 1) * P],
                                           ident[:, :])
                return ins

            def rows(dst, lhsT, w, n):
                for half in range(INNER // 512):
                    for kd in range(KD):
                        ins = pe.matmul(dst[0:n, half * 512:(half + 1) * 512], lhsT(kd),
                                        w[:, kd, half * 512:(half + 1) * 512], start=(kd == 0), stop=(kd == KD - 1))
                return ins

            with pe.Fori(0, B) as i:
                pe.wait_ge(s["cn"], i + 1)
                for kd in range(KD):
                    ins = pe.transpose(cT_ps[:, kd, :], cx[0:SC, kd * P:(kd + 1) * P], ident[0:SC, 0:SC])
                ins.then_inc(s["cT"], 1)
                pe.wait_ge(s["xn"], i + 1)
                transposes(xT_ps).then_inc(s["xT"], 1)
                pe.wait_ge(s["cTe"], i + 2)
                rows(lo, lambda kd: cT[:, kd, :], wk, SC).then_inc(s["k"], 1)
                rows(hi, lambda kd: cT[:, kd, :], wv, SC).then_inc(s["v"], 1)
                pe.wait_ge(s["kn"], i + 1)
                pe.wait_ge(s["ve"], i + 1)
                for c in range(IK):
                    cols = slice(c * P, (c + 1) * P)
                    ins = pe.matmul(lo[:, cols], vv[0:SC, cols], kn[0:SC, cols], start=True, stop=True)
                ins.then_inc(s["M"], 1)
                pe.wait_ge(s["Me"], i + 1)
                for c in range(IK):
                    ins = pe.matmul(g_ps[:, c, :], mT[:, c, :], wo[:, c, :], start=True, stop=True)
                ins.then_inc(s["G"], 1)
                pe.wait_ge(s["xTe"], i + 1)
                for tt in range(TPB):
                    if tt:
                        pe.wait_ge(s["qn"], TPB * i + tt)
                    rows(lo, lambda kd: xT[:, kd, tt * P:(tt + 1) * P], wq, P).then_inc(s["q"], 1)
                    pe.wait_ge(s["qn"], TPB * i + tt + 1)
                    if tt == 0:
                        pe.wait_ge(s["Ge"], i + 1)
                    else:
                        pe.wait_ge(s["qTe"], TPB * i + tt)
                    for c in range(IK):
                        ins = pe.transpose(hi[:, c * P:(c + 1) * P], qn[:, c * P:(c + 1) * P], ident[:, :])
                    ins.then_inc(s["qT"], 1)
                for tt in range(TPB):
                    pe.wait_ge(s["qTe"], TPB * i + tt + 1)
                    for c in range(IK):
                        ins = pe.matmul(o_ps[:, tt, :], qT[:, tt, c, :], gm[:, c, :], start=(c == 0), stop=(c == IK - 1))
                ins.then_inc(s["o"], 1)
                pe.wait_ge(s["x2"], i + 1)
                transposes(xT_ps).then_inc(s["x2T"], 1)
                pe.wait_ge(s["x2Te"], i + 1)
                for c in range(FK):
                    for kd in range(KD):
                        ins = pe.matmul(ps[:, 4 + c // 2, (c % 2) * S:(c % 2 + 1) * S],
                                        w1[:, kd, c * P:(c + 1) * P], xT[:, kd, :],
                                        start=(kd == 0), stop=(kd == KD - 1))
                ins.then_inc(s["h"], 1)
                pe.wait_ge(s["he"], i + 1)
                for tt in range(TPB):
                    for c in range(FK):
                        ins = pe.matmul(o_ps[:, tt, :], hT[:, c, tt * P:(tt + 1) * P], w2[:, c, :],
                                        start=(c == 0), stop=(c == FK - 1))
                ins.then_inc(s["y"], 1)
                pe.wait_ge(s["ye"], i + 1)


def ternary_layer(nc, sem, ps, t, x, ident, ident16, ones, minus_half, gates, stats, mv, var, rstd, out):
    st = ExitStack()

    def tb(name, shape, dt=F32):
        return st.enter_context(nc.sbuf_tensor("d_" + name, shape, dt))

    FK = FF // P
    wf = [tb("wf1", [P, KD, FF]), tb("wf2", [P, FK, D])]
    wb = [tb("wb1", [P, KD, FF], BF16), tb("wb2", [P, FK, D], BF16)]
    neg = tb("neg", [P, KD * FF])
    part = tb("part", [P, 2])
    sw = tb("sw", [P, 2])
    half = tb("half", [P, 2, 2])
    xh = tb("xh", [P, D])
    xr = tb("xr", [P, D])
    xi = tb("xi", [P, D], BF16)
    xT = tb("xT", [P, KD, P], BF16)
    h = tb("h", [P, FF])
    hr = tb("hr", [P, FF])
    hi8 = tb("hi8", [P, FF], BF16)
    hT = tb("hT", [P, FK, P], BF16)
    am = tb("am", [P, 2])
    sc = tb("sc", [P, 2])
    un = tb("un", [P, 2])
    names = "w part sum var rstd xi xT xTe h he hi hT hTe y un store".split()
    s = {n: sem("d_s_" + n) for n in names}
    xT_ps = ps[:, 0, 0:P].bitcast(BF16).rearrange("p (k s) -> p k s", k=KD)
    sum_ps = ps[:, 1, 0:2]
    h_ps = ps[:, 2:4, :].rearrange("p b n -> p (b n)")
    hT_ps = ps[:, 4, :].bitcast(BF16).rearrange("p (k s) -> p k s", k=FK)
    y_ps = ps[:, 5, 0:D]
    ov = out.rearrange("b (t p) d -> (b t) p d", p=P)

    with st, nc.Block() as block:
        @block.sync
        def _(sp):
            sp.dma_start(wf[0][:, :, :], t["ff_w1t"].rearrange("(k p) n -> p k n", p=P)).then_inc(s["w"], 16)
            sp.dma_start(wf[1][:, :, :], t["ff_w2t"].rearrange("(k p) n -> p k n", p=P)).then_inc(s["w"], 16)
            with sp.Fori(0, NT) as i:
                sp.wait_ge(s["un"], i + 1)
                sp.dma_start(ov[bass.ds(i, 1)].rearrange("a p d -> (a p) d"),
                             x[:, bass.ds(i, 1), :].rearrange("p a d -> p (a d)")).then_inc(s["store"], 16)
            sp.wait_ge(s["store"], 16 * NT)

        @block.gpsimd
        def _(pool):
            with pool.Fori(0, NT) as i:
                pool.wait_ge(s["var"], i + 1)
                pool.tensor_tensor(rstd[:, 0:1], var[:, 0:1], minus_half[:, 0:1], ALU.pow).then_inc(s["rstd"], 1)

        @block.tensor
        def _(pe):
            pe.wait_ge(s["part"], 1)
            pe.matmul(sum_ps, ones[:, :], part[:, :], start=True, stop=True).then_inc(s["sum"], 1)
            with pe.Fori(0, NT) as i:
                pe.wait_ge(s["xi"], i + 1)
                for kd in range(KD):
                    ins = pe.transpose(xT_ps[:, kd, :], xi[:, kd * P:(kd + 1) * P], ident16[:, :])
                ins.then_inc(s["xT"], 1)
                pe.wait_ge(s["xTe"], i + 1)
                for hf in range(FF // 512):
                    for kd in range(KD):
                        ins = pe.matmul(h_ps[:, hf * 512:(hf + 1) * 512], xT[:, kd, :],
                                        wb[0][:, kd, hf * 512:(hf + 1) * 512], start=(kd == 0), stop=(kd == KD - 1))
                ins.then_inc(s["h"], 1)
                pe.wait_ge(s["hi"], i + 1)
                for c in range(FK):
                    ins = pe.transpose(hT_ps[:, c, :], hi8[:, c * P:(c + 1) * P], ident16[:, :])
                ins.then_inc(s["hT"], 1)
                pe.wait_ge(s["hTe"], i + 1)
                for c in range(FK):
                    ins = pe.matmul(y_ps, hT[:, c, :], wb[1][:, c, :], start=(c == 0), stop=(c == FK - 1))
                ins.then_inc(s["y"], 1)

        @block.scalar
        def _(act):
            with act.Fori(0, NT) as i:
                act.wait_ge(s["xT"], i + 1)
                act.activation(xT[:, :, :], xT_ps, ACT.Copy).then_inc(s["xTe"], 1)
                act.wait_ge(s["h"], i + 1)
                act.activation(h[:, :], h_ps, ACT.Gelu, scale=un[:, 0:1]).then_inc(s["he"], 1)
                act.wait_ge(s["hT"], i + 1)
                act.activation(hT[:, :, :], hT_ps, ACT.Copy).then_inc(s["hTe"], 1)

        @block.vector
        def _(dve):
            dve.wait_ge(s["w"], 32)
            flat = [w[:, :, :].rearrange("p k n -> p (k n)") for w in wf]
            flatb = [w[:, :, :].rearrange("p k n -> p (k n)") for w in wb]
            for n in range(2):
                ins = dve.tensor_reduce(part[:, n:n + 1], flat[n], X, ALU.add, apply_absolute_value=True)
            ins.then_inc(s["part"], 1)
            dve.wait_ge(s["sum"], 1)
            dve.tensor_scalar(sw[:, :], sum_ps, 1.0 / (D * FF), EPS, ALU.mult, ALU.max)
            dve.drain()
            dve.tensor_scalar(half[:, :, 0], sw[:, :], 0.5, None, ALU.mult)
            dve.tensor_scalar(half[:, :, 1], sw[:, :], -0.5, None, ALU.mult)
            dve.drain()
            for n in range(2):
                dve.tensor_scalar(neg[:, :], flat[n], half[:, n, 1:2], None, ALU.is_lt)
                dve.drain()
                dve.scalar_tensor_tensor(flatb[n], flat[n], half[:, n, 0:1], neg[:, :], ALU.is_gt, ALU.subtract)
                dve.drain()

            def quantise(src, n, rounded, dst):
                dve.tensor_reduce(am[:, n:n + 1], src, X, ALU.max, apply_absolute_value=True)
                dve.drain()
                dve.tensor_scalar(am[:, n:n + 1], am[:, n:n + 1], EPS, None, ALU.max)
                dve.drain()
                dve.reciprocal(sc[:, n:n + 1], am[:, n:n + 1])
                dve.tensor_scalar(un[:, n:n + 1], am[:, n:n + 1], sw[:, n:n + 1], 1.0 / 127, ALU.mult, ALU.mult)
                dve.drain()
                dve.tensor_scalar(sc[:, n:n + 1], sc[:, n:n + 1], 127.0, None, ALU.mult)
                dve.drain()
                dve.tensor_scalar(rounded, src, sc[:, n:n + 1], ROUND, ALU.mult, ALU.add)
                dve.drain()
                return dve.tensor_scalar(dst, rounded, -ROUND, 127.0, ALU.add, ALU.min)

            with dve.Fori(0, NT) as i:
                xt = x[:, bass.ds(i, 1), :].rearrange("p a d -> p (a d)")
                dve.bn_stats(stats[:, 0, :], xt)
                dve.drain()
                dve.bn_aggr(mv[:, 0, :], stats[:, 0, :])
                dve.drain()
                dve.tensor_scalar(var[:, 0:1], mv[:, 0, 1:2], EPS, None, ALU.add).then_inc(s["var"], 1)
                dve.wait_ge(s["rstd"], i + 1)
                dve.tensor_scalar(xh[:, :], xt, mv[:, 0, 0:1], rstd[:, 0:1], ALU.subtract, ALU.mult)
                dve.drain()
                quantise(xh[:, :], 0, xr[:, :], xi[:, :]).then_inc(s["xi"], 1)
                dve.wait_ge(s["he"], i + 1)
                quantise(h[:, :], 1, hr[:, :], hi8[:, :]).then_inc(s["hi"], 1)
                dve.wait_ge(s["y"], i + 1)
                dve.tensor_scalar(xr[:, :], y_ps, un[:, 1:2], gates[:, 3:4], ALU.mult, ALU.mult)
                dve.drain()
                dve.tensor_tensor(xt, xr[:, :], xt, ALU.add).then_inc(s["un"], 1)
                dve.drain()


def _spread(w, src, width):
    import numpy as np
    w = np.asarray(w)
    o = np.zeros(w.shape[:-1] + (CH * P,), w.dtype)
    for h in range(H):
        o[..., 32 * h:32 * h + width] = w[..., h * src:h * src + width]
    return o


def kernel(**inputs):
    import numpy as np
    import concourse.bacc as bacc
    from concourse.bass_utils import run_bass_kernel_spmd

    i = {n: np.ascontiguousarray(a) for n, a in inputs.items()}

    def columns(v):
        return np.ascontiguousarray(v.reshape(-1, P).T)

    def key_bias(v, src, width):
        o = _spread(v, src, width)
        for h in range(H):
            o[32 * h + width] = 1.0
        return columns(o)

    lat = D // 2
    arrays = {
        "x": i["x"], "ctx": i["ctx_1024"], "g_xattn": i["g_xattn"], "g_ffn": i["g_ffn"],
        "a_wq": _spread(i["L0_xattn_Wq"], D // H, D // H), "a_bq": columns(_spread(i["L0_xattn_bq"], D // H, D // H)),
        "a_wk": _spread(i["L0_xattn_Wk"], D // H, D // H), "a_bk": key_bias(i["L0_xattn_bk"], D // H, D // H),
        "a_wv": i["L0_xattn_Wv"], "a_bv": i["L0_xattn_bv"], "a_wo": i["L0_xattn_Wo"], "a_bo": i["L0_xattn_bo"],
        "b_wq": _spread(i["L0_ffn_q_w"], D // H, lat // H), "b_bq": columns(_spread(i["L0_ffn_q_b"], D // H, lat // H)),
        "b_wk": _spread(i["L0_ffn_k_w"], lat // H, lat // H), "b_bk": key_bias(i["L0_ffn_k_b"], lat // H, lat // H),
        "b_wv": i["L0_ffn_v_w"], "b_bv": i["L0_ffn_v_b"], "b_wo": np.ascontiguousarray(i["L0_ffn_o_w"][:lat]),
        "b_bo": i["L0_ffn_o_b"], "router_w": i["L0_ffn_router_w"], "router_b": i["L0_ffn_router_b"],
        "moe_w1": i["L0_ffn_w1"], "moe_b1": i["L0_ffn_b1"], "moe_w2": i["L0_ffn_w2"], "moe_b2": i["L0_ffn_b2"],
        "l1_wq": i["L1_xattn_wq"], "l1_wk": i["L1_xattn_wk"], "l1_wv": i["L1_xattn_wv"], "l1_wo": i["L1_xattn_wo"],
        "l1_bo": i["L1_xattn_bo"], "l1_w1": i["L1_xattn_w1"], "l1_b1": columns(i["L1_xattn_b1"]),
        "l1_w2": i["L1_xattn_w2"], "l1_b2": i["L1_xattn_b2"],
        "l1_ln": np.ascontiguousarray(np.stack([i["L1_xattn_" + n].reshape(KD, P).T for n in
                                                ("ln1_g", "ln1_b", "ln2_g", "ln2_b")], axis=1)),
        "ff_w1t": np.ascontiguousarray(i["L1_ffn_w1"].T), "ff_w2t": np.ascontiguousarray(i["L1_ffn_w2"].T),
    }
    nc = bacc.Bacc("TRN2", target_bir_lowering=False, num_devices=1)
    t = {n: nc.dram_tensor(f"in_{n}", a.shape, mybir.dt.from_np(a.dtype), kind="ExternalInput").ap()
         for n, a in arrays.items()}
    out = nc.dram_tensor("out", (B, S, D), F32, kind="ExternalOutput").ap()
    program(nc, t, out)
    r = run_bass_kernel_spmd(nc, [{f"in_{n}": a for n, a in arrays.items()}], core_ids=[0])
    return r.results[0]["out"]
```

```python
import concourse.bass as bass
from concourse import mybir
from contextlib import ExitStack

F32 = mybir.dt.float32
BF16 = mybir.dt.bfloat16
F32R = mybir.dt.float32r
I32 = mybir.dt.int32
U32 = mybir.dt.uint32
ALU = mybir.AluOpType
ACT = mybir.ActivationFunctionType
X = mybir.AxisListType.X

P = 128
B, S, D = 8, 256, 256
SC = 77
H = 16
TPB = S // P
NT = B * TPB
KD = D // P
GR = 4
CH = H // GR
E, F0 = 8, 512
TOPK = 2
INNER = 1024
HD1 = INNER // H
FF = 1024
SLOT_TILES = NT * TOPK + E
EPS = 1e-5
ROUND = 1.5 * 2.0 ** 23


def program(nc, t, out):
    ctx = ExitStack()
    with ctx:
        def sb(name, shape, dt=F32):
            return ctx.enter_context(nc.sbuf_tensor(name, shape, dt))

        stage_sems = []

        def sem(name):
            stage_sems.append(nc.alloc_semaphore(name))
            return stage_sems[-1]

        def stage_done():
            nc.clear_and_free_semaphores(list(stage_sems))
            stage_sems.clear()
            nc.all_engine_barrier()

        x_slots = nc.dram_tensor("x_slots", [SLOT_TILES * P, D], F32, kind="Internal").ap()
        y_slots = nc.dram_tensor("y_slots", [SLOT_TILES * P, D], F32, kind="Internal").ap()

        ps = ctx.enter_context(nc.psum_tensor("ps", [P, 8, 512], F32))

        def banks(b, n, shape):
            flat = ps[:, b:b + n, :].rearrange("p b n -> p (b n)")
            return flat

        x = sb("x", [P, NT, D])
        ident = sb("ident", [P, P])
        ident16 = sb("ident16", [P, P], BF16)
        ones = sb("ones", [P, P])
        before = sb("before", [P, P])
        gates = sb("gates", [P, 4])
        minus_half = sb("minus_half", [P, H])
        stats = sb("stats", [P, 3, 6])
        mv = sb("mv", [P, 3, 2])
        var = sb("var", [P, 3])
        rstd = sb("rstd", [P, 3])
        route_i = sb("route_i", [P, NT, TOPK], U32)
        route_w = sb("route_w", [P, NT, TOPK])

        layers = {}

        s_x = sem("s_x")
        s_gate = sem("s_gate")
        s_const = sem("s_const")
        s_ones = sem("s_ones")
        with nc.Block() as block:
            @block.sync
            def _(sp):
                sp.dma_start(x[:, :, :], t["x"].rearrange("b (t p) d -> p (b t) d", p=P)).then_inc(s_x, 16)
                for i, g in enumerate(("g_xattn", "g_ffn")):
                    for j in range(2):
                        sp.dma_start(gates[:, 2 * j + i:2 * j + i + 1],
                                     t[g][j:j + 1].partition_broadcast(P)).then_inc(s_gate, 16)
                sp.wait_ge(s_x, 16)

            @block.gpsimd
            def _(pool):
                pool.memset(ident[:, :], 0.0)
                pool.memset(ident16[:, :], 0.0)
                pool.memset(ones[:, :], 1.0)
                pool.memset(before[:, :], 1.0)
                pool.memset(minus_half[:, :], -0.5)
                pool.drain()
                pool.affine_select(out=ident[:, :], in_=ident[:, :], compare_op=ALU.not_equal, fill=1.0,
                                   base=0, pattern=[[-1, P]], channel_multiplier=1)
                pool.affine_select(out=ident16[:, :], in_=ident16[:, :], compare_op=ALU.not_equal, fill=1.0,
                                   base=0, pattern=[[-1, P]], channel_multiplier=1)
                pool.affine_select(out=before[:, :], in_=before[:, :], compare_op=ALU.is_gt, fill=0.0,
                                   base=0, pattern=[[1, P]], channel_multiplier=-1)

            @block.scalar
            def _(act):
                act.wait_ge(s_gate, 64)
                act.activation(gates[:, :], gates[:, :], ACT.Tanh)

        def softmax_attention(tag, hd, band, NK, KC, cross, rest):
            HC = P // band
            NC = H // HC
            VD = H * hd
            OK = VD // P
            W = NC * P
            scale = float(hd) ** -0.5
            KW = P if cross else P * KC
            R = H * KC // 2
            st = ExitStack()

            def tb(name, shape, dt=F32):
                return st.enter_context(nc.sbuf_tensor(tag + name, shape, dt))

            def ts(name):
                return sem(tag + name)

            wq = [tb("wqh", [P, KD, W], F32R), tb("wql", [P, KD, W], F32R)]
            wk = [tb("wkh", [P, KD, W], F32R), tb("wkl", [P, KD, W], F32R)]
            wv = [tb("wvh", [P, KD, 256], F32R), tb("wvl", [P, KD, 256], F32R)]
            wo = [tb("woh", [P, OK, D], F32R), tb("wol", [P, OK, D], F32R)]
            bq = tb("bq", [P, NC])
            bk = tb("bk", [P, NC])
            sbq = tb("sbq", [P, NC])
            sbk = tb("sbk", [P, NC])
            low = tb("low", [P, 2])
            bv = tb("bv", [P, 256])
            bo = tb("bo", [P, D])
            xn = tb("xn", [P, TPB, D])
            xT = [tb("xTh", [P, KD, S], F32R), tb("xTl", [P, KD, S], F32R)]
            q = [tb("q0", [P, NC, S], F32R), tb("q1", [P, NC, S], F32R)]
            hm = tb("hm", [P, 4, S], F32R)
            k = [tb("k0", [P, NC, HC, KW], F32R), tb("k1", [P, NC, HC, KW], F32R)]
            kk = tb("kk", [P, NC, B * SC if cross else KW], F32R)
            v = [tb("v0", [P, KC, H, P], F32R), tb("v1", [P, KC, H, P], F32R)]
            negmax = tb("negmax", [P, TPB, NC, P], BF16)
            pt = tb("pt", [P, 3, 2, S])
            pth = tb("pth", [P, 3, 2, S], F32R)
            ptl = tb("ptl", [P, 3, 2, S], F32R)
            av = tb("av", [P, NC, S])
            rsum = tb("rsum", [P, H])
            parts = tb("parts", [P, 2, H, hd])
            ao = tb("ao", [P, TPB, H, hd])
            aoT = [tb("aoTh", [P, OK, S], F32R), tb("aoTl", [P, OK, S], F32R)]
            tmp = tb("tmp", [P, TPB, D])
            if cross:
                cx = av[:, 0:5, :]
                cT = [tb("cTh", [P, KD, B * SC], F32R), tb("cTl", [P, KD, B * SC], F32R)]
                vall = [tb("vallh", [P, B, 256], F32R), tb("valll", [P, B, 256], F32R)]
            else:
                mo, hln, rw, rb, moT, lgT, zeros = rest
                rwf = tb("rwf", [P, KD, E])
                vf = tb("vf", [P, KC, 256])
            names = "w0 w1 w2 wh wl cx var rstd xn xT xTh xTl pp phm pe kp khm kst vp vf vh vl kx kd " \
                "max maxe mT q2 sc exp ph pl free ave at pa ao aoT aoTh aoTl o oe".split()
            names += ("cT cTh cTl vx" if cross else "z zero moT moTh moTl lg lge hc mc").split()
            s = {n: ts("s_" + n) for n in names}

            def bank(b, w=512, parts=P):
                return ps[0:parts, b, 0:w]

            SR, PVB = [0, 1], [2, 3]
            XB, PB, VB = 4, [5, 6], 7
            xT_ps = bank(XB).rearrange("p (k s) -> p k s", k=KD)
            v_ps = bank(VB).rearrange("p (k n) -> p k n", n=256)
            mT_ps = ps[:, 4:6, :].rearrange("p b n -> p (b n)").bitcast(BF16)[:, 0:NC * S] \
                .rearrange("p (c s) -> p c s", c=NC)
            aoT_ps = bank(3, OK * S).rearrange("p (k s) -> p k s", k=OK)
            moT_ps = bank(3).rearrange("p (k s) -> p k s", k=KD)
            o_ps = bank(2).rearrange("p (t d) -> p t d", t=TPB)
            MR = NC // 4
            MROUNDS = TPB * (4 if MR == 1 else 2)
            AT = TPB * MR
            per = R // (NC // 2)

            def max_ps(m):
                return ps[:, 4 + 2 * (m % 2):6 + 2 * (m % 2), :].rearrange("p b n -> p (b n)")

            def head(r, j):
                return (r // HC, r % HC, j) if KC == 2 else (r, j, 0)

            def pair(n):
                return (False, 2 * n) if cross else (n >= 2, 2 * (n % 2))

            F = "stats xn xT xTl p0 p1 e0 p2 e1 p3 e2 v e3 kx ve vs".split()
            F += [word for m in range(MROUNDS + 1) for word in ([f"m{m}"] if m < MROUNDS else []) + ([f"me{m - 1}"] if m else [])]
            F += ["mT", "q2"]
            K = [f"r{r}" for r in range(R + 3)]
            K += [word for n in range(AT + 1) for word in ([f"t{n}"] if n < AT else []) + ([f"te{n - 1}"] if n else [])]
            K += "aoT aoTl o oe moT moTl lg".split()
            STEPS = sorted([((n + 0.5) / len(F), "f", word) for n, word in enumerate(F)]
                           + [((n + 0.5) / len(K), "b", word) for n, word in enumerate(K)])

            def run(steps, i, p, streams):
                for _, kind, name in STEPS:
                    word = name.rstrip("0123456789")
                    if kind in streams and (kind, word) in steps:
                        n = [int(name[len(word):])] if name != word else []
                        if kind == "f":
                            steps[kind, word](i + 1, 1 - p, *n)
                        else:
                            steps[kind, word](i, p, *n)

            def pipeline(eng, steps):
                run(steps, -1, 1, "f")
                run(steps, 0, 0, "fb")
                with eng.Fori(0, B // 2 - 1) as j:
                    run(steps, 2 * j + 1, 1, "fb")
                    run(steps, 2 * j + 2, 0, "fb")
                run(steps, B - 1, 1, "b")

            def after(eng, semaphore, n):
                if not (isinstance(n, int) and n <= 0):
                    eng.wait_ge(semaphore, n)

            passes = [(0, 0), (0, 1), (1, 0)]

            def product(eng, dst, lhsT, rhs, n):
                for kd in range(n):
                    for m, (a, b) in enumerate(passes):
                        ins = eng.matmul(dst, lhsT[a](kd), rhs[b](kd), start=(kd == 0 and m == 0),
                                         stop=(kd == n - 1 and m == 2))
                return ins

            pieces, whole = [], {}
            for dst, name, w, chunks in ((wk, "wk", W, KD), (wv, "wv", 256, KD), (wq, "wq", W, KD), (wo, "wo", D, OK)):
                src = t[tag + name].rearrange("(k p) n -> p k n", p=P)
                kn = max(1, min(chunks, 512 // w))
                for kd in range(0, chunks, kn):
                    for c in range(0, w, 512):
                        cut = (slice(None), slice(kd, kd + kn), slice(c, min(w, c + 512)))
                        pieces.append((dst[0][cut], dst[1][cut], src[cut], kn, min(w, 512)))
                whole[name] = len(pieces)

            def staged(n):
                kn, w = pieces[n][3:]
                return pt[:, n % 3, :, :].rearrange("p a s -> p (a s)")[:, 0:kn * w].rearrange("p (k n) -> p k n", k=kn)

            def hm_of(n):
                return hm[:, 2 * (n % 2):2 * (n % 2) + 2, :].rearrange("p a s -> p (a s)")[:, 0:4 * SC]

            def lo_of(eng, dst, src, hi):
                return eng.tensor_tensor(dst, src, hi.bitcast(F32), ALU.subtract)

            def dve_steps(dve):
                def stats_(f, p):
                    for tt in range(TPB):
                        dve.bn_stats(stats[:, tt, :], x[:, bass.ds(TPB * f + tt, 1), :])
                    dve.drain()
                    for tt in range(TPB):
                        dve.bn_aggr(mv[:, tt, :], stats[:, tt, :])
                    dve.drain()
                    dve.tensor_scalar(var[:, 0:TPB], mv[:, 0:TPB, 1], EPS, None, ALU.add).then_inc(s["var"], 1)

                def xn_(f, p):
                    dve.wait_ge(s["rstd"], f + 1)
                    after(dve, s["xT"], f)
                    if not cross:
                        after(dve, s["hc"], f)
                    for tt in range(TPB):
                        ins = dve.tensor_scalar(xn[:, tt, :],
                                                x[:, bass.ds(TPB * f + tt, 1), :].rearrange("p a d -> p (a d)"),
                                                mv[:, tt, 0:1], rstd[:, tt:tt + 1], ALU.subtract, ALU.mult)
                    ins.then_inc(s["xn"], 1)

                def xTl(f, p):
                    dve.wait_ge(s["xTh"], f + 1)
                    lo_of(dve, xT[1][:, :, :], xT_ps, xT[0][:, :, :]).then_inc(s["xTl"], 1)

                def e(f, p, n):
                    dve.wait_ge(s["phm"], 4 * f + n + 1)
                    keys, c = pair(n)
                    if keys:
                        after(dve, s["kx"], f)
                    elif n == 0:
                        after(dve, s["free"], R * (f - 1))
                    for u in range(2):
                        ins = dve.scalar_tensor_tensor((kk if keys else q[p])[:, c + u, :],
                                                       bank(PB[n % 2])[:, u * S:(u + 1) * S],
                                                       (bk if keys else bq)[:, c + u:c + u + 1],
                                                       hm[:, 2 * (n % 2) + u, :].bitcast(F32), ALU.add, ALU.subtract)
                    ins.then_inc(s["pe"], 1)

                def ve(f, p):
                    dve.drain()
                    dve.wait_ge(s["vp"], f + 1)
                    dve.tensor_tensor(vf[:, :, :], v_ps, bv[:, :].unsqueeze(1).to_broadcast([P, KC, 256]), ALU.add)\
                        .then_inc(s["vf"], 1)

                def vs(f, p):
                    dve.drain()
                    after(dve, s["free"], R * (f - 1))
                    views = []
                    for kc in range(KC):
                        for g in range(HC):
                            src = vf[:, kc, :].rearrange("p (c g n) -> p c g n", g=HC, n=2 * hd)[:, :, g, :]
                            dst = v[p][:, kc, :, g * band:g * band + 2 * hd]\
                                .rearrange("p (c g) n -> p c g n", g=HC)[:, :, g, :]
                            views.append((dst, src))
                    for dst, src in views:
                        dve.tensor_copy(dst[:, :, 0:hd], src[:, :, 0:hd])
                    dve.drain()
                    for dst, src in views:
                        ins = lo_of(dve, dst[:, :, hd:2 * hd], src[:, :, hd:2 * hd], dst[:, :, 0:hd])
                    ins.then_inc(s["vl"], 1)

                def me(f, p, m):
                    dve.wait_ge(s["max"], MROUNDS * f + m + 1)
                    if m == 0:
                        after(dve, s["mT"], f)
                    if MR == 1:
                        tt, c0, n = m // 4, m % 4, 1
                    else:
                        tt, c0, n = m // 2, 4 * (m % 2), 4
                    src = max_ps(m).rearrange("p (c g n) -> p c g n", c=n, g=HC)[:, :, :, 0:NK * KC]
                    dst = negmax[:, tt, c0:c0 + n, :].rearrange("p c (g r) -> p c g r", g=HC)[:, :, :, 3 * hd]
                    dve.tensor_reduce(dst, src, X, ALU.max, negate=True).then_inc(s["maxe"], 1)

                def q2(f, p):
                    dve.drain()
                    dve.wait_ge(s["mT"], f + 1)
                    dve.tensor_tensor(q[p][:, :, :], q[p][:, :, :].bitcast(F32), mT_ps, ALU.add).then_inc(s["q2"], 1)

                def r_(i, p, r):
                    if 1 <= r <= R:
                        dve.wait_ge(s["ph"], R * i + r)
                        r -= 1
                        lo_of(dve, ptl[0:NK, r % 3, :, :], pt[0:NK, r % 3, :, :], pth[0:NK, r % 3, :, :])\
                            .then_inc(s["pl"], 1)

                def te(i, p, m):
                    dve.wait_ge(s["at"], AT * i + m + 1)
                    tt, u = m // MR, m % MR
                    n = H // MR
                    at = bank(SR[m % 2]).rearrange("p (h r) -> p h r", r=band)
                    hs = slice(u * n, u * n + n)
                    dve.reciprocal(rsum[:, hs], at[:, :, 2 * hd])
                    dve.drain()
                    for part in range(2):
                        ins = dve.tensor_tensor(parts[:, part, hs, :], at[:, :, part * hd:(part + 1) * hd],
                                                rsum[:, hs].unsqueeze(2).to_broadcast([P, n, hd]), ALU.mult)
                    ins.then_inc(s["pa"], 1)
                    dve.drain()
                    if u == MR - 1:
                        if m < AT - 1:
                            after(dve, s["aoT"], i)
                        dve.tensor_tensor(ao[:, tt, :, :], parts[:, 0, :, :], parts[:, 1, :, :], ALU.add)\
                            .then_inc(s["ao"], 1)
                        dve.drain()

                def aoTl(i, p):
                    dve.wait_ge(s["aoTh"], i + 1)
                    lo_of(dve, aoT[1][:, :, :], aoT_ps, aoT[0][:, :, :]).then_inc(s["aoTl"], 1)

                def oe(i, p):
                    dve.wait_ge(s["o"], i + 1)
                    bob = bo[:, :].unsqueeze(1).to_broadcast([P, TPB, D])
                    if cross:
                        xb = x[:, bass.ds(TPB * i, TPB), :]
                        dve.tensor_tensor(tmp[:, :, :], o_ps, bob, ALU.add).then_inc(s["oe"], 1)
                        dve.drain()
                        dve.scalar_tensor_tensor(xb, tmp[:, :, :], gates[:, 0:1], xb, ALU.mult, ALU.add)
                        dve.drain()
                    else:
                        after(dve, s["mc"], i)
                        after(dve, s["moT"], i)
                        dve.tensor_tensor(tmp[:, :, :], o_ps, bob, ALU.add).then_inc(s["oe"], 1)

                def moTl(i, p):
                    dve.wait_ge(s["moTh"], i + 1)
                    lo_of(dve, moT[1][:, :, :], moT_ps, moT[0][:, :, :]).then_inc(s["moTl"], 1)

                steps = {("f", "stats"): stats_, ("f", "xn"): xn_, ("f", "xTl"): xTl, ("f", "e"): e, ("f", "me"): me,
                         ("f", "q"): lambda f, p, _: q2(f, p),
                         ("b", "r"): r_, ("b", "te"): te, ("b", "aoTl"): aoTl, ("b", "oe"): oe}
                if not cross:
                    steps.update({("f", "ve"): ve, ("f", "vs"): vs, ("b", "moTl"): moTl})
                return steps

            def act_steps(act):
                def xT_(f, p):
                    act.wait_ge(s["xT"], f + 1)
                    after(act, s["pp"], 4 * f)
                    if not cross:
                        after(act, s["vp"], f)
                    act.activation(xT[0][:, :, :], xT_ps, ACT.Copy).then_inc(s["xTh"], 1)

                def p_(f, p, n):
                    act.wait_ge(s["pp"], 4 * f + n + 1)
                    after(act, s["pe"], 4 * f + n - 1)
                    keys, c = pair(n)
                    for u in range(2):
                        ins = act.activation(hm[:, 2 * (n % 2) + u, :], bank(PB[n % 2])[:, u * S:(u + 1) * S],
                                             ACT.Identity, bias=(sbk if keys else sbq)[:, c + u:c + u + 1],
                                             scale=low[:, int(keys):int(keys) + 1])
                    ins.then_inc(s["phm"], 1)

                def r_(i, p, r):
                    if r < R:
                        act.wait_ge(s["sc"], R * i + r + 1)
                        after(act, s["pl"], R * i + r - 2)
                        act.activation(pt[0:NK, r % 3, :, :].rearrange("p j s -> p (j s)"), bank(SR[r % 2], 512, NK),
                                       ACT.Exp, scale=scale).then_inc(s["exp"], 1)
                    if r >= per + 2 and (r - 2) % per == 0:
                        n = (r - 2) // per - 1
                        act.wait_ge(s["free"], R * i + per * (n + 1))
                        if n == 0:
                            after(act, s["at"], AT * i)
                        act.activation(av[:, 2 * n:2 * n + 2, :], bank(PVB[n % 2]).rearrange("p (c s) -> p c s", c=2),
                                       ACT.Copy).then_inc(s["ave"], 1)

                def aoT_(i, p):
                    act.wait_ge(s["aoT"], i + 1)
                    after(act, s["o"], i)
                    act.activation(aoT[0][:, :, :], aoT_ps, ACT.Copy).then_inc(s["aoTh"], 1)

                def moT_(i, p):
                    act.wait_ge(s["moT"], i + 1)
                    after(act, s["lg"], i)
                    act.activation(moT[0][:, :, :], moT_ps, ACT.Copy).then_inc(s["moTh"], 1)

                def lg(i, p):
                    act.wait_ge(s["lg"], i + 1)
                    act.activation(lgT[:, bass.ds(S * i, S)], bank(2, S, E), ACT.Identity, bias=rb[:, 0:1])\
                        .then_inc(s["lge"], 1)

                steps = {("f", "xT"): xT_, ("f", "p"): p_, ("b", "r"): r_, ("b", "aoT"): aoT_}
                if not cross:
                    steps.update({("b", "moT"): moT_, ("b", "lg"): lg})
                return steps

            def pool_steps(pool):
                def copy(dst, src):
                    return pool.tensor_scalar(dst, src, 1.0, 0.0, ALU.mult, ALU.add)

                def stats_(f, p):
                    pool.wait_ge(s["var"], f + 1)
                    pool.tensor_tensor(rstd[:, 0:TPB], var[:, 0:TPB], minus_half[:, 0:TPB], ALU.pow)\
                        .then_inc(s["rstd"], 1)

                def kx_cross(f, p):
                    pool.drain()
                    after(pool, s["free"], R * (f - 1))
                    for g in range(HC):
                        rows = slice(g * band, (g + 1) * band)
                        if g:
                            pool.drain()
                        ins = pool.tensor_copy(k[p][rows, :, g, 0:SC], kk[rows, :, bass.ds(SC * f, SC)].bitcast(F32))
                    ins.then_inc(s["kx"], 1)
                    pool.drain()
                    for part in range(2):
                        for g in range(HC):
                            src = vall[part][0:SC, bass.ds(f, 1), :].rearrange("p a (c g n) -> p (a c) g n", g=HC, n=hd)
                            dst = v[p][0:SC, 0, :, g * band + part * hd:g * band + (part + 1) * hd]\
                                .rearrange("p (c g) n -> p c g n", g=HC)
                            ins = pool.tensor_copy(dst[:, :, g, :], src[:, :, g, :].bitcast(F32))
                    ins.then_inc(s["vx"], 1)
                    pool.drain()

                def kx_self(f, p):
                    pool.drain()
                    pool.wait_ge(s["pe"], 4 * f + 4)
                    after(pool, s["free"], R * (f - 1))
                    pool.tensor_tensor(k[p][0:band, 0, 0, 0:4], kk[0:band, 0, 0:4].bitcast(F32), ones[0:band, 0:4],
                                       ALU.mult)
                    pool.drain()
                    copy(k[p][0:band, 0, 0, 4:], kk[0:band, 0, 4:].bitcast(F32))
                    copy(k[p][0:band, 1:, 0, :], kk[0:band, 1:, :].bitcast(F32))
                    for g in range(1, HC):
                        rows = slice(g * band, (g + 1) * band)
                        pool.drain()
                        ins = copy(k[p][rows, :, g, :], kk[rows, :, :].bitcast(F32))
                    ins.then_inc(s["kx"], 1)
                    pool.drain()

                def r_(i, p, r):
                    if r < R:
                        pool.wait_ge(s["exp"], R * i + r + 1)
                        after(pool, s["free"], R * i + r - 2)
                        pool.tensor_tensor(pth[0:NK, r % 3, 0, 0:4], pt[0:NK, r % 3, 0, 0:4], ones[0:NK, 0:4], ALU.mult)
                        copy(pth[0:NK, r % 3, 0, 4:S], pt[0:NK, r % 3, 0, 4:S])
                        copy(pth[0:NK, r % 3, 1, :], pt[0:NK, r % 3, 1, :]).then_inc(s["ph"], 1)

                def hln_(f, p):
                    pool.wait_ge(s["xn"], f + 1)
                    pool.tensor_copy(hln[:, bass.ds(TPB * f, TPB), :], xn[:, :, :]).then_inc(s["hc"], 1)

                def mo_(i, p):
                    pool.wait_ge(s["oe"], i + 1)
                    pool.tensor_copy(mo[:, bass.ds(TPB * i, TPB), :], tmp[:, :, :]).then_inc(s["mc"], 1)

                steps = {("f", "stats"): stats_, ("f", "kx"): kx_cross if cross else kx_self, ("b", "r"): r_}
                if not cross:
                    steps.update({("f", "xT"): hln_, ("b", "moT"): mo_})
                return steps

            def pe_steps(pe):
                def xT_(f, p):
                    pe.wait_ge(s["xn"], f + 1)
                    after(pe, s["q2"], f)
                    for tt in range(TPB):
                        for kd in range(KD):
                            ins = pe.transpose(xT_ps[:, kd, tt * P:(tt + 1) * P], xn[:, tt, kd * P:(kd + 1) * P],
                                               ident[:, :])
                    ins.then_inc(s["xT"], 1)

                xs = [lambda kd, a=a: xT[a][:, kd, :] for a in range(2)]

                def p_(f, p, n):
                    if n == 0:
                        pe.wait_ge(s["xTl"], f + 1)
                    if n >= 2:
                        pe.wait_ge(s["pe"], 4 * f + n - 1)
                    keys, c = pair(n)
                    w = wk if keys else wq
                    for u in range(2):
                        ins = product(pe, bank(PB[n % 2])[:, u * S:(u + 1) * S],
                                      [lambda kd, a=a: w[a][:, kd, (c + u) * P:(c + u + 1) * P] for a in range(2)], xs, KD)
                    ins.then_inc(s["pp"], 1)

                def v_(f, p):
                    for kc in range(KC):
                        ins = product(pe, v_ps[:, kc, :],
                                      [lambda kd, a=a: xT[a][:, kd, kc * P:(kc + 1) * P] for a in range(2)],
                                      [lambda kd, a=a: wv[a][:, kd, :] for a in range(2)], KD)
                    ins.then_inc(s["vp"], 1)

                def m_(f, p, m):
                    if m == 0:
                        pe.wait_ge(s["pe"], 4 * f + 4)
                        pe.wait_ge(s["kx"], f + 1)
                        if not cross:
                            pe.wait_ge(s["vf"], f + 1)
                    if m >= 2:
                        pe.wait_ge(s["maxe"], MROUNDS * f + m - 1)
                    for half in range(2):
                        if MR == 1:
                            tt, c = m // 4, m % 4
                            ins = pe.matmul(max_ps(m)[:, half * 512:(half + 1) * 512], q[p][:, c, tt * P:(tt + 1) * P],
                                            k[p][:, c, 2 * half:2 * half + 2, :], start=True, stop=True)
                        else:
                            for u in range(2):
                                tt, c = m // 2, 4 * (m % 2) + 2 * half + u
                                o = half * 512 + u * 256
                                ins = pe.matmul(max_ps(m)[:, o:o + 256], q[p][:, c, tt * P:(tt + 1) * P],
                                                k[p][:, c, :, :], start=True, stop=True)
                    ins.then_inc(s["max"], 1)

                def mT_(f, p):
                    pe.wait_ge(s["maxe"], MROUNDS * f + MROUNDS)
                    for tt in range(TPB):
                        for c in range(NC):
                            ins = pe.transpose(mT_ps[:, c, tt * P:(tt + 1) * P], negmax[:, tt, c, :], ident16[:, :])
                    ins.then_inc(s["mT"], 1)

                def r_(i, p, r):
                    if r == 0:
                        pe.wait_ge(s["q2"], i + 1)
                        pe.wait_ge(s["vx" if cross else "vl"], i + 1)
                        after(pe, s["pa"], AT * i)
                    if r < R:
                        if r >= 2:
                            pe.wait_ge(s["exp"], R * i + r - 1)
                        for j in range(2):
                            c, g, kc = head(r, j)
                            ins = pe.matmul(bank(SR[r % 2], 512, NK)[:, j * S:(j + 1) * S],
                                            k[p][:, c, g, kc * P:kc * P + NK], q[p][:, c, :], start=True, stop=True)
                        ins.then_inc(s["sc"], 1)
                    r -= 2
                    if r == 0:
                        after(pe, s["oe" if cross else "lge"], i)
                    if 0 <= r < R:
                        pe.wait_ge(s["pl"], R * i + r + 1)
                        for j in range(2):
                            c, g, kc = head(r, j)
                            first = g == 0 and kc == 0
                            last = g == HC - 1 and kc == KC - 1
                            if first and c % 2 == 0 and c >= 4:
                                pe.wait_ge(s["ave"], NC // 2 * i + c // 2 - 1)
                            for n, w in enumerate((pth, ptl)):
                                ins = pe.matmul(bank(PVB[c // 2 % 2])[:, (c % 2) * S:(c % 2 + 1) * S],
                                                v[p][:, kc, c * HC + g, :], w[:, r % 3, j, :],
                                                start=(first and n == 0), stop=(last and n == 1))
                        ins.then_inc(s["free"], 1)

                def t_(i, p, m):
                    tt, u = m // MR, m % MR
                    if m == 0:
                        pe.wait_ge(s["ave"], NC // 2 * i + NC // 2)
                    if m >= 2:
                        pe.wait_ge(s["pa"], AT * i + m - 1)
                    for c in range(4):
                        ins = pe.transpose(bank(SR[m % 2])[:, c * P:(c + 1) * P], av[:, 4 * u + c, tt * P:(tt + 1) * P],
                                           ident[:, :])
                    ins.then_inc(s["at"], 1)

                def aoT_(i, p):
                    pe.wait_ge(s["ao"], TPB * i + TPB)
                    for tt in range(TPB):
                        flat = ao[:, tt, :, :].rearrange("p h e -> p (h e)")
                        for kd in range(OK):
                            ins = pe.transpose(aoT_ps[:, kd, tt * P:(tt + 1) * P], flat[:, kd * P:(kd + 1) * P], ident[:, :])
                    ins.then_inc(s["aoT"], 1)

                def o_(i, p):
                    pe.wait_ge(s["aoTl"], i + 1)
                    for tt in range(TPB):
                        ins = product(pe, o_ps[:, tt, :],
                                      [lambda kd, a=a: aoT[a][:, kd, tt * P:(tt + 1) * P] for a in range(2)],
                                      [lambda kd, a=a: wo[a][:, kd, :] for a in range(2)], OK)
                    ins.then_inc(s["o"], 1)

                def moT_(i, p):
                    pe.wait_ge(s["oe"], i + 1)
                    for tt in range(TPB):
                        for kd in range(KD):
                            ins = pe.transpose(moT_ps[:, kd, tt * P:(tt + 1) * P], tmp[:, tt, kd * P:(kd + 1) * P],
                                               ident[:, :])
                    ins.then_inc(s["moT"], 1)

                def lg(i, p):
                    pe.wait_ge(s["moTl"], i + 1)
                    product(pe, bank(2, S, E), [lambda kd, a=a: rw[a][:, kd, :] for a in range(2)],
                            [lambda kd, a=a: moT[a][:, kd, :] for a in range(2)], KD).then_inc(s["lg"], 1)

                steps = {("f", "xT"): xT_, ("f", "p"): p_, ("f", "m"): m_, ("f", "mT"): mT_,
                         ("b", "r"): r_, ("b", "t"): t_, ("b", "aoT"): aoT_, ("b", "o"): o_}
                if not cross:
                    steps.update({("f", "v"): v_, ("b", "moT"): moT_, ("b", "lg"): lg})
                return steps

            with st, nc.Block() as block:
                @block.sync
                def _(sp):
                    for n in range(len(pieces)):
                        if n >= 3:
                            sp.wait_ge(s["wl"], n - 2)
                        sp.dma_start(staged(n), pieces[n][2]).then_inc(s[f"w{n % 3}"], 16)
                        if n == 0:
                            for dst2, name2 in ((bq, tag + "bq"), (bk, tag + "bk"), (low, tag + "low")):
                                sp.dma_start(dst2[:, :], t[name2]).then_inc(s["cx"], 16)
                            for dst2, name2 in ((bv, tag + "bv"), (bo, tag + "bo")):
                                sp.dma_start(dst2[:, :], t[name2].partition_broadcast(P)).then_inc(s["cx"], 16)
                            if cross:
                                cflat = t["ctx"].rearrange("b s d -> (b s) d")
                                sp.dma_start(cx[:, 0:4, :], cflat[0:512, :].rearrange("(a p) d -> p a d", p=P))\
                                    .then_inc(s["cx"], 16)
                                sp.dma_start(cx[0:B * SC - 512, 4, :], cflat[512:B * SC, :]).then_inc(s["cx"], 16)
                            else:
                                sp.dma_start(rwf[:, :, :], t["router_w"].rearrange("(k p) n -> p k n", p=P))\
                                    .then_inc(s["cx"], 16)
                                sp.dma_start(rb[:, :], t["router_b"]).then_inc(s["cx"], 16)
                    if not cross:
                        sp.wait_ge(s["zero"], 1)
                        with sp.Fori(0, SLOT_TILES // 8) as i:
                            sp.dma_start(x_slots.rearrange("(i a p) d -> i p a d", a=8, p=P)[bass.ds(i, 1)]
                                         .rearrange("i p a d -> (i p) a d"),
                                         zeros[:, :].unsqueeze(1).to_broadcast([P, 8, D])).then_inc(s["z"], 16)
                        sp.wait_ge(s["z"], 16 * (SLOT_TILES // 8))

                @block.gpsimd
                def _(pool):
                    if not cross:
                        pool.memset(zeros[:, :], 0.0).then_inc(s["zero"], 1)
                    pool.memset(k[0][:, :, :, :].bitcast(F32), 0.0)
                    pool.memset(v[0][:, :, :, :].bitcast(F32), 0.0)
                    pool.memset(pth[:, :, :, :].bitcast(F32), 0.0)
                    pool.memset(ptl[:, :, :, :].bitcast(F32), 0.0)
                    pool.memset(k[1][:, :, :, :].bitcast(F32), 0.0)
                    pool.memset(v[1][:, :, :, :].bitcast(F32), 0.0)
                    pool.memset(negmax[:, :, :, :], 0.0)
                    pool.drain()
                    for w in v:
                        for g in range(HC):
                            ones_at = w[:, :, :, g * band + 2 * hd].rearrange("p k (c g) -> p k c g", g=HC)
                            ins = pool.memset(ones_at[:, :, :, g].bitcast(F32), 1.0)
                    ins.then_inc(s["kd"], 1)
                    pool.drain()
                    if cross:
                        pool.wait_ge(s["kst"], 2 * NC)
                        pool.wait_ge(s["vl"], 4)
                    pipeline(pool, pool_steps(pool))

                @block.vector
                def _(dve):
                    dve.wait_ge(s["cx"], 16 * 7)
                    dve.tensor_scalar(sbq[:, :], bq[:, :], low[:, 0:1], None, ALU.mult)
                    dve.tensor_scalar(sbk[:, :], bk[:, :], low[:, 1:2], None, ALU.mult).then_inc(s["vh"], 1)
                    if cross:
                        for n in range(5):
                            dve.wait_ge(s["cTh"], n + 1)
                            w = P if n < 4 else B * SC - 512
                            src = bank(n % 2, KD * P).rearrange("p (k s) -> p k s", k=KD)[:, :, 0:w]
                            lo_of(dve, cT[1][:, :, n * P:n * P + w], src, cT[0][:, :, n * P:n * P + w])\
                                .then_inc(s["cTl"], 1)
                    for n in range(len(pieces)):
                        dve.wait_ge(s["wh"], n + 1)
                        lo_of(dve, pieces[n][1], staged(n), pieces[n][0]).then_inc(s["wl"], 1)
                    if not cross:
                        dve.tensor_copy(rw[0][:, :, :], rwf[:, :, :])
                        dve.drain()
                        lo_of(dve, rw[1][:, :, :], rwf[:, :, :], rw[0][:, :, :]).then_inc(s["wl"], 1)
                    dve.wait_ge(s["kd"], 1)
                    if cross:
                        for n in range(2 * NC):
                            c, half = n // 2, n % 2
                            cols = slice(half * 4 * SC, (half + 1) * 4 * SC)
                            dve.wait_ge(s["khm"], n + 1)
                            dve.scalar_tensor_tensor(kk[:, c, cols], bank(n % 2, 4 * SC), bk[:, c:c + 1],
                                                     hm_of(n).bitcast(F32),
                                                     ALU.add, ALU.subtract).then_inc(s["kst"], 1)
                        for n in range(4):
                            dve.wait_ge(s["vp"], n + 1)
                            src = bank(2 + n % 2, 512, SC).rearrange("p (b n) -> p b n", b=2)
                            bb = bv[0:SC, :].unsqueeze(1).to_broadcast([SC, 2, 256])
                            dve.tensor_tensor(tmp[0:SC, :, :], src, bb, ALU.add)
                            dve.drain()
                            dve.tensor_copy(vall[0][0:SC, 2 * n:2 * n + 2, :], tmp[0:SC, :, :])
                            dve.drain()
                            lo_of(dve, vall[1][0:SC, 2 * n:2 * n + 2, :], tmp[0:SC, :, :],
                                  vall[0][0:SC, 2 * n:2 * n + 2, :]).then_inc(s["vl"], 1)
                            dve.drain()
                    pipeline(dve, dve_steps(dve))

                @block.scalar
                def _(act):
                    if cross:
                        for n in range(5):
                            act.wait_ge(s["cT"], n + 1)
                            w = P if n < 4 else B * SC - 512
                            src = bank(n % 2, KD * P).rearrange("p (k s) -> p k s", k=KD)[:, :, 0:w]
                            act.activation(cT[0][:, :, n * P:n * P + w], src, ACT.Copy).then_inc(s["cTh"], 1)
                    for n in range(len(pieces)):
                        act.wait_ge(s[f"w{n % 3}"], 16 * (n // 3) + 16)
                        act.activation(pieces[n][0], staged(n), ACT.Copy).then_inc(s["wh"], 1)
                    act.wait_ge(s["vh"], 1)
                    if cross:
                        for n in range(2 * NC):
                            c = n // 2
                            act.wait_ge(s["kp"], n + 1)
                            if n >= 2:
                                act.wait_ge(s["kst"], n - 1)
                            act.activation(hm_of(n),
                                           bank(n % 2, 4 * SC), ACT.Identity, bias=sbk[:, c:c + 1],
                                           scale=low[:, 1:2]).then_inc(s["khm"], 1)
                    pipeline(act, act_steps(act))

                @block.tensor
                def _(pe):
                    if cross:
                        pe.wait_ge(s["cx"], 16 * 7)
                        for n in range(5):
                            w = P if n < 4 else B * SC - 512
                            if n >= 2:
                                pe.wait_ge(s["cTl"], n - 1)
                            for kd in range(KD):
                                ins = pe.transpose(bank(n % 2)[:, kd * P:kd * P + w], cx[0:w, n, kd * P:(kd + 1) * P],
                                                   ident[0:w, 0:w])
                            ins.then_inc(s["cT"], 1)
                        pe.wait_ge(s["cTl"], 5)
                        pe.wait_ge(s["wl"], whole["wk"])
                        for n in range(2 * NC):
                            c, half = n // 2, n % 2
                            cols = slice(half * 4 * SC, (half + 1) * 4 * SC)
                            if n >= 2:
                                pe.wait_ge(s["kst"], n - 1)
                            product(pe, bank(n % 2, 4 * SC),
                                    [lambda kd, a=a: wk[a][:, kd, c * P:(c + 1) * P] for a in range(2)],
                                    [lambda kd, a=a: cT[a][:, kd, cols] for a in range(2)], KD).then_inc(s["kp"], 1)
                        pe.wait_ge(s["wl"], whole["wv"])
                        for n in range(4):
                            if n >= 2:
                                pe.wait_ge(s["vl"], n - 1)
                            for u in range(2):
                                b0 = (2 * n + u) * SC
                                ins = product(pe, bank(2 + n % 2, 512, SC)[:, u * 256:(u + 1) * 256],
                                              [lambda kd, a=a: cT[a][:, kd, b0:b0 + SC] for a in range(2)],
                                              [lambda kd, a=a: wv[a][:, kd, :] for a in range(2)], KD)
                            ins.then_inc(s["vp"], 1)
                        pe.wait_ge(s["kst"], 2 * NC)
                        pe.wait_ge(s["vl"], 4)
                    pe.wait_ge(s["kd"], 1)
                    pe.wait_ge(s["wl"], len(pieces) + (0 if cross else 1))
                    pipeline(pe, pe_steps(pe))

        stage_done()
        softmax_attention("a_", D // H, 64, SC, 1, True, None)
        stage_done()

        moe = ExitStack()
        with moe:
            def mb(name, shape, dt=F32):
                return moe.enter_context(nc.sbuf_tensor(name, shape, dt))

            hln = mb("hln", [P, NT, D])
            expert_of = mb("expert_of", [1, SLOT_TILES], I32)
            with nc.sbuf_tensor("mo", [P, NT, D], F32) as mo, nc.sbuf_tensor("lgT", [E, NT * P], F32) as lgT:
                with nc.sbuf_tensor("rwh", [P, KD, E], F32R) as rwh, nc.sbuf_tensor("rwl", [P, KD, E], F32R) as rwl, \
                        nc.sbuf_tensor("rb", [E, 1], F32) as rb, nc.sbuf_tensor("moTh", [P, KD, S], F32R) as moTh, \
                        nc.sbuf_tensor("moTl", [P, KD, S], F32R) as moTl, nc.sbuf_tensor("zeros", [P, D], F32) as zeros:
                    softmax_attention("b_", D // 2 // H, 32, P, TPB, False,
                                      (mo, hln, (rwh, rwl), rb, (moTh, moTl), lgT, zeros))
                    stage_done()
                route(nc, sem, ps, ident, ones, before, mo, lgT, route_i, route_w, expert_of, x_slots)
            stage_done()
            experts(nc, sem, ps, t, ident, expert_of, x_slots, y_slots)
            stage_done()
            layer_1(nc, sem, ps, t, x, hln, ident, ident16, ones, minus_half, gates, route_i, route_w, y_slots, out)


def route(nc, sem, ps, ident, ones, before, mo, lgT, route_i, route_w, expert_of, x_slots):
    st = ExitStack()

    def tb(name, shape, dt=F32):
        return st.enter_context(nc.sbuf_tensor("r_" + name, shape, dt))

    prob = tb("prob", [P, NT, E])
    red = tb("red", [P, NT])
    rec = tb("rec", [P, NT])
    top = tb("top", [P, NT, 8])
    topi = tb("topi", [P, NT, 8], U32)
    topf = tb("topf", [P, NT, TOPK])
    iota_e = tb("iota_e", [P, E])
    iota_s = tb("iota_s", [1, SLOT_TILES])
    one_hot = tb("one_hot", [P, TOPK, NT, E])
    both = tb("both", [P, NT, E])
    total = tb("total", [P, E, NT])
    upto = tb("upto", [P, E, NT])
    tiles = tb("tiles", [P, E])
    tend = tb("tend", [P, E])
    base = tb("base", [P, E])
    place = tb("place", [P, NT, E])
    pick = tb("pick", [P, TOPK, NT, E])
    pos = tb("pos", [P, TOPK, NT])
    passed = tb("passed", [1, SLOT_TILES, E])
    npass = tb("npass", [1, SLOT_TILES])
    idx = tb("idx", [P, TOPK], U32)
    logits = tb("logits", [P, NT, E])
    s_lg = sem("r_lg")
    s_iota = sem("r_iota")
    s_max = sem("r_max")
    s_exp = sem("r_exp")
    s_one = sem("r_one")
    s_cnt = sem("r_cnt")
    s_pos = sem("r_pos")
    s_idx = sem("r_idx")
    s_sent = sem("r_sent")
    rank_ps = ps[:, 0, 0:NT * E].rearrange("p (t e) -> p t e", t=NT)
    total_ps = ps[:, 1, 0:NT * E].rearrange("p (t e) -> p e t", t=NT)
    ones_nt = ones[:, 0:NT]

    def over_experts(a):
        return a.unsqueeze(2).to_broadcast([P, NT, E])

    with st, nc.Block() as block:
        @block.gpsimd
        def _(pool):
            pool.iota(iota_e[:, :], [[1, E]], base=0, channel_multiplier=0, allow_small_or_imprecise_dtypes=True)
            pool.iota(iota_s[:, :], [[1, SLOT_TILES]], base=0, channel_multiplier=0,
                      allow_small_or_imprecise_dtypes=True).then_inc(s_iota, 1)
            pool.wait_ge(s_pos, 1)
            for tt in range(NT):
                for j in range(TOPK):
                    pool.indirect_dma_start(x_slots[:, :], bass.IndirectOffsetOnAxis(route_i[:, tt, j:j + 1], axis=0),
                                            mo[:, tt, :], None).then_inc(s_sent, 16)
            pool.wait_ge(s_sent, 16 * NT * TOPK)

        @block.scalar
        def _(act):
            act.wait_ge(s_max, 1)
            act.activation(prob[:, :, :], prob[:, :, :], ACT.Exp).then_inc(s_exp, 1)

        @block.tensor
        def _(pe):
            for tt in range(NT):
                ins = pe.transpose(ps[:, 2, tt * E:(tt + 1) * E], lgT[:, tt * P:(tt + 1) * P], ident[0:E, 0:E])
            ins.then_inc(s_lg, 1)
            pe.wait_ge(s_one, 1)
            rhs = both[:, :, :].rearrange("p t e -> p (t e)")
            pe.matmul(ps[:, 0, 0:NT * E], before[:, :], rhs, start=True, stop=True)
            pe.matmul(ps[:, 1, 0:NT * E], ones[:, :], rhs, start=True, stop=True).then_inc(s_cnt, 1)

        @block.vector
        def _(dve):
            dve.wait_ge(s_lg, 1)
            dve.tensor_copy(logits[:, :, :], ps[:, 2, 0:NT * E].rearrange("p (t e) -> p t e", t=NT))
            dve.drain()
            dve.tensor_reduce(red[:, :], logits[:, :, :], X, ALU.max)
            dve.drain()
            dve.tensor_tensor(prob[:, :, :], logits[:, :, :], over_experts(red[:, :]), ALU.subtract).then_inc(s_max, 1)
            dve.wait_ge(s_exp, 1)
            dve.tensor_reduce(red[:, :], prob[:, :, :], X, ALU.add)
            dve.drain()
            dve.reciprocal(rec[:, :], red[:, :])
            dve.drain()
            dve.tensor_tensor(prob[:, :, :], prob[:, :, :], over_experts(rec[:, :]), ALU.mult)
            dve.drain()
            for tt in range(NT):
                dve.max(top[:, tt, :], prob[:, tt, :])
            dve.drain()
            for tt in range(NT):
                dve.max_index(topi[:, tt, :], top[:, tt, :], prob[:, tt, :])
            dve.drain()
            dve.tensor_reduce(red[:, :], top[:, :, 0:TOPK], X, ALU.add)
            dve.tensor_copy(topf[:, :, :], topi[:, :, 0:TOPK])
            dve.drain()
            dve.tensor_scalar(red[:, :], red[:, :], 1e-8, None, ALU.add)
            dve.wait_ge(s_iota, 1)
            for j in range(TOPK):
                dve.tensor_tensor(one_hot[:, j, :, :], over_experts(topf[:, :, j]),
                                  iota_e[:, :].unsqueeze(1).to_broadcast([P, NT, E]), ALU.is_equal)
            dve.drain()
            dve.reciprocal(rec[:, :], red[:, :])
            dve.tensor_tensor(both[:, :, :], one_hot[:, 0, :, :], one_hot[:, 1, :, :], ALU.add).then_inc(s_one, 1)
            dve.drain()
            dve.tensor_tensor(route_w[:, :, :], top[:, :, 0:TOPK],
                              rec[:, :].unsqueeze(2).to_broadcast([P, NT, TOPK]), ALU.mult)
            dve.wait_ge(s_cnt, 1)
            dve.tensor_copy(total[:, :, :], total_ps)
            dve.drain()
            for e in range(E):
                dve.tensor_tensor_scan(upto[:, e, :], ones_nt, total[:, e, :], 0.0, ALU.mult, ALU.add)
            dve.drain()
            dve.tensor_scalar(tiles[:, :], upto[:, :, NT - 1], 127.0, 1.0 / P, ALU.add, ALU.mult)
            dve.drain()
            dve.tensor_scalar(tiles[:, :], tiles[:, :], -127.0 / 256, ROUND, ALU.add, ALU.add)
            dve.drain()
            dve.tensor_scalar(tiles[:, :], tiles[:, :], -ROUND, None, ALU.add)
            dve.drain()
            dve.tensor_tensor_scan(tend[:, :], ones[:, 0:E], tiles[:, :], 0.0, ALU.mult, ALU.add)
            dve.drain()
            dve.tensor_tensor(base[:, :], tend[:, :], tiles[:, :], ALU.subtract)
            dve.tensor_tensor(upto[:, :, :], upto[:, :, :], total[:, :, :], ALU.subtract)
            dve.tensor_tensor(passed[:, :, :], iota_s[:, :].unsqueeze(2).to_broadcast([1, SLOT_TILES, E]),
                              tend[0:1, :].unsqueeze(1).to_broadcast([1, SLOT_TILES, E]), ALU.is_ge)
            dve.drain()
            dve.tensor_tensor(place[:, :, :], rank_ps, upto[:, :, :].rearrange("p e t -> p t e"), ALU.add)
            dve.tensor_reduce(npass[:, :], passed[:, :, :], X, ALU.add)
            dve.tensor_scalar(base[:, :], base[:, :], float(P), None, ALU.mult)
            dve.drain()
            dve.tensor_scalar(npass[:, :], npass[:, :], float(E - 1), None, ALU.min)
            dve.tensor_tensor(place[:, :, :], place[:, :, :], base[:, :].unsqueeze(1).to_broadcast([P, NT, E]),
                              ALU.add)
            dve.drain()
            dve.tensor_copy(expert_of[:, :], npass[:, :])
            for j in range(TOPK):
                dve.tensor_tensor(pick[:, j, :, :], one_hot[:, j, :, :], place[:, :, :], ALU.mult)
            dve.drain()
            for j in range(TOPK):
                dve.tensor_reduce(pos[:, j, :], pick[:, j, :, :], X, ALU.add)
            dve.drain()
            dve.tensor_copy(route_i[:, :, :], pos[:, :, :].rearrange("p j t -> p t j")).then_inc(s_pos, 1)


def experts(nc, sem, ps, t, ident, expert_of, x_slots, y_slots):
    st = ExitStack()

    def tb(name, shape, dt=F32):
        return st.enter_context(nc.sbuf_tensor("e_" + name, shape, dt))

    FK = F0 // P
    w1 = tb("w1", [P, E, KD, F0])
    w2 = tb("w2", [P, E, FK, D])
    b1 = tb("b1", [P, E, F0])
    b2 = tb("b2", [P, E, D])
    xs = tb("xs", [P, 2, D])
    xsT = tb("xsT", [P, 2, KD, P])
    h = tb("h", [P, 2, F0])
    hT = tb("hT", [P, 2, FK, P])
    ys = tb("ys", [P, 2, D])
    s_w = sem("e_w")
    s_in = [sem("e_in0"), sem("e_in1")]
    s_xT = sem("e_xT")
    s_xTe = sem("e_xTe")
    s_h = sem("e_h")
    s_he = sem("e_he")
    s_hT = sem("e_hT")
    s_hTe = sem("e_hTe")
    s_y = sem("e_y")
    s_ye = sem("e_ye")
    s_out = [sem("e_out0"), sem("e_out1")]
    xT_ps = [ps[:, u, 0:KD * P].rearrange("p (k s) -> p k s", k=KD) for u in range(2)]
    h_ps = [ps[:, 2 + u, :] for u in range(2)]
    hT_ps = [ps[:, 4 + u, :].rearrange("p (k s) -> p k s", k=FK) for u in range(2)]
    y_ps = [ps[:, 6 + u, 0:D] for u in range(2)]
    xv = x_slots.rearrange("(i p) d -> i p d", p=P)
    yv = y_slots.rearrange("(i p) d -> i p d", p=P)
    N = SLOT_TILES // 2

    with st, nc.Block() as block:
        @block.sync
        def _(sp):
            sp.dma_start(w1[:, :, :, :], t["moe_w1"].rearrange("e (k p) f -> p e k f", p=P)).then_inc(s_w, 16)
            sp.dma_start(b1[:, :, :].rearrange("p e f -> p (e f)"),
                         t["moe_b1"].rearrange("e f -> (e f)").partition_broadcast(P)).then_inc(s_w, 16)
            sp.dma_start(w2[:, :, :, :], t["moe_w2"].rearrange("e (k p) f -> p e k f", p=P)).then_inc(s_w, 16)
            sp.dma_start(b2[:, :, :].rearrange("p e f -> p (e f)"),
                         t["moe_b2"].rearrange("e f -> (e f)").partition_broadcast(P)).then_inc(s_w, 16)
            sp.sem_inc(s_ye, 2)
            sp.sem_inc(s_out[0], 16)
            sp.sem_inc(s_out[1], 16)
            with sp.Fori(0, N) as i:
                for u in range(2):
                    sp.wait_ge(s_ye, 2 * i + u + 3)
                    sp.dma_start(yv[bass.ds(2 * i + u, 1)].rearrange("a p d -> (a p) d"), ys[:, u, :])\
                        .then_inc(s_out[u], 16)
            for u in range(2):
                sp.wait_ge(s_out[u], 16 * (N + 1))

        @block.gpsimd
        def _(pool):
            pool.sem_inc(s_xT, 2)
            with pool.Fori(0, N) as i:
                for u in range(2):
                    pool.wait_ge(s_xT, 2 * i + u + 1)
                    pool.dma_start(xs[:, u, :], xv[bass.ds(2 * i + u, 1)].rearrange("a p d -> (a p) d"))\
                        .then_inc(s_in[u], 16)

        @block.tensor
        def _(pe):
            pe.wait_ge(s_w, 64)
            with pe.Fori(0, N) as i:
                e = [pe.value_load(expert_of[0:1, bass.ds(2 * i + u, 1)], min_val=0, max_val=E - 1) for u in range(2)]
                for u in range(2):
                    pe.wait_ge(s_in[u], 16 * i + 16)
                    for kd in range(KD):
                        ins = pe.transpose(xT_ps[u][:, kd, :], xs[:, u, kd * P:(kd + 1) * P], ident[:, :])
                    ins.then_inc(s_xT, 1)
                for u in range(2):
                    pe.wait_ge(s_xTe, 2 * i + u + 1)
                    for kd in range(KD):
                        ins = pe.matmul(h_ps[u], xsT[:, u, kd, :], w1[:, bass.ds(e[u], 1), kd, :],
                                        start=(kd == 0), stop=(kd == KD - 1))
                    ins.then_inc(s_h, 1)
                for u in range(2):
                    pe.wait_ge(s_he, 2 * i + u + 1)
                    for kd in range(FK):
                        ins = pe.transpose(hT_ps[u][:, kd, :], h[:, u, kd * P:(kd + 1) * P], ident[:, :])
                    ins.then_inc(s_hT, 1)
                for u in range(2):
                    pe.wait_ge(s_hTe, 2 * i + u + 1)
                    for kd in range(FK):
                        ins = pe.matmul(y_ps[u], hT[:, u, kd, :], w2[:, bass.ds(e[u], 1), kd, :],
                                        start=(kd == 0), stop=(kd == FK - 1))
                    ins.then_inc(s_y, 1)

        @block.scalar
        def _(act):
            with act.Fori(0, N) as i:
                for u in range(2):
                    act.wait_ge(s_xT, 2 * i + u + 3)
                    act.activation(xsT[:, u, :, :], xT_ps[u], ACT.Copy).then_inc(s_xTe, 1)
                for u in range(2):
                    act.wait_ge(s_hT, 2 * i + u + 1)
                    act.activation(hT[:, u, :, :], hT_ps[u], ACT.Gelu).then_inc(s_hTe, 1)

        @block.vector
        def _(dve):
            dve.wait_ge(s_w, 64)
            with dve.Fori(0, N) as i:
                e = [dve.value_load(expert_of[0:1, bass.ds(2 * i + u, 1)], min_val=0, max_val=E - 1) for u in range(2)]
                for u in range(2):
                    dve.wait_ge(s_h, 2 * i + u + 1)
                    dve.tensor_tensor(h[:, u, :], h_ps[u], b1[:, bass.ds(e[u], 1), :]
                                      .rearrange("p a f -> p (a f)"), ALU.add).then_inc(s_he, 1)
                for u in range(2):
                    dve.wait_ge(s_y, 2 * i + u + 1)
                    dve.wait_ge(s_out[u], 16 * i + 16)
                    dve.tensor_tensor(ys[:, u, :], y_ps[u], b2[:, bass.ds(e[u], 1), :]
                                      .rearrange("p a f -> p (a f)"), ALU.add).then_inc(s_ye, 1)


def layer_1(nc, sem, ps, t, x, hln, ident, ident16, ones, minus_half, gates, route_i, route_w, y_slots, out):
    st = ExitStack()

    def tb(name, shape, dt=F32):
        return st.enter_context(nc.sbuf_tensor("c_" + name, shape, dt))

    IK = INNER // P
    FK = FF // P
    wq = tb("wq", [P, KD, INNER])
    wk = tb("wk", [P, KD, INNER])
    wv = tb("wv", [P, KD, INNER])
    wo = tb("wo", [P, IK, D])
    w1 = tb("w1", [P, KD, FF])
    w2 = tb("w2", [P, FK, D])
    b1 = tb("b1", [P, FK])
    lnw = tb("lnw", [P, 4, KD])
    bo = tb("bo", [P, D])
    b2 = tb("b2", [P, D])
    f_stats = tb("f_stats", [P, TPB, 6])
    f_mv = tb("f_mv", [P, TPB, 2])
    f_var = tb("f_var", [P, TPB])
    f_rstd = tb("f_rstd", [P, TPB])
    c_stats = tb("c_stats", [P, 6])
    c_mv = tb("c_mv", [P, 2])
    c_var = tb("c_var", [P, 1])
    c_rstd = tb("c_rstd", [P, 1])
    idx = tb("idx", [P, TPB * TOPK], U32)
    yg = tb("yg", [P, TPB, TOPK, D])
    mix = tb("mix", [P, TPB, D])
    xq = tb("xq", [P, TPB, D])
    xh = tb("xh", [P, TPB, D])
    xT = tb("xT", [P, KD, S])
    cx = tb("cx", [P, D])
    cT = tb("cT", [P, KD, SC])
    ksq = tb("ksq", [P, INNER])
    kss = tb("kss", [P, H])
    krn = tb("krn", [P, H])
    kn = tb("kn", [P, INNER])
    vv = tb("vv", [P, INNER])
    mT = tb("mT", [P, IK, P])
    gm = tb("gm", [P, IK, D])
    b_stats = tb("b_stats", [P, TPB, 6])
    b_mv = tb("b_mv", [P, TPB, 2])
    b_var = tb("b_var", [P, TPB])
    b_rstd = tb("b_rstd", [P, TPB])
    qsq = tb("qsq", [P, INNER])
    qss = tb("qss", [P, H])
    qrn = tb("qrn", [P, H])
    qn = tb("qn", [P, INNER])
    qT = tb("qT", [P, TPB, IK, P])
    xo = tb("xo", [P, TPB, D])
    xh2 = tb("xh2", [P, TPB, D])
    xT2 = tb("xT2", [P, KD, S])
    hT = tb("hT", [P, FK, S])
    wb = [tb("wb1", [P, KD, FF], BF16), tb("wb2", [P, FK, D], BF16)]
    part = tb("part", [P, 2])
    sw = tb("sw", [P, 2])
    half = tb("half", [P, 2, 2])
    t_stats = tb("t_stats", [P, 6])
    t_mv = tb("t_mv", [P, 2])
    t_var = tb("t_var", [P, 1])
    t_rstd = tb("t_rstd", [P, 1])
    th = tb("th", [P, D])
    tr = tb("tr", [P, D])
    ti = tb("ti", [P, D], BF16)
    tT = tb("tT", [P, KD, P], BF16)
    g = tb("g", [P, FF])
    gr = tb("gr", [P, FF])
    gi = tb("gi", [P, FF], BF16)
    gT = tb("gT", [P, FK, P], BF16)
    am = tb("am", [P, 2])
    sc = tb("sc", [P, 2])
    un = tb("un", [P, 2])
    wf = [tb("wf1", [P, KD, FF]), tb("wf2", [P, FK, D])]
    neg = tb("neg", [P, KD * FF])

    names = "w wt ctx gath cvar crstd cn cT cTe v ve k ks kss kr kn M Me G Ge xvar xrstd qvar qrstd xn xT xTe " \
            "q qs qss qr qn qT qTe o ovar orstd x2 x2T x2Te h he y ye " \
            "part sum tvar trstd ti tT tTe g ge gi gT gTe ty fin store".split()
    s = {n: sem("c_s_" + n) for n in names}

    front = ps[:, 0:2, :].rearrange("p b n -> p (b n)")
    back = ps[:, 2:4, :].rearrange("p b n -> p (b n)")
    cT_ps = ps[:, 0, 0:KD * SC].rearrange("p (k s) -> p k s", k=KD)
    xT_ps = ps[:, 0, :].rearrange("p (k s) -> p k s", k=KD)
    x2T_ps = ps[:, 4, :].rearrange("p (k s) -> p k s", k=KD)
    o_ps = ps[:, 4, :].rearrange("p (t d) -> p t d", t=TPB)
    g_ps = ps[:, 5:7, :].rearrange("p b n -> p (b n)")
    tT_ps = ps[:, 7, 0:P].bitcast(BF16).rearrange("p (k s) -> p k s", k=KD)
    gT_ps = ps[:, 7, :].bitcast(BF16).rearrange("p (k s) -> p k s", k=FK)
    ty_ps = ps[:, 7, 0:D]
    sum_ps = ps[:, 7, 0:2]
    ov = out.rearrange("b (t p) d -> (b t) p d", p=P)

    STEPS = ("t0_stats f_gather t0_i b_q0 b_xo f_v t0_h b_n0 t0_q b_q1 f_k t0_y b_n1 f_kn t0_out t1_stats t1_i f_mix "
             "b_o f_m f_me t1_h b_x f_g0 b_h f_q t1_q t1_y f_g1 g_ctx f_x g_cn f_xT g_cT b_y t1_out").split()

    def heads(a):
        return a.rearrange("p (h e) -> p h e", h=H)

    def after(eng, semaphore, n):
        if not (isinstance(n, int) and n <= 0):
            eng.wait_ge(semaphore, n)

    def run(parts, i, streams):
        for name in STEPS:
            if name in parts and name[0] in streams:
                kind = name[0]
                if kind == "g":
                    parts[name](i + 2)
                elif kind == "f":
                    parts[name](i + 1)
                elif kind == "b":
                    parts[name](i)
                else:
                    parts[name](TPB * (i - 1) + int(name[1]))

    def pipeline(eng, parts, prepare=None):
        run(parts, -2, "g")
        run(parts, -1, "gf")
        run(parts, 0, "gfb")
        if prepare:
            prepare()
        with eng.Fori(0, B - 3) as j:
            run(parts, j + 1, "gfbt")
        run(parts, B - 2, "fbt")
        run(parts, B - 1, "bt")
        run(parts, B, "t")

    with st, nc.Block() as block:
        @block.sync
        def _(sp):
            sp.dma_start(cx[0:SC, :], t["ctx"][0]).then_inc(s["ctx"], 16)
            for dst, n in ((wv, "l1_wv"), (wk, "l1_wk"), (wo, "l1_wo"), (wq, "l1_wq"), (w1, "l1_w1"), (w2, "l1_w2")):
                sp.dma_start(dst[:, :, :], t[n].rearrange("(k p) n -> p k n", p=P)).then_inc(s["w"], 16)
            sp.dma_start(b1[:, :], t["l1_b1"]).then_inc(s["w"], 16)
            sp.dma_start(lnw[:, :, :], t["l1_ln"]).then_inc(s["w"], 16)
            sp.dma_start(bo[:, :], t["l1_bo"].partition_broadcast(P)).then_inc(s["w"], 16)
            sp.dma_start(b2[:, :], t["l1_b2"].partition_broadcast(P)).then_inc(s["w"], 16)
            sp.dma_start(wf[0][:, :, :], t["ff_w1t"].rearrange("(k p) n -> p k n", p=P)).then_inc(s["wt"], 16)
            sp.dma_start(wf[1][:, :, :], t["ff_w2t"].rearrange("(k p) n -> p k n", p=P)).then_inc(s["wt"], 16)
            with sp.Fori(0, B - 1) as j:
                sp.wait_ge(s["cT"], j + 1)
                sp.dma_start(cx[0:SC, :], t["ctx"][bass.ds(j + 1, 1)].rearrange("a s d -> (a s) d"))\
                    .then_inc(s["ctx"], 16)

        @block.gpsimd
        def _(pool):
            def rsqrt(dst, src, n, wanted, done):
                pool.wait_ge(s[wanted], n)
                w = src.shape[-1]
                r = src.shape[0]
                pool.tensor_tensor(dst, src, minus_half[0:r, 0:w], ALU.pow).then_inc(s[done], 1)

            def gather(f):
                after(pool, s["gath"], 64 * f)
                after(pool, s["xvar"], f)
                pool.tensor_copy(idx[:, :], route_i[:, bass.ds(TPB * f, TPB), :].rearrange("p t j -> p (t j)"))
                pool.drain()
                for tt in range(TPB):
                    for j in range(TOPK):
                        n = tt * TOPK + j
                        pool.indirect_dma_start(yg[:, tt, j, :], None, y_slots[:, :],
                                                bass.IndirectOffsetOnAxis(idx[:, n:n + 1], axis=0))\
                            .then_inc(s["gath"], 16)

            parts = {
                "f_gather": gather,
                "g_ctx": lambda f: rsqrt(c_rstd[0:SC, :], c_var[0:SC, :], f + 1, "cvar", "crstd"),
                "f_k": lambda f: rsqrt(krn[0:SC, :], kss[0:SC, :], f + 1, "kss", "kr"),
                "f_mix": lambda f: rsqrt(f_rstd[:, :], f_var[:, :], f + 1, "xvar", "xrstd"),
                "f_q": lambda f: rsqrt(f_rstd[:, :], f_var[:, :], f + 1, "qvar", "qrstd"),
                "b_q0": lambda i: rsqrt(qrn[:, :], qss[:, :], TPB * i + 1, "qss", "qr"),
                "b_q1": lambda i: rsqrt(qrn[:, :], qss[:, :], TPB * i + 2, "qss", "qr"),
                "b_o": lambda i: rsqrt(b_rstd[:, :], b_var[:, :], i + 1, "ovar", "orstd"),
                "t0_stats": lambda n: rsqrt(t_rstd[:, :], t_var[:, :], n + 1, "tvar", "trstd"),
                "t1_stats": lambda n: rsqrt(t_rstd[:, :], t_var[:, :], n + 1, "tvar", "trstd"),
            }
            pipeline(pool, parts)

        @block.vector
        def _(dve):
            def norm_stats(src, n, stats, mv, var, done):
                for tt in range(n):
                    dve.bn_stats(stats[:, tt, :], src(tt))
                dve.drain()
                for tt in range(n):
                    dve.bn_aggr(mv[:, tt, :], stats[:, tt, :])
                dve.drain()
                dve.tensor_scalar(var[:, :], mv[:, :, 1], EPS, None, ALU.add).then_inc(s[done], 1)

            def gained(dst, src, first):
                for kd in range(KD):
                    ins = dve.tensor_scalar(dst[:, kd, :], src[:, kd, :], lnw[:, first, kd:kd + 1],
                                            lnw[:, first + 1, kd:kd + 1], ALU.mult, ALU.add)
                return ins

            def f_ctx(f):
                dve.wait_ge(s["ctx"], 16 * f + 16)
                dve.bn_stats(c_stats[0:SC, :], cx[0:SC, :])
                dve.drain()
                dve.bn_aggr(c_mv[0:SC, :], c_stats[0:SC, :])
                dve.drain()
                dve.tensor_scalar(c_var[0:SC, :], c_mv[0:SC, 1:2], EPS, None, ALU.add).then_inc(s["cvar"], 1)

            def f_cn(f):
                dve.wait_ge(s["crstd"], f + 1)
                dve.tensor_scalar(cx[0:SC, :], cx[0:SC, :], c_mv[0:SC, 0:1], c_rstd[0:SC, 0:1],
                                  ALU.subtract, ALU.mult).then_inc(s["cn"], 1)

            def f_cTe(f):
                dve.wait_ge(s["cT"], f + 1)
                after(dve, s["k"], f)
                gained(cT, cT_ps, 0).then_inc(s["cTe"], 1)

            def f_k(f):
                dve.wait_ge(s["ks"], f + 1)
                dve.tensor_reduce(kss[0:SC, :], heads(ksq[0:SC, :]), X, ALU.add)
                dve.drain()
                dve.tensor_scalar(kss[0:SC, :], kss[0:SC, :], 1e-24, None, ALU.max).then_inc(s["kss"], 1)

            def f_kn(f):
                dve.wait_ge(s["kr"], f + 1)
                dve.tensor_tensor(heads(kn[0:SC, :]), heads(front[0:SC, :]),
                                  krn[0:SC, :].unsqueeze(2).to_broadcast([SC, H, HD1]), ALU.mult)\
                    .then_inc(s["kn"], 1)

            def f_me(f):
                dve.wait_ge(s["M"], f + 1)
                after(dve, s["G"], 2 * f)
                for u in range(2):
                    rows = slice(64 * u, 64 * u + 64)
                    ins = dve.tensor_copy(mT[rows, :, rows],
                                          front[rows, :].rearrange("p (c n) -> p c n", c=IK)[:, :, rows])
                ins.then_inc(s["Me"], 1)

            def f_mix(f):
                dve.wait_ge(s["gath"], 64 * f + 64)
                for tt in range(TPB):
                    dve.tensor_scalar(mix[:, tt, :], yg[:, tt, 0, :], route_w[:, bass.ds(TPB * f + tt, 1), 0],
                                      None, ALU.mult)
                dve.drain()
                for tt in range(TPB):
                    dve.scalar_tensor_tensor(mix[:, tt, :], yg[:, tt, 1, :], route_w[:, bass.ds(TPB * f + tt, 1), 1],
                                             mix[:, tt, :], ALU.mult, ALU.add)
                dve.drain()
                dve.scalar_tensor_tensor(mix[:, :, :], mix[:, :, :], 0.3, hln[:, bass.ds(TPB * f, TPB), :],
                                         ALU.mult, ALU.add)
                dve.drain()
                xb = x[:, bass.ds(TPB * f, TPB), :]
                dve.scalar_tensor_tensor(xb, mix[:, :, :], gates[:, 1:2], xb, ALU.mult, ALU.add)
                dve.drain()
                norm_stats(lambda tt: x[:, bass.ds(TPB * f + tt, 1), :], TPB, f_stats, f_mv, f_var, "xvar")

            def f_q(f):
                dve.wait_ge(s["xrstd"], f + 1)
                for tt in range(TPB):
                    dve.tensor_scalar(xq[:, tt:tt + 1, :], x[:, bass.ds(TPB * f + tt, 1), :], f_mv[:, tt, 0:1],
                                      f_rstd[:, tt:tt + 1], ALU.subtract, ALU.mult)
                dve.drain()
                norm_stats(lambda tt: xq[:, tt, :], TPB, f_stats, f_mv, f_var, "qvar")

            def f_x(f):
                dve.wait_ge(s["qrstd"], f + 1)
                after(dve, s["xT"], f)
                for tt in range(TPB):
                    ins = dve.tensor_scalar(xh[:, tt, :], xq[:, tt, :], f_mv[:, tt, 0:1], f_rstd[:, tt:tt + 1],
                                            ALU.subtract, ALU.mult)
                ins.then_inc(s["xn"], 1)

            def f_xT(f):
                dve.wait_ge(s["xT"], f + 1)
                after(dve, s["q"], TPB * f)
                gained(xT, xT_ps, 0).then_inc(s["xTe"], 1)

            def b_q(n):
                dve.wait_ge(s["qs"], n + 1)
                dve.tensor_reduce(qss[:, :], heads(qsq[:, :]), X, ALU.add)
                dve.drain()
                dve.tensor_scalar(qss[:, :], qss[:, :], 1e-24, None, ALU.max).then_inc(s["qss"], 1)

            def b_n(n):
                dve.wait_ge(s["qr"], n + 1)
                after(dve, s["qT"], n)
                dve.tensor_tensor(heads(qn[:, :]), heads(back), qrn[:, :].unsqueeze(2).to_broadcast([P, H, HD1]),
                                  ALU.mult).then_inc(s["qn"], 1)

            def b_xo(i):
                dve.tensor_tensor(xo[:, :, :], xq[:, :, :], bo[:, :].unsqueeze(1).to_broadcast([P, TPB, D]), ALU.add)
                dve.drain()

            def b_o(i):
                dve.wait_ge(s["o"], i + 1)
                dve.tensor_tensor(xo[:, :, :], xo[:, :, :], o_ps, ALU.add)
                dve.drain()
                norm_stats(lambda tt: xo[:, tt, :], TPB, b_stats, b_mv, b_var, "ovar")

            def b_x(i):
                dve.wait_ge(s["orstd"], i + 1)
                after(dve, s["x2T"], i)
                for tt in range(TPB):
                    ins = dve.tensor_scalar(xh2[:, tt, :], xo[:, tt, :], b_mv[:, tt, 0:1], b_rstd[:, tt:tt + 1],
                                            ALU.subtract, ALU.mult)
                ins.then_inc(s["x2"], 1)
                dve.drain()
                dve.tensor_tensor(xo[:, :, :], xo[:, :, :], b2[:, :].unsqueeze(1).to_broadcast([P, TPB, D]), ALU.add)

            def b_h(i):
                dve.wait_ge(s["x2T"], i + 1)
                after(dve, s["h"], 4 * i)
                gained(xT2, x2T_ps, 2).then_inc(s["x2Te"], 1)

            def b_y(i):
                dve.wait_ge(s["y"], i + 1)
                dve.tensor_tensor(xo[:, :, :], xo[:, :, :], o_ps, ALU.add).then_inc(s["ye"], 1)
                dve.drain()
                xb = x[:, bass.ds(TPB * i, TPB), :]
                dve.scalar_tensor_tensor(xb, xo[:, :, :], gates[:, 2:3], xb, ALU.mult, ALU.add)
                dve.drain()

            def quantise(src, n, rounded, dst):
                dve.tensor_reduce(am[:, n:n + 1], src, X, ALU.max, apply_absolute_value=True)
                dve.drain()
                dve.tensor_scalar(am[:, n:n + 1], am[:, n:n + 1], EPS, None, ALU.max)
                dve.drain()
                dve.reciprocal(sc[:, n:n + 1], am[:, n:n + 1])
                dve.tensor_scalar(un[:, n:n + 1], am[:, n:n + 1], sw[:, n:n + 1], 1.0 / 127, ALU.mult, ALU.mult)
                dve.drain()
                dve.tensor_scalar(sc[:, n:n + 1], sc[:, n:n + 1], 127.0, None, ALU.mult)
                dve.drain()
                dve.tensor_scalar(rounded, src, sc[:, n:n + 1], ROUND, ALU.mult, ALU.add)
                dve.drain()
                return dve.tensor_scalar(dst, rounded, -ROUND, 127.0, ALU.add, ALU.min)

            def tile(n):
                return x[:, bass.ds(n, 1), :].rearrange("p a d -> p (a d)")

            def t_stats_of(n):
                dve.bn_stats(t_stats[:, :], tile(n))
                dve.drain()
                dve.bn_aggr(t_mv[:, :], t_stats[:, :])
                dve.drain()
                dve.tensor_scalar(t_var[:, :], t_mv[:, 1:2], EPS, None, ALU.add).then_inc(s["tvar"], 1)

            def t_i(n):
                dve.wait_ge(s["trstd"], n + 1)
                dve.tensor_scalar(th[:, :], tile(n), t_mv[:, 0:1], t_rstd[:, 0:1], ALU.subtract, ALU.mult)
                dve.drain()
                after(dve, s["tT"], n)
                quantise(th[:, :], 0, tr[:, :], ti[:, :]).then_inc(s["ti"], 1)

            def t_q(n):
                dve.wait_ge(s["ge"], n + 1)
                after(dve, s["gT"], n)
                quantise(g[:, :], 1, gr[:, :], gi[:, :]).then_inc(s["gi"], 1)

            def t_out(n):
                dve.wait_ge(s["ty"], n + 1)
                dve.tensor_scalar(tr[:, :], ty_ps, un[:, 1:2], gates[:, 3:4], ALU.mult, ALU.mult)
                dve.drain()
                dve.tensor_tensor(tile(n), tr[:, :], tile(n), ALU.add).then_inc(s["fin"], 1)

            def ternary_weights():
                dve.wait_ge(s["wt"], 32)
                flat = [w[:, :, :].rearrange("p k n -> p (k n)") for w in wf]
                flatb = [w[:, :, :].rearrange("p k n -> p (k n)") for w in wb]
                for n in range(2):
                    ins = dve.tensor_reduce(part[:, n:n + 1], flat[n], X, ALU.add, apply_absolute_value=True)
                ins.then_inc(s["part"], 1)
                dve.wait_ge(s["sum"], 1)
                dve.tensor_scalar(sw[:, :], sum_ps, 1.0 / (D * FF), EPS, ALU.mult, ALU.max)
                dve.drain()
                dve.tensor_scalar(half[:, :, 0], sw[:, :], 0.5, None, ALU.mult)
                dve.tensor_scalar(half[:, :, 1], sw[:, :], -0.5, None, ALU.mult)
                dve.drain()
                for n in range(2):
                    dve.tensor_scalar(neg[:, :], flat[n], half[:, n, 1:2], None, ALU.is_lt)
                    dve.drain()
                    dve.scalar_tensor_tensor(flatb[n], flat[n], half[:, n, 0:1], neg[:, :], ALU.is_gt, ALU.subtract)
                    dve.drain()

            dve.memset(mT[:, :, :], 0.0)
            dve.wait_ge(s["w"], 160)
            parts = {
                "g_ctx": f_ctx, "g_cn": f_cn, "g_cT": f_cTe, "f_k": f_k, "f_kn": f_kn, "f_me": f_me, "f_mix": f_mix,
                "f_q": f_q, "f_x": f_x, "f_xT": f_xT,
                "b_q0": lambda i: b_q(TPB * i), "b_q1": lambda i: b_q(TPB * i + 1),
                "b_n0": lambda i: b_n(TPB * i), "b_n1": lambda i: b_n(TPB * i + 1),
                "b_o": b_o, "b_x": b_x, "b_h": b_h, "b_y": b_y,
                "t0_stats": t_stats_of, "t1_stats": t_stats_of, "t0_i": t_i, "t1_i": t_i,
                "b_xo": b_xo, "t0_q": t_q, "t1_q": t_q, "t0_out": t_out, "t1_out": t_out,
            }
            pipeline(dve, parts, ternary_weights)

        @block.scalar
        def _(act):
            def f_v(f):
                act.wait_ge(s["v"], f + 1)
                after(act, s["M"], f)
                act.activation(vv[0:SC, :], front[0:SC, :], ACT.Copy).then_inc(s["ve"], 1)

            def f_k(f):
                act.wait_ge(s["k"], f + 1)
                after(act, s["kss"], f)
                act.activation(ksq[0:SC, :], front[0:SC, :], ACT.Square).then_inc(s["ks"], 1)

            def f_g(f, h):
                act.wait_ge(s["G"], 2 * f + h + 1)
                if h == 0:
                    after(act, s["o"], f)
                act.activation(gm[:, 4 * h:4 * h + 4, :].rearrange("p c n -> p (c n)"), front, ACT.Copy)\
                    .then_inc(s["Ge"], 1)

            def b_q(n):
                act.wait_ge(s["q"], n + 1)
                after(act, s["qss"], n)
                act.activation(qsq[:, :], back, ACT.Square).then_inc(s["qs"], 1)

            def b_n(i, tt):
                act.wait_ge(s["qT"], TPB * i + tt + 1)
                if tt == 0:
                    after(act, s["o"], i)
                act.activation(qT[:, tt, :, :].rearrange("p c n -> p (c n)"), back, ACT.Copy).then_inc(s["qTe"], 1)

            def b_h(i):
                for n in range(4):
                    act.wait_ge(s["h"], 4 * i + n + 1)
                    if n == 0:
                        after(act, s["y"], i)
                    for c in (2 * n, 2 * n + 1):
                        ins = act.activation(hT[:, c, :], back[:, (c % 4) * S:(c % 4 + 1) * S], ACT.Gelu,
                                             bias=b1[:, c:c + 1])
                    ins.then_inc(s["he"], 1)

            def t_h(n):
                act.wait_ge(s["tT"], n + 1)
                after(act, s["g"], n)
                act.activation(tT[:, :, :], tT_ps, ACT.Copy).then_inc(s["tTe"], 1)
                act.wait_ge(s["g"], n + 1)
                after(act, s["gi"], n)
                act.activation(g[:, :], g_ps, ACT.Gelu, scale=un[:, 0:1]).then_inc(s["ge"], 1)

            def t_y(n):
                act.wait_ge(s["gT"], n + 1)
                after(act, s["ty"], n)
                act.activation(gT[:, :, :], gT_ps, ACT.Copy).then_inc(s["gTe"], 1)

            parts = {
                "f_v": f_v, "f_k": f_k, "f_g0": lambda f: f_g(f, 0), "f_g1": lambda f: f_g(f, 1),
                "b_q0": lambda i: b_q(TPB * i), "b_q1": lambda i: b_q(TPB * i + 1),
                "b_n0": lambda i: b_n(i, 0), "b_n1": lambda i: b_n(i, 1), "b_h": b_h,
                "t0_h": t_h, "t1_h": t_h, "t0_y": t_y, "t1_y": t_y,
            }
            act.wait_ge(s["w"], 160)
            pipeline(act, parts)

        @block.tensor
        def _(pe):
            def transposes(dst, src):
                for tt in range(TPB):
                    for kd in range(KD):
                        ins = pe.transpose(dst[:, kd, tt * P:(tt + 1) * P], src[:, tt, kd * P:(kd + 1) * P], ident[:, :])
                return ins

            def rows(dst, lhsT, w, n):
                for half in range(INNER // 512):
                    for kd in range(KD):
                        ins = pe.matmul(dst[0:n, half * 512:(half + 1) * 512], lhsT(kd),
                                        w[:, kd, half * 512:(half + 1) * 512], start=(kd == 0), stop=(kd == KD - 1))
                return ins

            def f_cT(f):
                pe.wait_ge(s["cn"], f + 1)
                after(pe, s["xTe"], f)
                for kd in range(KD):
                    ins = pe.transpose(cT_ps[:, kd, :], cx[0:SC, kd * P:(kd + 1) * P], ident[0:SC, 0:SC])
                ins.then_inc(s["cT"], 1)

            def f_v(f):
                pe.wait_ge(s["cTe"], f + 1)
                rows(front, lambda kd: cT[:, kd, :], wv, SC).then_inc(s["v"], 1)

            def f_k(f):
                pe.wait_ge(s["ve"], f + 1)
                rows(front, lambda kd: cT[:, kd, :], wk, SC).then_inc(s["k"], 1)

            def f_m(f):
                pe.wait_ge(s["kn"], f + 1)
                for c in range(IK):
                    cols = slice(c * P, (c + 1) * P)
                    ins = pe.matmul(front[:, cols], vv[0:SC, cols], kn[0:SC, cols], start=True, stop=True)
                ins.then_inc(s["M"], 1)

            def f_g(f, h):
                if h == 0:
                    pe.wait_ge(s["Me"], f + 1)
                else:
                    pe.wait_ge(s["Ge"], 2 * f + 1)
                for c in range(4):
                    ins = pe.matmul(front[:, c * D:(c + 1) * D], mT[:, 4 * h + c, :], wo[:, 4 * h + c, :],
                                    start=True, stop=True)
                ins.then_inc(s["G"], 1)

            def f_x(f):
                pe.wait_ge(s["xn"], f + 1)
                pe.wait_ge(s["Ge"], 2 * f + 2)
                transposes(xT_ps, xh).then_inc(s["xT"], 1)

            def b_q(i, tt):
                if tt == 0:
                    pe.wait_ge(s["xTe"], i + 1)
                    after(pe, s["he"], 4 * i)
                else:
                    pe.wait_ge(s["qTe"], TPB * i + 1)
                rows(back, lambda kd: xT[:, kd, tt * P:(tt + 1) * P], wq, P).then_inc(s["q"], 1)

            def b_n(n):
                pe.wait_ge(s["qn"], n + 1)
                for c in range(IK):
                    ins = pe.transpose(back[:, c * P:(c + 1) * P], qn[:, c * P:(c + 1) * P], ident[:, :])
                ins.then_inc(s["qT"], 1)

            def b_o(i):
                pe.wait_ge(s["qTe"], TPB * i + 2)
                pe.wait_ge(s["Ge"], 2 * i + 2)
                after(pe, s["ye"], i)
                for tt in range(TPB):
                    for c in range(IK):
                        ins = pe.matmul(o_ps[:, tt, :], qT[:, tt, c, :], gm[:, c, :], start=(c == 0), stop=(c == IK - 1))
                ins.then_inc(s["o"], 1)

            def b_x(i):
                pe.wait_ge(s["x2"], i + 1)
                transposes(x2T_ps, xh2).then_inc(s["x2T"], 1)

            def b_h(i):
                pe.wait_ge(s["x2Te"], i + 1)
                for n in range(4):
                    if n >= 2:
                        pe.wait_ge(s["he"], 4 * i + n - 1)
                    for c in (2 * n, 2 * n + 1):
                        for kd in range(KD):
                            ins = pe.matmul(back[:, (c % 4) * S:(c % 4 + 1) * S], w1[:, kd, c * P:(c + 1) * P],
                                            xT2[:, kd, :], start=(kd == 0), stop=(kd == KD - 1))
                    ins.then_inc(s["h"], 1)

            def b_y(i):
                pe.wait_ge(s["he"], 4 * i + 4)
                for tt in range(TPB):
                    for c in range(FK):
                        ins = pe.matmul(o_ps[:, tt, :], hT[:, c, tt * P:(tt + 1) * P], w2[:, c, :],
                                        start=(c == 0), stop=(c == FK - 1))
                ins.then_inc(s["y"], 1)

            def t_h(n):
                pe.wait_ge(s["ti"], n + 1)
                after(pe, s["fin"], n)
                for kd in range(KD):
                    ins = pe.transpose(tT_ps[:, kd, :], ti[:, kd * P:(kd + 1) * P], ident16[:, :])
                ins.then_inc(s["tT"], 1)
                pe.wait_ge(s["tTe"], n + 1)
                after(pe, s["ge"], n)
                for hf in range(FF // 512):
                    for kd in range(KD):
                        ins = pe.matmul(g_ps[:, hf * 512:(hf + 1) * 512], tT[:, kd, :],
                                        wb[0][:, kd, hf * 512:(hf + 1) * 512], start=(kd == 0), stop=(kd == KD - 1))
                ins.then_inc(s["g"], 1)

            def t_y(n):
                pe.wait_ge(s["gi"], n + 1)
                for c in range(FK):
                    ins = pe.transpose(gT_ps[:, c, :], gi[:, c * P:(c + 1) * P], ident16[:, :])
                ins.then_inc(s["gT"], 1)
                pe.wait_ge(s["gTe"], n + 1)
                for c in range(FK):
                    ins = pe.matmul(ty_ps, gT[:, c, :], wb[1][:, c, :], start=(c == 0), stop=(c == FK - 1))
                ins.then_inc(s["ty"], 1)

            def weight_sums():
                pe.wait_ge(s["part"], 1)
                pe.matmul(sum_ps, ones[:, :], part[:, :], start=True, stop=True).then_inc(s["sum"], 1)

            parts = {
                "g_cT": f_cT, "f_v": f_v, "f_k": f_k, "f_m": f_m, "f_g0": lambda f: f_g(f, 0),
                "f_g1": lambda f: f_g(f, 1), "f_x": f_x,
                "b_q0": lambda i: b_q(i, 0), "b_q1": lambda i: b_q(i, 1),
                "b_n0": lambda i: b_n(TPB * i), "b_n1": lambda i: b_n(TPB * i + 1),
                "b_o": b_o, "b_x": b_x, "b_h": b_h, "b_y": b_y,
                "t0_h": t_h, "t1_h": t_h, "t0_y": t_y, "t1_y": t_y,
            }
            pe.wait_ge(s["w"], 160)
            pipeline(pe, parts, weight_sums)

        @block.sync
        def _(sp):
            with sp.Fori(0, NT) as i:
                sp.wait_ge(s["fin"], i + 1)
                sp.dma_start(ov[bass.ds(i, 1)].rearrange("a p d -> (a p) d"),
                             x[:, bass.ds(i, 1), :].rearrange("p a d -> p (a d)")).then_inc(s["store"], 16)
            sp.wait_ge(s["store"], 16 * NT)


def _spread(w, src, width, band, copies=3):
    import numpy as np
    w = np.asarray(w)
    o = np.zeros(w.shape[:-1] + (H * band,), w.dtype)
    for h in range(H):
        for c in range(copies):
            o[..., band * h + c * width:band * h + (c + 1) * width] = w[..., h * src:h * src + width]
    return o


def kernel(**inputs):
    import numpy as np
    import concourse.bacc as bacc
    from concourse.bass_utils import run_bass_kernel_spmd

    i = {n: np.ascontiguousarray(a) for n, a in inputs.items()}

    def columns(v):
        return np.ascontiguousarray(v.reshape(-1, P).T)

    def key_bias(v, src, width, band):
        o = _spread(v, src, width, band)
        for h in range(H):
            o[band * h + 3 * width] = 1.0
        return columns(o)

    def low_rows(width, band):
        o = np.zeros((P, 2), np.float32)
        for b in range(0, P, band):
            o[b + 2 * width:b + 3 * width, 0] = 1.0
            o[b + width:b + 2 * width, 1] = 1.0
        return o

    lat = D // 2
    ha, hb = D // H, lat // H
    arrays = {
        "x": i["x"], "ctx": i["ctx_1024"], "g_xattn": i["g_xattn"], "g_ffn": i["g_ffn"],
        "a_wq": _spread(i["L0_xattn_Wq"], ha, ha, 64), "a_bq": columns(_spread(i["L0_xattn_bq"], ha, ha, 64)),
        "a_wk": _spread(i["L0_xattn_Wk"], ha, ha, 64), "a_bk": key_bias(i["L0_xattn_bk"], ha, ha, 64),
        "a_wv": i["L0_xattn_Wv"], "a_bv": i["L0_xattn_bv"], "a_wo": i["L0_xattn_Wo"], "a_bo": i["L0_xattn_bo"],
        "a_low": low_rows(ha, 64), "b_low": low_rows(hb, 32),
        "b_wq": _spread(i["L0_ffn_q_w"], ha, hb, 32), "b_bq": columns(_spread(i["L0_ffn_q_b"], ha, hb, 32)),
        "b_wk": _spread(i["L0_ffn_k_w"], hb, hb, 32), "b_bk": key_bias(i["L0_ffn_k_b"], hb, hb, 32),
        "b_wv": _spread(i["L0_ffn_v_w"], hb, hb, 2 * hb, 2), "b_bv": _spread(i["L0_ffn_v_b"], hb, hb, 2 * hb, 2),
        "b_wo": np.ascontiguousarray(i["L0_ffn_o_w"][:lat]),
        "b_bo": i["L0_ffn_o_b"], "router_w": i["L0_ffn_router_w"], "router_b": i["L0_ffn_router_b"][:, None],
        "moe_w1": i["L0_ffn_w1"], "moe_b1": i["L0_ffn_b1"], "moe_w2": i["L0_ffn_w2"], "moe_b2": i["L0_ffn_b2"],
        "l1_wq": i["L1_xattn_wq"], "l1_wk": i["L1_xattn_wk"], "l1_wv": i["L1_xattn_wv"], "l1_wo": i["L1_xattn_wo"],
        "l1_bo": i["L1_xattn_bo"], "l1_w1": i["L1_xattn_w1"], "l1_b1": columns(i["L1_xattn_b1"]),
        "l1_w2": i["L1_xattn_w2"], "l1_b2": i["L1_xattn_b2"],
        "l1_ln": np.ascontiguousarray(np.stack([i["L1_xattn_" + n].reshape(KD, P).T for n in
                                                ("ln1_g", "ln1_b", "ln2_g", "ln2_b")], axis=1)),
        "ff_w1t": np.ascontiguousarray(i["L1_ffn_w1"].T), "ff_w2t": np.ascontiguousarray(i["L1_ffn_w2"].T),
    }
    nc = bacc.Bacc("TRN2", target_bir_lowering=False, num_devices=1)
    t = {n: nc.dram_tensor(f"in_{n}", a.shape, mybir.dt.from_np(a.dtype), kind="ExternalInput").ap()
         for n, a in arrays.items()}
    out = nc.dram_tensor("out", (B, S, D), F32, kind="ExternalOutput").ap()
    program(nc, t, out)
    r = run_bass_kernel_spmd(nc, [{f"in_{n}": a for n, a in arrays.items()}], core_ids=[0])
    return r.results[0]["out"]
```

```python
import concourse.bass as bass
from concourse import mybir
from contextlib import ExitStack

F32 = mybir.dt.float32
BF16 = mybir.dt.bfloat16
F32R = mybir.dt.float32r
I32 = mybir.dt.int32
U32 = mybir.dt.uint32
ALU = mybir.AluOpType
ACT = mybir.ActivationFunctionType
X = mybir.AxisListType.X

P = 128
B, S, D = 8, 256, 256
SC = 77
H = 16
TPB = S // P
NT = B * TPB
KD = D // P
E, F0 = 8, 512
TOPK = 2
INNER = 1024
HD1 = INNER // H
FF = 1024
SLOT_TILES = NT * TOPK + E
EPS = 1e-5
ROUND = 1.5 * 2.0 ** 23


def program(nc, t, out):
    ctx = ExitStack()
    with ctx:
        def sb(name, shape, dt=F32):
            return ctx.enter_context(nc.sbuf_tensor(name, shape, dt))

        stage_sems = []

        def sem(name):
            stage_sems.append(nc.alloc_semaphore(name))
            return stage_sems[-1]

        def stage_done():
            nc.clear_and_free_semaphores(list(stage_sems))
            stage_sems.clear()
            nc.all_engine_barrier()

        x_slots = nc.dram_tensor("x_slots", [SLOT_TILES * P, D], F32, kind="Internal").ap()
        y_slots = nc.dram_tensor("y_slots", [SLOT_TILES * P, D], F32, kind="Internal").ap()

        ps = ctx.enter_context(nc.psum_tensor("ps", [P, 8, 512], F32))

        x = sb("x", [P, NT, D])
        ident = sb("ident", [P, P])
        ident16 = sb("ident16", [P, P], BF16)
        ones = sb("ones", [P, P])
        before = sb("before", [P, P])
        gates = sb("gates", [P, 4])
        minus_half = sb("minus_half", [P, H])
        stats = sb("stats", [P, 3, 6])
        mv = sb("mv", [P, 3, 2])
        var = sb("var", [P, 3])
        rstd = sb("rstd", [P, 3])
        route_i = sb("route_i", [P, NT, TOPK], U32)
        route_w = sb("route_w", [P, NT, TOPK])

        s_x = sem("s_x")
        s_gate = sem("s_gate")
        s_tanh = sem("s_tanh")
        s_const = sem("s_const")
        s_ones = sem("s_ones")
        with nc.Block() as block:
            @block.sync
            def _(sp):
                sp.dma_start(x[:, :, :], t["x"].rearrange("b (t p) d -> p (b t) d", p=P)).then_inc(s_x, 16)
                for i, g in enumerate(("g_xattn", "g_ffn")):
                    for j in range(2):
                        sp.dma_start(gates[:, 2 * j + i:2 * j + i + 1],
                                     t[g][j:j + 1].partition_broadcast(P)).then_inc(s_gate, 16)

            @block.gpsimd
            def _(pool):
                pool.memset(ident[:, :], 0.0)
                pool.memset(ident16[:, :], 0.0)
                pool.memset(ones[:, :], 1.0)
                pool.memset(before[:, :], 1.0)
                pool.memset(minus_half[:, :], -0.5)
                pool.drain()
                pool.affine_select(out=ident[:, :], in_=ident[:, :], compare_op=ALU.not_equal, fill=1.0,
                                   base=0, pattern=[[-1, P]], channel_multiplier=1)
                pool.affine_select(out=ident16[:, :], in_=ident16[:, :], compare_op=ALU.not_equal, fill=1.0,
                                   base=0, pattern=[[-1, P]], channel_multiplier=1)
                pool.affine_select(out=before[:, :], in_=before[:, :], compare_op=ALU.is_gt, fill=0.0,
                                   base=0, pattern=[[1, P]], channel_multiplier=-1)

        def softmax_attention(tag, hd, band, NK, KC, cross, rest):
            HC = P // band
            NC = H // HC
            VD = H * hd
            OK = VD // P
            W = NC * P
            scale = float(hd) ** -0.5
            KW = P if cross else P * KC
            R = H * KC // 2
            st = ExitStack()

            def tb(name, shape, dt=F32):
                return st.enter_context(nc.sbuf_tensor(tag + name, shape, dt))

            def ts(name):
                return sem(tag + name)

            wq = [tb("wqh", [P, KD, W], F32R), tb("wql", [P, KD, W], F32R)]
            wk = [tb("wkh", [P, KD, W], F32R), tb("wkl", [P, KD, W], F32R)]
            wv = [tb("wvh", [P, KD, 256], F32R), tb("wvl", [P, KD, 256], F32R)]
            wo = [tb("woh", [P, OK, D], F32R), tb("wol", [P, OK, D], F32R)]
            bq = tb("bq", [P, NC])
            bk = tb("bk", [P, NC])
            sbq = tb("sbq", [P, NC])
            sbk = tb("sbk", [P, NC])
            low = tb("low", [P, 2])
            bv = tb("bv", [P, 256])
            bo = tb("bo", [P, D])
            xn = tb("xn", [P, TPB, D])
            xT = [tb("xTh", [P, KD, S], F32R), tb("xTl", [P, KD, S], F32R)]
            q = [tb("q0", [P, NC, S], F32R), tb("q1", [P, NC, S], F32R)]
            hm = tb("hm", [P, 4, S], F32R)
            k = [tb("k0", [P, NC, HC, KW], F32R), tb("k1", [P, NC, HC, KW], F32R)]
            kk = tb("kk", [P, NC, B * SC if cross else KW], F32R)
            v = [tb("v0", [P, KC, H, P], F32R), tb("v1", [P, KC, H, P], F32R)]
            negmax = tb("negmax", [P, TPB, NC, P], BF16)
            pt = tb("pt", [P, 3, 2, S])
            pth = tb("pth", [P, 3, 2, S], F32R)
            ptl = tb("ptl", [P, 3, 2, S], F32R)
            av = tb("av", [P, NC, S])
            rsum = tb("rsum", [P, H])
            parts = tb("parts", [P, 2, H, hd])
            ao = tb("ao", [P, TPB, H, hd])
            aoT = [tb("aoTh", [P, OK, S], F32R), tb("aoTl", [P, OK, S], F32R)]
            tmp = tb("tmp", [P, TPB, D])
            if cross:
                cx = av[:, 0:5, :]
                cT = [tb("cTh", [P, KD, B * SC], F32R), tb("cTl", [P, KD, B * SC], F32R)]
                vall = [tb("vallh", [P, B, 256], F32R), tb("valll", [P, B, 256], F32R)]
            else:
                mo, hln, rw, rb, moT, lgT, zeros = rest
                rwf = tb("rwf", [P, KD, E])
                vf = tb("vf", [P, KC, 256])
            names = "w0 w1 w2 wh wl cx var rstd xn xT xTh xTl pp phm pe kp khm kst vp vf vh vl kx kd " \
                "max maxe mT q2 sc exp ph pl free ave at pa ao aoT aoTh aoTl o oe".split()
            names += ("cT cTh cTl vx" if cross else "z zero moT moTh moTl lg lge hc mc").split()
            s = {n: ts("s_" + n) for n in names}

            def bank(b, w=512, parts=P):
                return ps[0:parts, b, 0:w]

            SR, PVB = [0, 1], [2, 3]
            XB, PB, VB = 4, [5, 6], 7
            KB = [0, 1, 4, 5]
            xT_ps = bank(XB).rearrange("p (k s) -> p k s", k=KD)
            v_ps = bank(VB).rearrange("p (k n) -> p k n", n=256)
            mT_ps = ps[:, 4:6, :].rearrange("p b n -> p (b n)").bitcast(BF16)[:, 0:NC * S] \
                .rearrange("p (c s) -> p c s", c=NC)
            aoT_ps = bank(3, OK * S).rearrange("p (k s) -> p k s", k=OK)
            moT_ps = bank(3).rearrange("p (k s) -> p k s", k=KD)
            o_ps = bank(2).rearrange("p (t d) -> p t d", t=TPB)
            MR = NC // 4
            MROUNDS = TPB * (4 if MR == 1 else 2)
            AT = TPB * MR
            per = R // (NC // 2)

            def max_ps(m):
                return ps[:, 4 + 2 * (m % 2):6 + 2 * (m % 2), :].rearrange("p b n -> p (b n)")

            def head(r, j):
                return (r // HC, r % HC, j) if KC == 2 else (r, j, 0)

            def pair(n):
                return (False, 2 * n) if cross else (n >= 2, 2 * (n % 2))

            if cross:
                F = "stats xn xT xTl p0 p1 e0 p2 e1 p3 e2 e3 kx0 kx1 vx0 vx1 vx2 vx3".split()
            else:
                F = "stats xn xT xTl p0 p1 e0 p2 e1 p3 e2 v e3 kx0 ve kx1 vs kx2 kx3".split()
            F += [word for m in range(MROUNDS + 1) for word in ([f"m{m}"] if m < MROUNDS else []) + ([f"me{m - 1}"] if m else [])]
            F += ["mT", "q2"]
            K = [f"r{r}" for r in range(R + 3)]
            K += [word for n in range(AT + 1) for word in ([f"t{n}"] if n < AT else []) + ([f"te{n - 1}"] if n else [])]
            K += "aoT aoTl o oe moT moTl lg".split()
            STEPS = sorted([((n + 0.5) / len(F), "f", word) for n, word in enumerate(F)]
                           + [((n + 0.5) / len(K), "b", word) for n, word in enumerate(K)])

            def run(steps, i, p, streams):
                for _, kind, name in STEPS:
                    word = name.rstrip("0123456789")
                    if kind in streams and (kind, word) in steps:
                        n = [int(name[len(word):])] if name != word else []
                        if kind == "f":
                            steps[kind, word](i + 1, 1 - p, *n)
                        else:
                            steps[kind, word](i, p, *n)

            def pipeline(eng, steps):
                run(steps, -1, 1, "f")
                run(steps, 0, 0, "fb")
                with eng.Fori(0, B // 2 - 1) as j:
                    run(steps, 2 * j + 1, 1, "fb")
                    run(steps, 2 * j + 2, 0, "fb")
                run(steps, B - 1, 1, "b")

            def after(eng, semaphore, n):
                if not (isinstance(n, int) and n <= 0):
                    eng.wait_ge(semaphore, n)

            passes = [(0, 0), (0, 1), (1, 0)]

            def product(eng, dst, lhsT, rhs, n):
                for kd in range(n):
                    for m, (a, b) in enumerate(passes):
                        ins = eng.matmul(dst, lhsT[a](kd), rhs[b](kd), start=(kd == 0 and m == 0),
                                         stop=(kd == n - 1 and m == 2))
                return ins

            pieces, whole = [], {}
            for dst, name, w, chunks in ((wk, "wk", W, KD), (wv, "wv", 256, KD), (wq, "wq", W, KD), (wo, "wo", D, OK)):
                src = t[tag + name].rearrange("(k p) n -> p k n", p=P)
                kn = max(1, min(chunks, 512 // w))
                for kd in range(0, chunks, kn):
                    for c in range(0, w, 512):
                        cut = (slice(None), slice(kd, kd + kn), slice(c, min(w, c + 512)))
                        pieces.append((dst[0][cut], dst[1][cut], src[cut], kn, min(w, 512)))
                whole[name] = len(pieces)

            def staged(n):
                kn, w = pieces[n][3:]
                return pt[:, n % 3, :, :].rearrange("p a s -> p (a s)")[:, 0:kn * w].rearrange("p (k n) -> p k n", k=kn)

            def hm_of(n):
                return hm[:, 2 * (n % 2):2 * (n % 2) + 2, :].rearrange("p a s -> p (a s)")[:, 0:4 * SC]

            def lo_of(eng, dst, src, hi):
                return eng.tensor_tensor(dst, src, hi.bitcast(F32), ALU.subtract)

            def dve_steps(dve):
                def stats_(f, p):
                    for tt in range(TPB):
                        dve.bn_stats(stats[:, tt, :], x[:, bass.ds(TPB * f + tt, 1), :])
                    dve.drain()
                    for tt in range(TPB):
                        dve.bn_aggr(mv[:, tt, :], stats[:, tt, :])
                    dve.drain()
                    dve.tensor_scalar(var[:, 0:TPB], mv[:, 0:TPB, 1], EPS, None, ALU.add).then_inc(s["var"], 1)

                def xn_(f, p):
                    dve.wait_ge(s["rstd"], f + 1)
                    after(dve, s["xT"], f)
                    if not cross:
                        after(dve, s["hc"], f)
                    for tt in range(TPB):
                        ins = dve.tensor_scalar(xn[:, tt, :],
                                                x[:, bass.ds(TPB * f + tt, 1), :].rearrange("p a d -> p (a d)"),
                                                mv[:, tt, 0:1], rstd[:, tt:tt + 1], ALU.subtract, ALU.mult)
                    ins.then_inc(s["xn"], 1)

                def xTl(f, p):
                    dve.wait_ge(s["xTh"], f + 1)
                    lo_of(dve, xT[1][:, :, :], xT_ps, xT[0][:, :, :]).then_inc(s["xTl"], 1)

                def e(f, p, n):
                    dve.wait_ge(s["phm"], 4 * f + n + 1)
                    keys, c = pair(n)
                    if keys:
                        after(dve, s["kx"], HC * f)
                    elif n == 0:
                        after(dve, s["free"], R * (f - 1))
                    for u in range(2):
                        ins = dve.scalar_tensor_tensor((kk if keys else q[p])[:, c + u, :],
                                                       bank(PB[n % 2])[:, u * S:(u + 1) * S],
                                                       (bk if keys else bq)[:, c + u:c + u + 1],
                                                       hm[:, 2 * (n % 2) + u, :].bitcast(F32), ALU.add, ALU.subtract)
                    ins.then_inc(s["pe"], 1)

                def ve(f, p):
                    dve.drain()
                    dve.wait_ge(s["vp"], f + 1)
                    dve.tensor_tensor(vf[:, :, :], v_ps, bv[:, :].unsqueeze(1).to_broadcast([P, KC, 256]), ALU.add)\
                        .then_inc(s["vf"], 1)

                def vs(f, p):
                    dve.drain()
                    after(dve, s["free"], R * (f - 1))
                    views = []
                    for kc in range(KC):
                        for g in range(HC):
                            src = vf[:, kc, :].rearrange("p (c g n) -> p c g n", g=HC, n=2 * hd)[:, :, g, :]
                            dst = v[p][:, kc, :, g * band:g * band + 2 * hd]\
                                .rearrange("p (c g) n -> p c g n", g=HC)[:, :, g, :]
                            views.append((dst, src))
                    for dst, src in views:
                        dve.tensor_copy(dst[:, :, 0:hd], src[:, :, 0:hd])
                    dve.drain()
                    for dst, src in views:
                        ins = lo_of(dve, dst[:, :, hd:2 * hd], src[:, :, hd:2 * hd], dst[:, :, 0:hd])
                    ins.then_inc(s["vl"], 1)

                def me(f, p, m):
                    dve.wait_ge(s["max"], MROUNDS * f + m + 1)
                    if m == 0:
                        after(dve, s["mT"], f)
                    if MR == 1:
                        tt, c0, n = m // 4, m % 4, 1
                    else:
                        tt, c0, n = m // 2, 4 * (m % 2), 4
                    src = max_ps(m).rearrange("p (c g n) -> p c g n", c=n, g=HC)[:, :, :, 0:NK * KC]
                    dst = negmax[:, tt, c0:c0 + n, :].rearrange("p c (g r) -> p c g r", g=HC)[:, :, :, 3 * hd]
                    dve.tensor_reduce(dst, src, X, ALU.max, negate=True).then_inc(s["maxe"], 1)

                def q2(f, p):
                    dve.drain()
                    dve.wait_ge(s["mT"], f + 1)
                    dve.tensor_tensor(q[p][:, :, :], q[p][:, :, :].bitcast(F32), mT_ps, ALU.add).then_inc(s["q2"], 1)

                def r_(i, p, r):
                    if 1 <= r <= R:
                        r -= 1
                        if r % 2:
                            dve.wait_ge(s["exp"], R * i + r + 1)
                        else:
                            dve.wait_ge(s["ph"], R // 2 * i + r // 2 + 1)
                        lo_of(dve, ptl[0:NK, r % 3, :, :], pt[0:NK, r % 3, :, :], pth[0:NK, r % 3, :, :])\
                            .then_inc(s["pl"], 1)

                def te(i, p, m):
                    dve.wait_ge(s["at"], AT * i + m + 1)
                    tt, u = m // MR, m % MR
                    n = H // MR
                    at = bank(SR[m % 2]).rearrange("p (h r) -> p h r", r=band)
                    hs = slice(u * n, u * n + n)
                    dve.reciprocal(rsum[:, hs], at[:, :, 2 * hd])
                    dve.drain()
                    for part in range(2):
                        ins = dve.tensor_tensor(parts[:, part, hs, :], at[:, :, part * hd:(part + 1) * hd],
                                                rsum[:, hs].unsqueeze(2).to_broadcast([P, n, hd]), ALU.mult)
                    ins.then_inc(s["pa"], 1)
                    dve.drain()
                    if u == MR - 1:
                        if m < AT - 1:
                            after(dve, s["aoT"], i)
                        dve.tensor_tensor(ao[:, tt, :, :], parts[:, 0, :, :], parts[:, 1, :, :], ALU.add)\
                            .then_inc(s["ao"], 1)
                        dve.drain()

                def aoTl(i, p):
                    dve.wait_ge(s["aoTh"], i + 1)
                    lo_of(dve, aoT[1][:, :, :], aoT_ps, aoT[0][:, :, :]).then_inc(s["aoTl"], 1)

                def oe(i, p):
                    dve.wait_ge(s["o"], i + 1)
                    bob = bo[:, :].unsqueeze(1).to_broadcast([P, TPB, D])
                    if cross:
                        xb = x[:, bass.ds(TPB * i, TPB), :]
                        dve.tensor_tensor(tmp[:, :, :], o_ps, bob, ALU.add).then_inc(s["oe"], 1)
                        dve.drain()
                        dve.scalar_tensor_tensor(xb, tmp[:, :, :], gates[:, 0:1], xb, ALU.mult, ALU.add)
                        dve.drain()
                    else:
                        after(dve, s["mc"], i)
                        after(dve, s["moT"], i)
                        dve.tensor_tensor(tmp[:, :, :], o_ps, bob, ALU.add).then_inc(s["oe"], 1)

                def moTl(i, p):
                    dve.wait_ge(s["moTh"], i + 1)
                    lo_of(dve, moT[1][:, :, :], moT_ps, moT[0][:, :, :]).then_inc(s["moTl"], 1)

                steps = {("f", "stats"): stats_, ("f", "xn"): xn_, ("f", "xTl"): xTl, ("f", "e"): e, ("f", "me"): me,
                         ("f", "q"): lambda f, p, _: q2(f, p),
                         ("b", "r"): r_, ("b", "te"): te, ("b", "aoTl"): aoTl, ("b", "oe"): oe}
                if not cross:
                    steps.update({("f", "ve"): ve, ("f", "vs"): vs, ("b", "moTl"): moTl})
                return steps

            def act_steps(act):
                def xT_(f, p):
                    act.wait_ge(s["xT"], f + 1)
                    after(act, s["pp"], 4 * f)
                    if not cross:
                        after(act, s["vp"], f)
                    act.activation(xT[0][:, :, :], xT_ps, ACT.Copy).then_inc(s["xTh"], 1)

                def p_(f, p, n):
                    act.wait_ge(s["pp"], 4 * f + n + 1)
                    after(act, s["pe"], 4 * f + n - 1)
                    keys, c = pair(n)
                    for u in range(2):
                        ins = act.activation(hm[:, 2 * (n % 2) + u, :], bank(PB[n % 2])[:, u * S:(u + 1) * S],
                                             ACT.Identity, bias=(sbk if keys else sbq)[:, c + u:c + u + 1],
                                             scale=low[:, int(keys):int(keys) + 1])
                    ins.then_inc(s["phm"], 1)

                def r_(i, p, r):
                    if r < R:
                        act.wait_ge(s["sc"], R * i + r + 1)
                        after(act, s["pl"], R * i + r - 2)
                        if r % 2:
                            after(act, s["free"], R * i + r - 2)
                        for dst in (pt, pth)[0:1 + r % 2]:
                            ins = act.activation(dst[0:NK, r % 3, :, :].rearrange("p j s -> p (j s)"),
                                                 bank(SR[r % 2], 512, NK), ACT.Exp, scale=scale)
                        ins.then_inc(s["exp"], 1)
                    if r >= per + 2 and (r - 2) % per == 0:
                        n = (r - 2) // per - 1
                        act.wait_ge(s["free"], R * i + per * (n + 1))
                        if n == 0:
                            after(act, s["at"], AT * i)
                        act.activation(av[:, 2 * n:2 * n + 2, :], bank(PVB[n % 2]).rearrange("p (c s) -> p c s", c=2),
                                       ACT.Copy).then_inc(s["ave"], 1)

                def aoT_(i, p):
                    act.wait_ge(s["aoT"], i + 1)
                    after(act, s["o"], i)
                    act.activation(aoT[0][:, :, :], aoT_ps, ACT.Copy).then_inc(s["aoTh"], 1)

                def moT_(i, p):
                    act.wait_ge(s["moT"], i + 1)
                    after(act, s["lg"], i)
                    act.activation(moT[0][:, :, :], moT_ps, ACT.Copy).then_inc(s["moTh"], 1)

                def lg(i, p):
                    act.wait_ge(s["lg"], i + 1)
                    act.activation(lgT[:, bass.ds(S * i, S)], bank(2, S, E), ACT.Identity, bias=rb[:, 0:1])\
                        .then_inc(s["lge"], 1)

                steps = {("f", "xT"): xT_, ("f", "p"): p_, ("b", "r"): r_, ("b", "aoT"): aoT_}
                if not cross:
                    steps.update({("b", "moT"): moT_, ("b", "lg"): lg})
                return steps

            def pool_steps(pool):
                def copy(dst, src):
                    return pool.tensor_scalar(dst, src, 1.0, 0.0, ALU.mult, ALU.add)

                def stats_(f, p):
                    pool.wait_ge(s["var"], f + 1)
                    pool.tensor_tensor(rstd[:, 0:TPB], var[:, 0:TPB], minus_half[:, 0:TPB], ALU.pow)\
                        .then_inc(s["rstd"], 1)

                def kx(f, p, g):
                    rows = slice(g * band, (g + 1) * band)
                    pool.drain()
                    if cross:
                        after(pool, s["free"], R * (f - 1))
                        ins = pool.tensor_copy(k[p][rows, :, g, 0:SC], kk[rows, :, bass.ds(SC * f, SC)].bitcast(F32))
                    else:
                        pool.wait_ge(s["pe"], 4 * f + 4)
                        after(pool, s["free"], R * (f - 1))
                        pool.tensor_tensor(k[p][rows, 0, g, 0:4], kk[rows, 0, 0:4].bitcast(F32), ones[rows, 0:4],
                                           ALU.mult)
                        copy(k[p][rows, 0, g, 4:], kk[rows, 0, 4:].bitcast(F32))
                        ins = copy(k[p][rows, 1:, g, :], kk[rows, 1:, :].bitcast(F32))
                    ins.then_inc(s["kx"], 1)
                    pool.drain()

                def vx(f, p, n):
                    part, g = n // HC, n % HC
                    after(pool, s["free"], R * (f - 1))
                    src = vall[part][0:SC, bass.ds(f, 1), :].rearrange("p a (c g n) -> p (a c) g n", g=HC, n=hd)
                    dst = v[p][0:SC, 0, :, g * band + part * hd:g * band + (part + 1) * hd]\
                        .rearrange("p (c g) n -> p c g n", g=HC)
                    pool.tensor_copy(dst[:, :, g, :], src[:, :, g, :].bitcast(F32)).then_inc(s["vx"], 1)

                def r_(i, p, r):
                    if r < R and r % 2 == 0:
                        pool.wait_ge(s["exp"], R * i + r + 1)
                        after(pool, s["free"], R * i + r - 2)
                        pool.tensor_tensor(pth[0:NK, r % 3, 0, 0:4], pt[0:NK, r % 3, 0, 0:4], ones[0:NK, 0:4], ALU.mult)
                        copy(pth[0:NK, r % 3, 0, 4:S], pt[0:NK, r % 3, 0, 4:S])
                        copy(pth[0:NK, r % 3, 1, :], pt[0:NK, r % 3, 1, :]).then_inc(s["ph"], 1)

                def hln_(f, p):
                    pool.wait_ge(s["xn"], f + 1)
                    pool.tensor_copy(hln[:, bass.ds(TPB * f, TPB), :], xn[:, :, :]).then_inc(s["hc"], 1)

                def mo_(i, p):
                    pool.wait_ge(s["oe"], i + 1)
                    pool.tensor_copy(mo[:, bass.ds(TPB * i, TPB), :], tmp[:, :, :]).then_inc(s["mc"], 1)

                steps = {("f", "stats"): stats_, ("f", "kx"): kx, ("b", "r"): r_}
                if cross:
                    steps["f", "vx"] = vx
                else:
                    steps.update({("f", "xT"): hln_, ("b", "moT"): mo_})
                return steps

            def pe_steps(pe):
                def xT_(f, p):
                    pe.wait_ge(s["xn"], f + 1)
                    after(pe, s["q2"], f)
                    for tt in range(TPB):
                        for kd in range(KD):
                            ins = pe.transpose(xT_ps[:, kd, tt * P:(tt + 1) * P], xn[:, tt, kd * P:(kd + 1) * P],
                                               ident[:, :])
                    ins.then_inc(s["xT"], 1)

                xs = [lambda kd, a=a: xT[a][:, kd, :] for a in range(2)]

                def p_(f, p, n):
                    if n == 0:
                        pe.wait_ge(s["xTl"], f + 1)
                    if n >= 2:
                        pe.wait_ge(s["pe"], 4 * f + n - 1)
                    keys, c = pair(n)
                    w = wk if keys else wq
                    for u in range(2):
                        ins = product(pe, bank(PB[n % 2])[:, u * S:(u + 1) * S],
                                      [lambda kd, a=a: w[a][:, kd, (c + u) * P:(c + u + 1) * P] for a in range(2)], xs, KD)
                    ins.then_inc(s["pp"], 1)

                def v_(f, p):
                    for kc in range(KC):
                        ins = product(pe, v_ps[:, kc, :],
                                      [lambda kd, a=a: xT[a][:, kd, kc * P:(kc + 1) * P] for a in range(2)],
                                      [lambda kd, a=a: wv[a][:, kd, :] for a in range(2)], KD)
                    ins.then_inc(s["vp"], 1)

                def m_(f, p, m):
                    if m == 0:
                        pe.wait_ge(s["pe"], 4 * f + 4)
                        pe.wait_ge(s["kx"], HC * (f + 1))
                        if not cross:
                            pe.wait_ge(s["vf"], f + 1)
                    if m >= 2:
                        pe.wait_ge(s["maxe"], MROUNDS * f + m - 1)
                    for half in range(2):
                        if MR == 1:
                            tt, c = m // 4, m % 4
                            ins = pe.matmul(max_ps(m)[:, half * 512:(half + 1) * 512], q[p][:, c, tt * P:(tt + 1) * P],
                                            k[p][:, c, 2 * half:2 * half + 2, :], start=True, stop=True)
                        else:
                            for u in range(2):
                                tt, c = m // 2, 4 * (m % 2) + 2 * half + u
                                o = half * 512 + u * 256
                                ins = pe.matmul(max_ps(m)[:, o:o + 256], q[p][:, c, tt * P:(tt + 1) * P],
                                                k[p][:, c, :, :], start=True, stop=True)
                    ins.then_inc(s["max"], 1)

                def mT_(f, p):
                    pe.wait_ge(s["maxe"], MROUNDS * f + MROUNDS)
                    for tt in range(TPB):
                        for c in range(NC):
                            ins = pe.transpose(mT_ps[:, c, tt * P:(tt + 1) * P], negmax[:, tt, c, :], ident16[:, :])
                    ins.then_inc(s["mT"], 1)

                def r_(i, p, r):
                    if r == 0:
                        pe.wait_ge(s["q2"], i + 1)
                        pe.wait_ge(s["vx" if cross else "vl"], (4 if cross else 1) * (i + 1))
                        after(pe, s["pa"], AT * i)
                    if r < R:
                        if r >= 2:
                            pe.wait_ge(s["exp"], R * i + r - 1)
                        for j in range(2):
                            c, g, kc = head(r, j)
                            ins = pe.matmul(bank(SR[r % 2], 512, NK)[:, j * S:(j + 1) * S],
                                            k[p][:, c, g, kc * P:kc * P + NK], q[p][:, c, :], start=True, stop=True)
                        ins.then_inc(s["sc"], 1)
                    r -= 2
                    if r == 0:
                        after(pe, s["oe" if cross else "lge"], i)
                    if 0 <= r < R:
                        pe.wait_ge(s["pl"], R * i + r + 1)
                        for j in range(2):
                            c, g, kc = head(r, j)
                            first = g == 0 and kc == 0
                            last = g == HC - 1 and kc == KC - 1
                            if first and c % 2 == 0 and c >= 4:
                                pe.wait_ge(s["ave"], NC // 2 * i + c // 2 - 1)
                            for n, w in enumerate((pth, ptl)):
                                ins = pe.matmul(bank(PVB[c // 2 % 2])[:, (c % 2) * S:(c % 2 + 1) * S],
                                                v[p][:, kc, c * HC + g, :], w[:, r % 3, j, :],
                                                start=(first and n == 0), stop=(last and n == 1))
                        ins.then_inc(s["free"], 1)

                def t_(i, p, m):
                    tt, u = m // MR, m % MR
                    if m == 0:
                        pe.wait_ge(s["ave"], NC // 2 * i + NC // 2)
                    if m >= 2:
                        pe.wait_ge(s["pa"], AT * i + m - 1)
                    for c in range(4):
                        ins = pe.transpose(bank(SR[m % 2])[:, c * P:(c + 1) * P], av[:, 4 * u + c, tt * P:(tt + 1) * P],
                                           ident[:, :])
                    ins.then_inc(s["at"], 1)

                def aoT_(i, p):
                    pe.wait_ge(s["ao"], TPB * i + TPB)
                    for tt in range(TPB):
                        flat = ao[:, tt, :, :].rearrange("p h e -> p (h e)")
                        for kd in range(OK):
                            ins = pe.transpose(aoT_ps[:, kd, tt * P:(tt + 1) * P], flat[:, kd * P:(kd + 1) * P], ident[:, :])
                    ins.then_inc(s["aoT"], 1)

                def o_(i, p):
                    pe.wait_ge(s["aoTl"], i + 1)
                    for tt in range(TPB):
                        ins = product(pe, o_ps[:, tt, :],
                                      [lambda kd, a=a: aoT[a][:, kd, tt * P:(tt + 1) * P] for a in range(2)],
                                      [lambda kd, a=a: wo[a][:, kd, :] for a in range(2)], OK)
                    ins.then_inc(s["o"], 1)

                def moT_(i, p):
                    pe.wait_ge(s["oe"], i + 1)
                    for tt in range(TPB):
                        for kd in range(KD):
                            ins = pe.transpose(moT_ps[:, kd, tt * P:(tt + 1) * P], tmp[:, tt, kd * P:(kd + 1) * P],
                                               ident[:, :])
                    ins.then_inc(s["moT"], 1)

                def lg(i, p):
                    pe.wait_ge(s["moTl"], i + 1)
                    product(pe, bank(2, S, E), [lambda kd, a=a: rw[a][:, kd, :] for a in range(2)],
                            [lambda kd, a=a: moT[a][:, kd, :] for a in range(2)], KD).then_inc(s["lg"], 1)

                steps = {("f", "xT"): xT_, ("f", "p"): p_, ("f", "m"): m_, ("f", "mT"): mT_,
                         ("b", "r"): r_, ("b", "t"): t_, ("b", "aoT"): aoT_, ("b", "o"): o_}
                if not cross:
                    steps.update({("f", "v"): v_, ("b", "moT"): moT_, ("b", "lg"): lg})
                return steps

            with st, nc.Block() as block:
                @block.sync
                def _(sp):
                    for n in range(len(pieces)):
                        if n >= 3:
                            sp.wait_ge(s["wl"], n - 2)
                        sp.dma_start(staged(n), pieces[n][2]).then_inc(s[f"w{n % 3}"], 16)
                        if n == 0:
                            for dst2, name2 in ((bq, tag + "bq"), (bk, tag + "bk"), (low, tag + "low")):
                                sp.dma_start(dst2[:, :], t[name2]).then_inc(s["cx"], 16)
                            for dst2, name2 in ((bv, tag + "bv"), (bo, tag + "bo")):
                                sp.dma_start(dst2[:, :], t[name2].partition_broadcast(P)).then_inc(s["cx"], 16)
                            if cross:
                                cflat = t["ctx"].rearrange("b s d -> (b s) d")
                                sp.dma_start(cx[:, 0:4, :], cflat[0:512, :].rearrange("(a p) d -> p a d", p=P))\
                                    .then_inc(s["cx"], 16)
                                sp.dma_start(cx[0:B * SC - 512, 4, :], cflat[512:B * SC, :]).then_inc(s["cx"], 16)
                            else:
                                sp.dma_start(rwf[:, :, :], t["router_w"].rearrange("(k p) n -> p k n", p=P))\
                                    .then_inc(s["cx"], 16)
                                sp.dma_start(rb[:, :], t["router_b"]).then_inc(s["cx"], 16)
                    if not cross:
                        sp.wait_ge(s["zero"], 1)
                        with sp.Fori(0, SLOT_TILES // 8) as i:
                            sp.dma_start(x_slots.rearrange("(i a p) d -> i p a d", a=8, p=P)[bass.ds(i, 1)]
                                         .rearrange("i p a d -> (i p) a d"),
                                         zeros[:, :].unsqueeze(1).to_broadcast([P, 8, D])).then_inc(s["z"], 16)
                        sp.wait_ge(s["z"], 16 * (SLOT_TILES // 8))

                @block.gpsimd
                def _(pool):
                    if not cross:
                        pool.memset(zeros[:, :], 0.0).then_inc(s["zero"], 1)
                    pool.memset(k[0][:, :, :, :].bitcast(F32), 0.0)
                    pool.memset(v[0][:, :, :, :].bitcast(F32), 0.0)
                    pool.memset(pth[:, :, :, :].bitcast(F32), 0.0)
                    pool.memset(ptl[:, :, :, :].bitcast(F32), 0.0)
                    pool.memset(k[1][:, :, :, :].bitcast(F32), 0.0)
                    pool.memset(v[1][:, :, :, :].bitcast(F32), 0.0)
                    pool.memset(negmax[:, :, :, :], 0.0)
                    pool.drain()
                    for w in v:
                        for g in range(HC):
                            ones_at = w[:, :, :, g * band + 2 * hd].rearrange("p k (c g) -> p k c g", g=HC)
                            ins = pool.memset(ones_at[:, :, :, g].bitcast(F32), 1.0)
                    ins.then_inc(s["kd"], 1)
                    pool.drain()
                    if cross:
                        pool.wait_ge(s["kst"], 2 * NC)
                        pool.wait_ge(s["vl"], 4)
                    pipeline(pool, pool_steps(pool))

                @block.vector
                def _(dve):
                    dve.wait_ge(s["cx"], 16 * 7)
                    dve.tensor_scalar(sbq[:, :], bq[:, :], low[:, 0:1], None, ALU.mult)
                    dve.tensor_scalar(sbk[:, :], bk[:, :], low[:, 1:2], None, ALU.mult).then_inc(s["vh"], 1)
                    if cross:
                        for n in range(5):
                            dve.wait_ge(s["cTh"], n + 1)
                            w = P if n < 4 else B * SC - 512
                            src = bank(n % 2, KD * P).rearrange("p (k s) -> p k s", k=KD)[:, :, 0:w]
                            lo_of(dve, cT[1][:, :, n * P:n * P + w], src, cT[0][:, :, n * P:n * P + w])\
                                .then_inc(s["cTl"], 1)
                    for n in range(len(pieces)):
                        dve.wait_ge(s["wh"], n + 1)
                        lo_of(dve, pieces[n][1], staged(n), pieces[n][0]).then_inc(s["wl"], 1)
                    if not cross:
                        dve.tensor_copy(rw[0][:, :, :], rwf[:, :, :])
                        dve.drain()
                        lo_of(dve, rw[1][:, :, :], rwf[:, :, :], rw[0][:, :, :]).then_inc(s["wl"], 1)
                    dve.wait_ge(s["kd"], 1)
                    if cross:
                        for n in range(2 * NC):
                            c, half = n // 2, n % 2
                            cols = slice(half * 4 * SC, (half + 1) * 4 * SC)
                            dve.wait_ge(s["khm"], n + 1)
                            dve.scalar_tensor_tensor(kk[:, c, cols], bank(KB[n % 4], 4 * SC), bk[:, c:c + 1],
                                                     hm_of(n).bitcast(F32),
                                                     ALU.add, ALU.subtract).then_inc(s["kst"], 1)
                        for n in range(4):
                            dve.wait_ge(s["vp"], n + 1)
                            src = bank(2 + n % 2, 512, SC).rearrange("p (b n) -> p b n", b=2)
                            bb = bv[0:SC, :].unsqueeze(1).to_broadcast([SC, 2, 256])
                            dve.tensor_tensor(tmp[0:SC, :, :], src, bb, ALU.add)
                            dve.drain()
                            dve.tensor_copy(vall[0][0:SC, 2 * n:2 * n + 2, :], tmp[0:SC, :, :])
                            dve.drain()
                            lo_of(dve, vall[1][0:SC, 2 * n:2 * n + 2, :], tmp[0:SC, :, :],
                                  vall[0][0:SC, 2 * n:2 * n + 2, :]).then_inc(s["vl"], 1)
                            dve.drain()
                    if cross:
                        dve.wait_ge(s_x, 16)
                        dve.wait_ge(s_tanh, 1)
                    pipeline(dve, dve_steps(dve))

                @block.scalar
                def _(act):
                    if cross:
                        act.wait_ge(s_gate, 64)
                        act.activation(gates[:, :], gates[:, :], ACT.Tanh).then_inc(s_tanh, 1)
                        for n in range(5):
                            act.wait_ge(s["cT"], n + 1)
                            w = P if n < 4 else B * SC - 512
                            src = bank(n % 2, KD * P).rearrange("p (k s) -> p k s", k=KD)[:, :, 0:w]
                            act.activation(cT[0][:, :, n * P:n * P + w], src, ACT.Copy).then_inc(s["cTh"], 1)
                    for n in range(len(pieces)):
                        act.wait_ge(s[f"w{n % 3}"], 16 * (n // 3) + 16)
                        act.activation(pieces[n][0], staged(n), ACT.Copy).then_inc(s["wh"], 1)
                    act.wait_ge(s["vh"], 1)
                    if cross:
                        for n in range(2 * NC):
                            c = n // 2
                            act.wait_ge(s["kp"], n + 1)
                            if n >= 2:
                                act.wait_ge(s["kst"], n - 1)
                            act.activation(hm_of(n),
                                           bank(KB[n % 4], 4 * SC), ACT.Identity, bias=sbk[:, c:c + 1],
                                           scale=low[:, 1:2]).then_inc(s["khm"], 1)
                    pipeline(act, act_steps(act))

                @block.tensor
                def _(pe):
                    if cross:
                        pe.wait_ge(s["cx"], 16 * 7)
                        for n in range(5):
                            w = P if n < 4 else B * SC - 512
                            if n >= 2:
                                pe.wait_ge(s["cTl"], n - 1)
                            for kd in range(KD):
                                ins = pe.transpose(bank(n % 2)[:, kd * P:kd * P + w], cx[0:w, n, kd * P:(kd + 1) * P],
                                                   ident[0:w, 0:w])
                            ins.then_inc(s["cT"], 1)
                        pe.wait_ge(s["cTl"], 5)
                        pe.wait_ge(s["wl"], whole["wk"])
                        for n in range(2 * NC):
                            c, half = n // 2, n % 2
                            cols = slice(half * 4 * SC, (half + 1) * 4 * SC)
                            if n >= 4:
                                pe.wait_ge(s["kst"], n - 3)
                            product(pe, bank(KB[n % 4], 4 * SC),
                                    [lambda kd, a=a: wk[a][:, kd, c * P:(c + 1) * P] for a in range(2)],
                                    [lambda kd, a=a: cT[a][:, kd, cols] for a in range(2)], KD).then_inc(s["kp"], 1)
                        pe.wait_ge(s["wl"], whole["wv"])
                        for n in range(4):
                            if n >= 2:
                                pe.wait_ge(s["vl"], n - 1)
                            for u in range(2):
                                b0 = (2 * n + u) * SC
                                ins = product(pe, bank(2 + n % 2, 512, SC)[:, u * 256:(u + 1) * 256],
                                              [lambda kd, a=a: cT[a][:, kd, b0:b0 + SC] for a in range(2)],
                                              [lambda kd, a=a: wv[a][:, kd, :] for a in range(2)], KD)
                            ins.then_inc(s["vp"], 1)
                        pe.wait_ge(s["kst"], 2 * NC)
                        pe.wait_ge(s["vl"], 4)
                    pe.wait_ge(s["kd"], 1)
                    pe.wait_ge(s["wl"], len(pieces) + (0 if cross else 1))
                    pipeline(pe, pe_steps(pe))

        softmax_attention("a_", D // H, 64, SC, 1, True, None)
        stage_done()

        moe = ExitStack()
        with moe:
            def mb(name, shape, dt=F32):
                return moe.enter_context(nc.sbuf_tensor(name, shape, dt))

            hln = mb("hln", [P, NT, D])
            expert_of = mb("expert_of", [1, SLOT_TILES], I32)
            with nc.sbuf_tensor("mo", [P, NT, D], F32) as mo, nc.sbuf_tensor("lgT", [E, NT * P], F32) as lgT:
                with nc.sbuf_tensor("rwh", [P, KD, E], F32R) as rwh, nc.sbuf_tensor("rwl", [P, KD, E], F32R) as rwl, \
                        nc.sbuf_tensor("rb", [E, 1], F32) as rb, nc.sbuf_tensor("moTh", [P, KD, S], F32R) as moTh, \
                        nc.sbuf_tensor("moTl", [P, KD, S], F32R) as moTl, nc.sbuf_tensor("zeros", [P, D], F32) as zeros:
                    softmax_attention("b_", D // 2 // H, 32, P, TPB, False,
                                      (mo, hln, (rwh, rwl), rb, (moTh, moTl), lgT, zeros))
                    stage_done()
                with nc.sbuf_tensor("moe_w1h", [P, E, KD, F0], F32R) as w1h, \
                        nc.sbuf_tensor("moe_w1l", [P, E, KD, F0], F32R) as w1l, \
                        nc.sbuf_tensor("moe_w2h", [P, E, F0 // P, D], F32R) as w2h, \
                        nc.sbuf_tensor("moe_w2l", [P, E, F0 // P, D], F32R) as w2l:
                    weights = ((w1h, w1l), (w2h, w2l))
                    route(nc, sem, ps, t, ident, ones, before, mo, lgT, route_i, route_w, expert_of, weights, x_slots)
                    stage_done()
                    experts(nc, sem, ps, t, ident, expert_of, *weights, mo, x_slots, y_slots)
                    stage_done()
            layer_1(nc, sem, ps, t, x, hln, ident, ident16, ones, minus_half, gates, route_i, route_w, y_slots, out)


def route(nc, sem, ps, t, ident, ones, before, mo, lgT, route_i, route_w, expert_of, weights, x_slots):
    st = ExitStack()

    def tb(name, shape, dt=F32):
        return st.enter_context(nc.sbuf_tensor("r_" + name, shape, dt))

    prob = tb("prob", [P, NT, E])
    red = tb("red", [P, NT])
    rec = tb("rec", [P, NT])
    top = tb("top", [P, NT, 8])
    topi = tb("topi", [P, NT, 8], U32)
    topf = tb("topf", [P, NT, TOPK])
    iota_e = tb("iota_e", [P, E])
    iota_s = tb("iota_s", [1, SLOT_TILES])
    one_hot = tb("one_hot", [P, TOPK, NT, E])
    both = tb("both", [P, NT, E])
    total = tb("total", [P, E, NT])
    upto = tb("upto", [P, E, NT])
    tiles = tb("tiles", [P, E])
    tend = tb("tend", [P, E])
    base = tb("base", [P, E])
    place = tb("place", [P, NT, E])
    pick = tb("pick", [P, TOPK, NT, E])
    pos = tb("pos", [P, TOPK, NT])
    passed = tb("passed", [1, SLOT_TILES, E])
    npass = tb("npass", [1, SLOT_TILES])
    idx = tb("idx", [P, TOPK], U32)
    logits = tb("logits", [P, NT, E])
    stage = [tb("stage0", [P, KD * F0]), tb("stage1", [P, F0 // P * D])]
    s_w = [sem("r_w0"), sem("r_w1")]
    s_wh = [sem("r_wh0"), sem("r_wh1")]
    s_wl = [sem("r_wl0"), sem("r_wl1")]
    s_lg = sem("r_lg")
    s_iota = sem("r_iota")
    s_max = sem("r_max")
    s_exp = sem("r_exp")
    s_one = sem("r_one")
    s_cnt = sem("r_cnt")
    s_pos = sem("r_pos")
    s_sent = sem("r_sent")
    rank_ps = ps[:, 0, 0:NT * E].rearrange("p (t e) -> p t e", t=NT)
    total_ps = ps[:, 1, 0:NT * E].rearrange("p (t e) -> p e t", t=NT)
    ones_nt = ones[:, 0:NT]

    def over_experts(a):
        return a.unsqueeze(2).to_broadcast([P, NT, E])

    def flat(w, e):
        return w[:, bass.ds(e, 1), :, :].rearrange("p a k n -> p (a k n)")

    with st, nc.Block() as block:
        @block.sync
        def _(sp):
            def load(e, m):
                src = t[("moe_w1", "moe_w2")[m]][bass.ds(e, 1)].rearrange("a (k p) n -> p (a k) n", p=P)
                sp.dma_start(stage[m][:, :].rearrange("p (k n) -> p k n", k=src.shape[1]), src).then_inc(s_w[m], 16)

            for m in range(2):
                load(0, m)
            with sp.Fori(0, E - 1) as j:
                for m in range(2):
                    sp.wait_ge(s_wl[m], j + 1)
                    load(j + 1, m)

        @block.gpsimd
        def _(pool):
            pool.iota(iota_e[:, :], [[1, E]], base=0, channel_multiplier=0, allow_small_or_imprecise_dtypes=True)
            pool.iota(iota_s[:, :], [[1, SLOT_TILES]], base=0, channel_multiplier=0,
                      allow_small_or_imprecise_dtypes=True).then_inc(s_iota, 1)
            pool.wait_ge(s_pos, 1)
            for tt in range(NT):
                for j in range(TOPK):
                    pool.indirect_dma_start(x_slots[:, :], bass.IndirectOffsetOnAxis(route_i[:, tt, j:j + 1], axis=0),
                                            mo[:, tt, :], None).then_inc(s_sent, 16)
            pool.wait_ge(s_sent, 16 * NT * TOPK)

        @block.scalar
        def _(act):
            act.wait_ge(s_max, 1)
            act.activation(prob[:, :, :], prob[:, :, :], ACT.Exp).then_inc(s_exp, 1)
            with act.Fori(0, E) as e:
                for m in range(2):
                    act.wait_ge(s_w[m], 16 * e + 16)
                    act.activation(flat(weights[m][0], e), stage[m][:, :], ACT.Copy).then_inc(s_wh[m], 1)

        @block.tensor
        def _(pe):
            for tt in range(NT):
                ins = pe.transpose(ps[:, 2, tt * E:(tt + 1) * E], lgT[:, tt * P:(tt + 1) * P], ident[0:E, 0:E])
            ins.then_inc(s_lg, 1)
            pe.wait_ge(s_one, 1)
            rhs = both[:, :, :].rearrange("p t e -> p (t e)")
            pe.matmul(ps[:, 0, 0:NT * E], before[:, :], rhs, start=True, stop=True)
            pe.matmul(ps[:, 1, 0:NT * E], ones[:, :], rhs, start=True, stop=True).then_inc(s_cnt, 1)

        @block.vector
        def _(dve):
            dve.wait_ge(s_lg, 1)
            dve.tensor_copy(logits[:, :, :], ps[:, 2, 0:NT * E].rearrange("p (t e) -> p t e", t=NT))
            dve.drain()
            dve.tensor_reduce(red[:, :], logits[:, :, :], X, ALU.max)
            dve.drain()
            dve.tensor_tensor(prob[:, :, :], logits[:, :, :], over_experts(red[:, :]), ALU.subtract).then_inc(s_max, 1)
            dve.wait_ge(s_exp, 1)
            dve.tensor_reduce(red[:, :], prob[:, :, :], X, ALU.add)
            dve.drain()
            dve.reciprocal(rec[:, :], red[:, :])
            dve.drain()
            dve.tensor_tensor(prob[:, :, :], prob[:, :, :], over_experts(rec[:, :]), ALU.mult)
            dve.drain()
            for tt in range(NT):
                dve.max(top[:, tt, :], prob[:, tt, :])
            dve.drain()
            for tt in range(NT):
                dve.max_index(topi[:, tt, :], top[:, tt, :], prob[:, tt, :])
            dve.drain()
            dve.tensor_reduce(red[:, :], top[:, :, 0:TOPK], X, ALU.add)
            dve.tensor_copy(topf[:, :, :], topi[:, :, 0:TOPK])
            dve.drain()
            dve.tensor_scalar(red[:, :], red[:, :], 1e-8, None, ALU.add)
            dve.wait_ge(s_iota, 1)
            for j in range(TOPK):
                dve.tensor_tensor(one_hot[:, j, :, :], over_experts(topf[:, :, j]),
                                  iota_e[:, :].unsqueeze(1).to_broadcast([P, NT, E]), ALU.is_equal)
            dve.drain()
            dve.reciprocal(rec[:, :], red[:, :])
            dve.tensor_tensor(both[:, :, :], one_hot[:, 0, :, :], one_hot[:, 1, :, :], ALU.add).then_inc(s_one, 1)
            dve.drain()
            dve.tensor_tensor(route_w[:, :, :], top[:, :, 0:TOPK],
                              rec[:, :].unsqueeze(2).to_broadcast([P, NT, TOPK]), ALU.mult)
            dve.wait_ge(s_cnt, 1)
            dve.tensor_copy(total[:, :, :], total_ps)
            dve.drain()
            for e in range(E):
                dve.tensor_tensor_scan(upto[:, e, :], ones_nt, total[:, e, :], 0.0, ALU.mult, ALU.add)
            dve.drain()
            dve.tensor_scalar(tiles[:, :], upto[:, :, NT - 1], 127.0, 1.0 / P, ALU.add, ALU.mult)
            dve.drain()
            dve.tensor_scalar(tiles[:, :], tiles[:, :], -127.0 / 256, ROUND, ALU.add, ALU.add)
            dve.drain()
            dve.tensor_scalar(tiles[:, :], tiles[:, :], -ROUND, None, ALU.add)
            dve.drain()
            dve.tensor_tensor_scan(tend[:, :], ones[:, 0:E], tiles[:, :], 0.0, ALU.mult, ALU.add)
            dve.drain()
            dve.tensor_tensor(base[:, :], tend[:, :], tiles[:, :], ALU.subtract)
            dve.tensor_tensor(upto[:, :, :], upto[:, :, :], total[:, :, :], ALU.subtract)
            dve.tensor_tensor(passed[:, :, :], iota_s[:, :].unsqueeze(2).to_broadcast([1, SLOT_TILES, E]),
                              tend[0:1, :].unsqueeze(1).to_broadcast([1, SLOT_TILES, E]), ALU.is_ge)
            dve.drain()
            dve.tensor_tensor(place[:, :, :], rank_ps, upto[:, :, :].rearrange("p e t -> p t e"), ALU.add)
            dve.tensor_reduce(npass[:, :], passed[:, :, :], X, ALU.add)
            dve.tensor_scalar(base[:, :], base[:, :], float(P), None, ALU.mult)
            dve.drain()
            dve.tensor_scalar(npass[:, :], npass[:, :], float(E - 1), None, ALU.min)
            dve.tensor_tensor(place[:, :, :], place[:, :, :], base[:, :].unsqueeze(1).to_broadcast([P, NT, E]),
                              ALU.add)
            dve.drain()
            dve.tensor_copy(expert_of[:, :], npass[:, :])
            for j in range(TOPK):
                dve.tensor_tensor(pick[:, j, :, :], one_hot[:, j, :, :], place[:, :, :], ALU.mult)
            dve.drain()
            for j in range(TOPK):
                dve.tensor_reduce(pos[:, j, :], pick[:, j, :, :], X, ALU.add)
            dve.drain()
            dve.tensor_copy(route_i[:, :, :], pos[:, :, :].rearrange("p j t -> p t j")).then_inc(s_pos, 1)
            with dve.Fori(0, E) as e:
                for m in range(2):
                    dve.wait_ge(s_wh[m], e + 1)
                    dve.tensor_tensor(flat(weights[m][1], e), stage[m][:, :], flat(weights[m][0], e).bitcast(F32),
                                      ALU.subtract).then_inc(s_wl[m], 1)


def experts(nc, sem, ps, t, ident, expert_of, w1, w2, room, x_slots, y_slots):
    st = ExitStack()

    def tb(name, shape, dt=F32):
        return st.enter_context(nc.sbuf_tensor("e_" + name, shape, dt))

    FK = F0 // P
    b1 = tb("b1", [P, E, FK])
    b2 = tb("b2", [P, E, D])
    xT = [tb("xTh", [P, 2, KD, P], F32R), tb("xTl", [P, 2, KD, P], F32R)]
    xs, ys = room[:, 0:2, :], room[:, 2:4, :]
    h = room[:, 4:8, :].rearrange("p (u a) d -> p u (a d)", u=2)
    g = room[:, 8:12, :].rearrange("p (u k) (c s) -> p u (k c) s", u=2, s=P)
    gT = [tb("gTh", [P, 2, FK, P], F32R), tb("gTl", [P, 2, FK, P], F32R)]
    names = "w in0 in1 xT xTh xTl h he hT g gl y ye out0 out1".split()
    s = {n: sem("e_s_" + n) for n in names}
    xT_ps = [ps[:, u, 0:KD * P].rearrange("p (k s) -> p k s", k=KD) for u in range(2)]
    h_ps = [ps[:, 2 + u, :] for u in range(2)]
    hT_ps = [ps[:, 4 + u, :].rearrange("p (k s) -> p k s", k=FK) for u in range(2)]
    y_ps = [ps[:, 6 + u, 0:D] for u in range(2)]
    xv = x_slots.rearrange("(i p) d -> i p d", p=P)
    yv = y_slots.rearrange("(i p) d -> i p d", p=P)
    N = SLOT_TILES // 2
    passes = [(0, 0), (0, 1), (1, 0)]

    STEPS = "h0 y-1 t0 h1 x2 y0 t1 x3".split()

    def after(eng, semaphore, n):
        if not (isinstance(n, int) and n <= 0):
            eng.wait_ge(semaphore, n)

    def run(parts, i, steps, load=None):
        expert = {}
        for name in steps:
            u = int(name[1:])
            if name[0] in parts:
                n = 2 * i + u
                if load and name[0] in load[1]:
                    if u not in expert:
                        expert[u] = load[0].value_load(expert_of[0:1, bass.ds(n, 1)], min_val=0, max_val=E - 1)
                    parts[name[0]](n, u % 2, expert[u])
                else:
                    parts[name[0]](n, u % 2)

    def pipeline(eng, parts, load=None):
        run(parts, 0, ["x0", "x1"], load)
        run(parts, 0, [name for name in STEPS if name != "y-1"], load)
        run(parts, 1, STEPS, load)
        with eng.Fori(0, N - 3) as j:
            run(parts, j + 2, STEPS, load)
        run(parts, N - 1, [name for name in STEPS if name[0] != "x"] + ["y1"], load)

    with st, nc.Block() as block:
        @block.sync
        def _(sp):
            sp.dma_start(b1[:, :, :], t["moe_b1"]).then_inc(s["w"], 16)
            sp.dma_start(b2[:, :, :].rearrange("p e f -> p (e f)"),
                         t["moe_b2"].rearrange("e f -> (e f)").partition_broadcast(P)).then_inc(s["w"], 16)
            with sp.Fori(0, N) as i:
                for u in range(2):
                    sp.wait_ge(s["ye"], 2 * i + u + 1)
                    sp.dma_start(yv[bass.ds(2 * i + u, 1)].rearrange("a p d -> (a p) d"), ys[:, u, :])\
                        .then_inc(s[f"out{u}"], 16)
            for u in range(2):
                sp.wait_ge(s[f"out{u}"], 16 * N)

        @block.gpsimd
        def _(pool):
            for u in range(2):
                pool.dma_start(xs[:, u, :], xv[u]).then_inc(s[f"in{u}"], 16)
            with pool.Fori(0, N - 1) as i:
                for u in range(2):
                    pool.wait_ge(s["xT"], 2 * i + u + 1)
                    pool.dma_start(xs[:, u, :], xv[bass.ds(2 * i + u + 2, 1)].rearrange("a p d -> (a p) d"))\
                        .then_inc(s[f"in{u}"], 16)

        @block.tensor
        def _(pe):
            def x_(n, u):
                pe.wait_ge(s[f"in{u}"], 8 * (n - u) + 16)
                after(pe, s["xTl"], n - 1)
                for kd in range(KD):
                    ins = pe.transpose(xT_ps[u][:, kd, :], xs[:, u, kd * P:(kd + 1) * P], ident[:, :])
                ins.then_inc(s["xT"], 1)

            def h_(n, u, e):
                pe.wait_ge(s["xTl"], n + 1)
                after(pe, s["he"], n - 1)
                for kd in range(KD):
                    for m, (a, b) in enumerate(passes):
                        ins = pe.matmul(h_ps[u], xT[a][:, u, kd, :], w1[b][:, bass.ds(e, 1), kd, :],
                                        start=(kd == 0 and m == 0), stop=(kd == KD - 1 and m == 2))
                ins.then_inc(s["h"], 1)

            def t_(n, u):
                pe.wait_ge(s["he"], n + 1)
                after(pe, s["g"], 2 * (n - 1))
                for c in range(FK):
                    ins = pe.transpose(hT_ps[u][:, c, :], h[:, u, c * P:(c + 1) * P], ident[:, :])
                ins.then_inc(s["hT"], 1)

            def y_(n, u, e):
                after(pe, s["ye"], n - 1)
                for c in range(FK):
                    if c % 2 == 0:
                        pe.wait_ge(s["gl"], 2 * n + c // 2 + 1)
                    for m, (a, b) in enumerate(passes):
                        ins = pe.matmul(y_ps[u], gT[a][:, u, c, :], w2[b][:, bass.ds(e, 1), c, :],
                                        start=(c == 0 and m == 0), stop=(c == FK - 1 and m == 2))
                ins.then_inc(s["y"], 1)

            pipeline(pe, {"x": x_, "h": h_, "t": t_, "y": y_}, (pe, "hy"))

        @block.scalar
        def _(act):
            def x_(n, u):
                act.wait_ge(s["xT"], n + 1)
                after(act, s["h"], n - 1)
                act.activation(xT[0][:, u, :, :], xT_ps[u], ACT.Identity).then_inc(s["xTh"], 1)

            def t_(n, u, e):
                act.wait_ge(s["hT"], n + 1)
                after(act, s["gl"], 2 * (n - 1))
                for c in range(FK):
                    ins = act.activation(g[:, u, c, :], hT_ps[u][:, c, :], ACT.Gelu,
                                         bias=b1[:, bass.ds(e, 1), c])
                    if c % 2:
                        ins.then_inc(s["g"], 1)

            act.wait_ge(s["w"], 32)
            pipeline(act, {"x": x_, "t": t_}, (act, "t"))

        @block.vector
        def _(dve):
            def x_(n, u):
                dve.wait_ge(s["xTh"], n + 1)
                dve.tensor_tensor(xT[1][:, u, :, :], xT_ps[u], xT[0][:, u, :, :].bitcast(F32), ALU.subtract)\
                    .then_inc(s["xTl"], 1)

            def h_(n, u):
                dve.wait_ge(s["h"], n + 1)
                after(dve, s["hT"], n - 1)
                dve.tensor_copy(h[:, u, :], h_ps[u]).then_inc(s["he"], 1)

            def t_(n, u):
                for half in range(2):
                    cs = slice(2 * half, 2 * half + 2)
                    dve.wait_ge(s["g"], 2 * n + half + 1)
                    if half == 0:
                        after(dve, s["y"], n - 1)
                    dve.tensor_copy(gT[0][:, u, cs, :], g[:, u, cs, :])
                    dve.drain()
                    dve.tensor_tensor(gT[1][:, u, cs, :], g[:, u, cs, :], gT[0][:, u, cs, :].bitcast(F32),
                                      ALU.subtract).then_inc(s["gl"], 1)

            def y_(n, u, e):
                dve.wait_ge(s["y"], n + 1)
                after(dve, s[f"out{u}"], 8 * (n - u))
                dve.tensor_tensor(ys[:, u, :], y_ps[u], b2[:, bass.ds(e, 1), :].rearrange("p a f -> p (a f)"),
                                  ALU.add).then_inc(s["ye"], 1)

            dve.wait_ge(s["w"], 32)
            pipeline(dve, {"x": x_, "h": h_, "t": t_, "y": y_}, (dve, "y"))


def layer_1(nc, sem, ps, t, x, hln, ident, ident16, ones, minus_half, gates, route_i, route_w, y_slots, out):
    st = ExitStack()

    def tb(name, shape, dt=F32):
        return st.enter_context(nc.sbuf_tensor("c_" + name, shape, dt))

    IK = INNER // P
    FK = FF // P
    wq = [tb("wqh", [P, KD, INNER], F32R), tb("wql", [P, KD, INNER], F32R)]
    wk = tb("wk", [P, KD, INNER])
    wv = tb("wv", [P, KD, INNER])
    wo = tb("wo", [P, IK, D])
    w1 = tb("w1", [P, KD, FF])
    w2 = tb("w2", [P, FK, D])
    b1 = tb("b1", [P, FK])
    lnw = tb("lnw", [P, 4, KD])
    bo = tb("bo", [P, D])
    b2 = tb("b2", [P, D])
    f_stats = tb("f_stats", [P, TPB, 6])
    f_mv = tb("f_mv", [P, TPB, 2])
    f_var = tb("f_var", [P, TPB])
    f_rstd = tb("f_rstd", [P, TPB])
    c_stats = tb("c_stats", [P, 6])
    c_mv = tb("c_mv", [P, 2])
    c_var = tb("c_var", [P, 1])
    c_rstd = tb("c_rstd", [P, 1])
    idx = tb("idx", [P, TPB * TOPK], U32)
    yg = tb("yg", [P, TPB, TOPK, D])
    mix = tb("mix", [P, TPB, D])
    xq = tb("xq", [P, TPB, D])
    xh = tb("xh", [P, TPB, D])
    xT = tb("xT", [P, KD, S])
    xTs = [tb("xTh", [P, KD, S], F32R), tb("xTl", [P, KD, S], F32R)]
    cx = tb("cx", [P, D])
    cT = tb("cT", [P, KD, SC])
    ksq = tb("ksq", [P, INNER])
    kss = tb("kss", [P, H])
    krn = tb("krn", [P, H])
    kn = tb("kn", [P, INNER])
    vv = tb("vv", [P, INNER])
    mT = tb("mT", [P, IK, P])
    gm = tb("gm", [P, IK, D])
    b_stats = tb("b_stats", [P, TPB, 6])
    b_mv = tb("b_mv", [P, TPB, 2])
    b_var = tb("b_var", [P, TPB])
    b_rstd = tb("b_rstd", [P, TPB])
    qsq = tb("qsq", [P, INNER])
    qss = tb("qss", [P, H])
    qrn = tb("qrn", [P, H])
    qn = tb("qn", [P, INNER])
    qT = tb("qT", [P, TPB, IK, P])
    xo = tb("xo", [P, TPB, D])
    xh2 = tb("xh2", [P, TPB, D])
    xT2 = tb("xT2", [P, KD, S])
    hT = tb("hT", [P, FK, S])
    wb = [tb("wb1", [P, KD, FF], BF16), tb("wb2", [P, FK, D], BF16)]
    part = tb("part", [P, 2])
    sw = tb("sw", [P, 2])
    half = tb("half", [P, 2, 2])
    t_stats = tb("t_stats", [P, 6])
    t_mv = tb("t_mv", [P, 2])
    t_var = tb("t_var", [P, 1])
    t_rstd = tb("t_rstd", [P, 1])
    th = tb("th", [P, D])
    tr = tb("tr", [P, D])
    ti = tb("ti", [P, D], BF16)
    tT = tb("tT", [P, KD, P], BF16)
    g2 = tb("g2", [P, 2, FF])
    g, gr = g2[:, 0, :], g2[:, 1, :]
    gi = tb("gi", [P, FF], BF16)
    gT = tb("gT", [P, FK, P], BF16)
    am = tb("am", [P, 2])
    sc = tb("sc", [P, 2])
    un = tb("un", [P, 2])
    wf = [tb("wf1", [P, KD, FF]), tb("wf2", [P, FK, D])]
    neg = g2[:, :, :].rearrange("p a n -> p (a n)")
    wq_f = hT[:, :, :].rearrange("p c s -> p (c s)")

    names = "wg wf wq wqh wql wb wt ctx gath cvar crstd cn cT cTe v ve k ks kss kr kn M Me G Ge xvar xrstd qvar qrstd xn xT xTe " \
            "q qs qss qr qn qT qTe o ovar orstd x2 x2T x2Te h he y ye xTl " \
            "part sum tvar trstd ti tT tTe g ge gi gT gTe ty fin store".split()
    s = {n: sem("c_s_" + n) for n in names}

    front = ps[:, 0:2, :].rearrange("p b n -> p (b n)")
    back = ps[:, 2:4, :].rearrange("p b n -> p (b n)")
    cT_ps = ps[:, 0, 0:KD * SC].rearrange("p (k s) -> p k s", k=KD)
    xT_ps = ps[:, 0, :].rearrange("p (k s) -> p k s", k=KD)
    x2T_ps = ps[:, 4, :].rearrange("p (k s) -> p k s", k=KD)
    attended = [ps[:, 4, 0:D], ps[:, 2, 0:D]]
    g_ps = ps[:, 5:7, :].rearrange("p b n -> p (b n)")
    tT_ps = ps[:, 7, 0:P].bitcast(BF16).rearrange("p (k s) -> p k s", k=KD)
    gT_ps = ps[:, 7, :].bitcast(BF16).rearrange("p (k s) -> p k s", k=FK)
    ty_ps = ps[:, 7, 0:D]
    sum_ps = ps[:, 7, 0:2]
    ov = out.rearrange("b (t p) d -> (b t) p d", p=P)

    passes = [(0, 0), (0, 1), (1, 0)]

    STEPS = ("s_wq t0_stats b_q0 t0_i b_xo f_k t0_h b_n0 f_ks f_gather t0_g f_kn t0_scale t0_round b_q1 f_v "
             "t0_gT f_m t0_y w_part b_n1 w_sum t0_out t1_stats f_me t1_i b_o b_o0 f_mix b_x0 b_o1 t1_h f_g0 t1_g "
             "b_x1 b_x f_g1 w_round0 b_h f_res w_round1 f_q f_x t1_scale t1_round b_y0 t1_gT f_xT g_ctx "
             "g_cn b_r0 b_y1 b_r1 g_cT t1_y t1_out").split()

    def heads(a):
        return a.rearrange("p (h e) -> p h e", h=H)

    def after(eng, semaphore, n):
        if not (isinstance(n, int) and n <= 0):
            eng.wait_ge(semaphore, n)

    def run(parts, i, streams):
        for name in STEPS:
            if name in parts and name[0] in streams:
                kind = name[0]
                if kind == "g":
                    parts[name](i + 2)
                elif kind == "f":
                    parts[name](i + 1)
                elif kind == "b":
                    parts[name](i)
                elif kind in "ws":
                    parts[name]()
                else:
                    parts[name](TPB * (i - 1) + int(name[1]))

    def pipeline(eng, parts):
        eng.wait_ge(s["wg"], 16)
        run(parts, -2, "g")
        eng.wait_ge(s["wf"], 48)
        run(parts, -1, "gf")
        eng.wait_ge(s["wb"], 80)
        run(parts, 0, "gfbws")
        run(parts, 1, "gfbt")
        with eng.Fori(0, B - 4) as j:
            run(parts, j + 2, "gfbt")
        run(parts, B - 2, "fbt")
        run(parts, B - 1, "bt")
        run(parts, B, "t")

    with st, nc.Block() as block:
        @block.sync
        def _(sp):
            sp.dma_start(cx[0:SC, :], t["ctx"][0]).then_inc(s["ctx"], 16)
            sp.dma_start(lnw[:, :, :], t["l1_ln"]).then_inc(s["wg"], 16)

            def load(dst, n, semaphore):
                sp.dma_start(dst[:, :, :], t[n].rearrange("(k p) n -> p k n", p=P)).then_inc(s[semaphore], 16)

            for dst, n in ((wv, "l1_wv"), (wk, "l1_wk"), (wo, "l1_wo")):
                load(dst, n, "wf")
            sp.dma_start(wq_f.rearrange("p (k n) -> p k n", k=KD), t["l1_wq"].rearrange("(k p) n -> p k n", p=P))\
                .then_inc(s["wq"], 16)
            for dst, n in ((w1, "l1_w1"), (w2, "l1_w2")):
                load(dst, n, "wb")
            sp.dma_start(b1[:, :], t["l1_b1"]).then_inc(s["wb"], 16)
            sp.dma_start(bo[:, :], t["l1_bo"].partition_broadcast(P)).then_inc(s["wb"], 16)
            sp.dma_start(b2[:, :], t["l1_b2"].partition_broadcast(P)).then_inc(s["wb"], 16)
            for dst, n in ((wf[0], "ff_w1t"), (wf[1], "ff_w2t")):
                load(dst, n, "wt")
            with sp.Fori(0, B - 1) as j:
                sp.wait_ge(s["cT"], j + 1)
                sp.dma_start(cx[0:SC, :], t["ctx"][bass.ds(j + 1, 1)].rearrange("a s d -> (a s) d"))\
                    .then_inc(s["ctx"], 16)

        @block.gpsimd
        def _(pool):
            def rsqrt(dst, src, n, wanted, done):
                pool.wait_ge(s[wanted], n)
                w = src.shape[-1]
                r = src.shape[0]
                pool.tensor_tensor(dst, src, minus_half[0:r, 0:w], ALU.pow).then_inc(s[done], 1)

            def queries(n):
                for hf in range(2):
                    hs = slice(hf * H // 2, (hf + 1) * H // 2)
                    rsqrt(qrn[:, hs], qss[:, hs], 2 * n + hf + 1, "qss", "qr")

            def gather(f):
                after(pool, s["gath"], 64 * f)
                after(pool, s["xvar"], f)
                pool.tensor_copy(idx[:, :], route_i[:, bass.ds(TPB * f, TPB), :].rearrange("p t j -> p (t j)"))
                pool.drain()
                for tt in range(TPB):
                    for j in range(TOPK):
                        n = tt * TOPK + j
                        pool.indirect_dma_start(yg[:, tt, j, :], None, y_slots[:, :],
                                                bass.IndirectOffsetOnAxis(idx[:, n:n + 1], axis=0))\
                            .then_inc(s["gath"], 16)

            parts = {
                "f_gather": gather,
                "g_ctx": lambda f: rsqrt(c_rstd[0:SC, :], c_var[0:SC, :], f + 1, "cvar", "crstd"),
                "f_ks": lambda f: rsqrt(krn[0:SC, :], kss[0:SC, :], f + 1, "kss", "kr"),
                "f_res": lambda f: rsqrt(f_rstd[:, :], f_var[:, :], f + 1, "xvar", "xrstd"),
                "f_q": lambda f: rsqrt(f_rstd[:, :], f_var[:, :], f + 1, "qvar", "qrstd"),
                "b_q0": lambda i: queries(TPB * i),
                "b_q1": lambda i: queries(TPB * i + 1),
                "b_o0": lambda i: rsqrt(b_rstd[:, 0:1], b_var[:, 0:1], TPB * i + 1, "ovar", "orstd"),
                "b_o1": lambda i: rsqrt(b_rstd[:, 1:2], b_var[:, 1:2], TPB * i + 2, "ovar", "orstd"),
                "t0_stats": lambda n: rsqrt(t_rstd[:, :], t_var[:, :], n + 1, "tvar", "trstd"),
                "t1_stats": lambda n: rsqrt(t_rstd[:, :], t_var[:, :], n + 1, "tvar", "trstd"),
            }
            pipeline(pool, parts)

        @block.vector
        def _(dve):
            def norm_stats(src, n, stats, mv, var, done):
                for tt in range(n):
                    dve.bn_stats(stats[:, tt, :], src(tt))
                dve.drain()
                for tt in range(n):
                    dve.bn_aggr(mv[:, tt, :], stats[:, tt, :])
                dve.drain()
                dve.tensor_scalar(var[:, :], mv[:, :, 1], EPS, None, ALU.add).then_inc(s[done], 1)

            def gained(dst, src, first):
                for kd in range(KD):
                    ins = dve.tensor_scalar(dst[:, kd, :], src[:, kd, :], lnw[:, first, kd:kd + 1],
                                            lnw[:, first + 1, kd:kd + 1], ALU.mult, ALU.add)
                return ins

            def f_ctx(f):
                dve.wait_ge(s["ctx"], 16 * f + 16)
                dve.bn_stats(c_stats[0:SC, :], cx[0:SC, :])
                dve.drain()
                dve.bn_aggr(c_mv[0:SC, :], c_stats[0:SC, :])
                dve.drain()
                dve.tensor_scalar(c_var[0:SC, :], c_mv[0:SC, 1:2], EPS, None, ALU.add).then_inc(s["cvar"], 1)

            def f_cn(f):
                dve.wait_ge(s["crstd"], f + 1)
                dve.tensor_scalar(cx[0:SC, :], cx[0:SC, :], c_mv[0:SC, 0:1], c_rstd[0:SC, 0:1],
                                  ALU.subtract, ALU.mult).then_inc(s["cn"], 1)

            def f_cTe(f):
                dve.wait_ge(s["cT"], f + 1)
                after(dve, s["v"], f)
                gained(cT, cT_ps, 0).then_inc(s["cTe"], 1)

            def f_k(f):
                dve.wait_ge(s["ks"], f + 1)
                dve.tensor_reduce(kss[0:SC, :], heads(ksq[0:SC, :]), X, ALU.add)
                dve.drain()
                dve.tensor_scalar(kss[0:SC, :], kss[0:SC, :], 1e-24, None, ALU.max).then_inc(s["kss"], 1)

            def f_kn(f):
                dve.wait_ge(s["kr"], f + 1)
                after(dve, s["M"], f)
                dve.tensor_tensor(heads(kn[0:SC, :]), heads(front[0:SC, :]),
                                  krn[0:SC, :].unsqueeze(2).to_broadcast([SC, H, HD1]), ALU.mult)\
                    .then_inc(s["kn"], 1)

            def f_me(f):
                dve.wait_ge(s["M"], f + 1)
                after(dve, s["G"], 2 * f)
                for u in range(2):
                    rows = slice(64 * u, 64 * u + 64)
                    ins = dve.tensor_copy(mT[rows, :, rows],
                                          front[rows, :].rearrange("p (c n) -> p c n", c=IK)[:, :, rows])
                ins.then_inc(s["Me"], 1)

            def f_mix(f):
                dve.wait_ge(s["gath"], 64 * f + 64)
                for tt in range(TPB):
                    dve.tensor_scalar(mix[:, tt, :], yg[:, tt, 0, :], route_w[:, bass.ds(TPB * f + tt, 1), 0],
                                      None, ALU.mult)
                dve.drain()
                for tt in range(TPB):
                    dve.scalar_tensor_tensor(mix[:, tt, :], yg[:, tt, 1, :], route_w[:, bass.ds(TPB * f + tt, 1), 1],
                                             mix[:, tt, :], ALU.mult, ALU.add)
                dve.drain()

            def f_res(f):
                dve.scalar_tensor_tensor(mix[:, :, :], mix[:, :, :], 0.3, hln[:, bass.ds(TPB * f, TPB), :],
                                         ALU.mult, ALU.add)
                dve.drain()
                xb = x[:, bass.ds(TPB * f, TPB), :]
                dve.scalar_tensor_tensor(xb, mix[:, :, :], gates[:, 1:2], xb, ALU.mult, ALU.add)
                dve.drain()
                norm_stats(lambda tt: x[:, bass.ds(TPB * f + tt, 1), :], TPB, f_stats, f_mv, f_var, "xvar")

            def f_q(f):
                dve.wait_ge(s["xrstd"], f + 1)
                for tt in range(TPB):
                    dve.tensor_scalar(xq[:, tt:tt + 1, :], x[:, bass.ds(TPB * f + tt, 1), :], f_mv[:, tt, 0:1],
                                      f_rstd[:, tt:tt + 1], ALU.subtract, ALU.mult)
                dve.drain()
                norm_stats(lambda tt: xq[:, tt, :], TPB, f_stats, f_mv, f_var, "qvar")

            def f_x(f):
                dve.wait_ge(s["qrstd"], f + 1)
                after(dve, s["xT"], f)
                for tt in range(TPB):
                    ins = dve.tensor_scalar(xh[:, tt, :], xq[:, tt, :], f_mv[:, tt, 0:1], f_rstd[:, tt:tt + 1],
                                            ALU.subtract, ALU.mult)
                ins.then_inc(s["xn"], 1)

            def f_xT(f):
                dve.wait_ge(s["xT"], f + 1)
                after(dve, s["q"], 2 * TPB * f)
                gained(xT, xT_ps, 0).then_inc(s["xTe"], 1)
                dve.drain()
                dve.tensor_copy(xTs[0][:, :, :], xT[:, :, :])
                dve.drain()
                dve.tensor_tensor(xTs[1][:, :, :], xT[:, :, :], xTs[0][:, :, :].bitcast(F32), ALU.subtract)\
                    .then_inc(s["xTl"], 1)

            def b_q(n):
                for hf in range(2):
                    hs = slice(hf * H // 2, (hf + 1) * H // 2)
                    dve.wait_ge(s["qs"], 2 * n + hf + 1)
                    dve.tensor_reduce(qss[:, hs], heads(qsq[:, :])[:, hs, :], X, ALU.add)
                    dve.drain()
                    dve.tensor_scalar(qss[:, hs], qss[:, hs], 1e-24, None, ALU.max).then_inc(s["qss"], 1)

            def b_n(n):
                after(dve, s["qT"], n)
                for hf in range(2):
                    hs = slice(hf * H // 2, (hf + 1) * H // 2)
                    dve.wait_ge(s["qr"], 2 * n + hf + 1)
                    dve.tensor_tensor(heads(qn[:, :])[:, hs, :], heads(back)[:, hs, :],
                                      qrn[:, hs].unsqueeze(2).to_broadcast([P, H // 2, HD1]),
                                      ALU.mult).then_inc(s["qn"], 1)

            def b_xo(i):
                dve.tensor_tensor(xo[:, :, :], xq[:, :, :], bo[:, :].unsqueeze(1).to_broadcast([P, TPB, D]), ALU.add)
                dve.drain()

            def b_o(i, tt):
                dve.wait_ge(s["o"], TPB * i + tt + 1)
                dve.tensor_tensor(xo[:, tt, :], xo[:, tt, :], attended[tt], ALU.add)
                dve.drain()
                norm_stats(lambda _: xo[:, tt, :], 1, b_stats[:, tt:tt + 1, :], b_mv[:, tt:tt + 1, :],
                           b_var[:, tt:tt + 1], "ovar")

            def b_x(i, tt):
                dve.wait_ge(s["orstd"], TPB * i + tt + 1)
                after(dve, s["x2T"], i)
                dve.tensor_scalar(xh2[:, tt, :], xo[:, tt, :], b_mv[:, tt, 0:1], b_rstd[:, tt:tt + 1],
                                  ALU.subtract, ALU.mult).then_inc(s["x2"], 1)

            def b_h(i):
                dve.wait_ge(s["x2T"], i + 1)
                after(dve, s["h"], 4 * i)
                gained(xT2, x2T_ps, 2).then_inc(s["x2Te"], 1)
                dve.drain()
                dve.tensor_tensor(xo[:, :, :], xo[:, :, :], b2[:, :].unsqueeze(1).to_broadcast([P, TPB, D]), ALU.add)
                dve.drain()

            def b_r(i, tt):
                dve.wait_ge(s["y"], TPB * i + tt + 1)
                dve.tensor_tensor(xo[:, tt, :], xo[:, tt, :], attended[tt], ALU.add).then_inc(s["ye"], 1)
                dve.drain()
                xb = tile(TPB * i + tt)
                dve.scalar_tensor_tensor(xb, xo[:, tt, :], gates[:, 2:3], xb, ALU.mult, ALU.add)
                dve.drain()

            def magnitude(src, n):
                dve.tensor_reduce(am[:, n:n + 1], src, X, ALU.max, apply_absolute_value=True)
                dve.drain()
                dve.tensor_scalar(am[:, n:n + 1], am[:, n:n + 1], EPS, None, ALU.max)
                dve.drain()
                dve.reciprocal(sc[:, n:n + 1], am[:, n:n + 1])
                dve.tensor_scalar(un[:, n:n + 1], am[:, n:n + 1], sw[:, n:n + 1], 1.0 / 127, ALU.mult, ALU.mult)
                dve.drain()
                dve.tensor_scalar(sc[:, n:n + 1], sc[:, n:n + 1], 127.0, None, ALU.mult)
                dve.drain()

            def quantised(src, n, rounded, dst):
                dve.tensor_scalar(rounded, src, sc[:, n:n + 1], ROUND, ALU.mult, ALU.add)
                dve.drain()
                return dve.tensor_scalar(dst, rounded, -ROUND, 127.0, ALU.add, ALU.min)

            def tile(n):
                return x[:, bass.ds(n, 1), :].rearrange("p a d -> p (a d)")

            def t_stats_of(n):
                dve.bn_stats(t_stats[:, :], tile(n))
                dve.drain()
                dve.bn_aggr(t_mv[:, :], t_stats[:, :])
                dve.drain()
                dve.tensor_scalar(t_var[:, :], t_mv[:, 1:2], EPS, None, ALU.add).then_inc(s["tvar"], 1)

            def t_i(n):
                dve.wait_ge(s["trstd"], n + 1)
                dve.tensor_scalar(th[:, :], tile(n), t_mv[:, 0:1], t_rstd[:, 0:1], ALU.subtract, ALU.mult)
                dve.drain()
                after(dve, s["tT"], n)
                magnitude(th[:, :], 0)
                quantised(th[:, :], 0, tr[:, :], ti[:, :]).then_inc(s["ti"], 1)

            def t_scale(n):
                dve.wait_ge(s["ge"], n + 1)
                magnitude(g[:, :], 1)

            def t_round(n):
                after(dve, s["gT"], n)
                quantised(g[:, :], 1, gr[:, :], gi[:, :]).then_inc(s["gi"], 1)

            def t_out(n):
                dve.wait_ge(s["ty"], n + 1)
                dve.tensor_scalar(tr[:, :], ty_ps, un[:, 1:2], gates[:, 3:4], ALU.mult, ALU.mult)
                dve.drain()
                dve.tensor_tensor(tile(n), tr[:, :], tile(n), ALU.add).then_inc(s["fin"], 1)

            flat = [w[:, :, :].rearrange("p k n -> p (k n)") for w in wf]
            flatb = [w[:, :, :].rearrange("p k n -> p (k n)") for w in wb]

            def s_wq():
                dve.wait_ge(s["wqh"], 1)
                dve.tensor_tensor(wq[1][:, :, :].rearrange("p k n -> p (k n)"), wq_f,
                                  wq[0][:, :, :].rearrange("p k n -> p (k n)").bitcast(F32), ALU.subtract)\
                    .then_inc(s["wql"], 1)

            def w_part():
                dve.wait_ge(s["wt"], 32)
                for n in range(2):
                    ins = dve.tensor_reduce(part[:, n:n + 1], flat[n], X, ALU.add, apply_absolute_value=True)
                ins.then_inc(s["part"], 1)

            def w_sum():
                dve.wait_ge(s["sum"], 1)
                dve.tensor_scalar(sw[:, :], sum_ps, 1.0 / (D * FF), EPS, ALU.mult, ALU.max)
                dve.drain()
                dve.tensor_scalar(half[:, :, 0], sw[:, :], 0.5, None, ALU.mult)
                dve.tensor_scalar(half[:, :, 1], sw[:, :], -0.5, None, ALU.mult)
                dve.drain()

            def w_round(n):
                dve.tensor_scalar(neg[:, :], flat[n], half[:, n, 1:2], None, ALU.is_lt)
                dve.drain()
                dve.scalar_tensor_tensor(flatb[n], flat[n], half[:, n, 0:1], neg[:, :], ALU.is_gt, ALU.subtract)
                dve.drain()

            dve.memset(mT[:, :, :], 0.0)
            parts = {
                "g_ctx": f_ctx, "g_cn": f_cn, "g_cT": f_cTe, "f_ks": f_k, "f_kn": f_kn, "f_me": f_me, "f_mix": f_mix,
                "f_res": f_res, "f_q": f_q, "f_x": f_x, "f_xT": f_xT,
                "b_q0": lambda i: b_q(TPB * i), "b_q1": lambda i: b_q(TPB * i + 1),
                "b_n0": lambda i: b_n(TPB * i), "b_n1": lambda i: b_n(TPB * i + 1),
                "b_o0": lambda i: b_o(i, 0), "b_o1": lambda i: b_o(i, 1),
                "b_x0": lambda i: b_x(i, 0), "b_x1": lambda i: b_x(i, 1), "b_h": b_h,
                "b_r0": lambda i: b_r(i, 0), "b_r1": lambda i: b_r(i, 1),
                "t0_stats": t_stats_of, "t1_stats": t_stats_of, "t0_i": t_i, "t1_i": t_i,
                "b_xo": b_xo, "t0_scale": t_scale, "t1_scale": t_scale,
                "t0_round": t_round, "t1_round": t_round, "t0_out": t_out, "t1_out": t_out,
                "s_wq": s_wq, "w_part": w_part, "w_sum": w_sum, "w_round0": lambda: w_round(0), "w_round1": lambda: w_round(1),
            }
            pipeline(dve, parts)

        @block.scalar
        def _(act):
            def f_v(f):
                act.wait_ge(s["v"], f + 1)
                after(act, s["M"], f)
                act.activation(vv[0:SC, :], front[0:SC, :], ACT.Copy).then_inc(s["ve"], 1)

            def f_k(f):
                act.wait_ge(s["k"], f + 1)
                after(act, s["kss"], f)
                act.activation(ksq[0:SC, :], front[0:SC, :], ACT.Square).then_inc(s["ks"], 1)

            def f_g(f, h):
                act.wait_ge(s["G"], 2 * f + h + 1)
                if h == 0:
                    after(act, s["o"], TPB * f)
                act.activation(gm[:, 4 * h:4 * h + 4, :].rearrange("p c n -> p (c n)"), front, ACT.Copy)\
                    .then_inc(s["Ge"], 1)

            def b_q(n):
                for hf in range(2):
                    cols = slice(hf * INNER // 2, (hf + 1) * INNER // 2)
                    act.wait_ge(s["q"], 2 * n + hf + 1)
                    after(act, s["qss"], 2 * n + hf - 1)
                    act.activation(qsq[:, cols], back[:, cols], ACT.Square).then_inc(s["qs"], 1)

            def b_n(i, tt):
                act.wait_ge(s["qT"], TPB * i + tt + 1)
                if tt == 0:
                    after(act, s["o"], TPB * i)
                act.activation(qT[:, tt, :, :].rearrange("p c n -> p (c n)"), back, ACT.Copy).then_inc(s["qTe"], 1)

            def b_h(i):
                for n in range(4):
                    act.wait_ge(s["h"], 4 * i + n + 1)
                    if n == 0:
                        after(act, s["y"], TPB * i)
                    for c in (2 * n, 2 * n + 1):
                        ins = act.activation(hT[:, c, :], back[:, (c % 4) * S:(c % 4 + 1) * S], ACT.Gelu,
                                             bias=b1[:, c:c + 1])
                    ins.then_inc(s["he"], 1)

            def t_h(n):
                act.wait_ge(s["tT"], n + 1)
                after(act, s["g"], n)
                act.activation(tT[:, :, :], tT_ps, ACT.Copy).then_inc(s["tTe"], 1)

            def t_g(n):
                act.wait_ge(s["g"], n + 1)
                after(act, s["gi"], n)
                act.activation(g[:, :], g_ps, ACT.Gelu, scale=un[:, 0:1]).then_inc(s["ge"], 1)

            def t_gT(n):
                act.wait_ge(s["gT"], n + 1)
                after(act, s["ty"], n)
                act.activation(gT[:, :, :], gT_ps, ACT.Copy).then_inc(s["gTe"], 1)

            def s_wq():
                act.wait_ge(s["wq"], 16)
                act.activation(wq[0][:, :, :].rearrange("p k n -> p (k n)"), wq_f, ACT.Copy).then_inc(s["wqh"], 1)

            parts = {
                "s_wq": s_wq, "f_v": f_v, "f_k": f_k, "f_g0": lambda f: f_g(f, 0), "f_g1": lambda f: f_g(f, 1),
                "b_q0": lambda i: b_q(TPB * i), "b_q1": lambda i: b_q(TPB * i + 1),
                "b_n0": lambda i: b_n(i, 0), "b_n1": lambda i: b_n(i, 1), "b_h": b_h,
                "t0_h": t_h, "t1_h": t_h, "t0_g": t_g, "t1_g": t_g, "t0_gT": t_gT, "t1_gT": t_gT,
            }
            pipeline(act, parts)

        @block.tensor
        def _(pe):
            def transposes(dst, src):
                for tt in range(TPB):
                    for kd in range(KD):
                        ins = pe.transpose(dst[:, kd, tt * P:(tt + 1) * P], src[:, tt, kd * P:(kd + 1) * P], ident[:, :])
                return ins

            def rows(dst, lhsT, w, n):
                for half in range(INNER // 512):
                    for kd in range(KD):
                        ins = pe.matmul(dst[0:n, half * 512:(half + 1) * 512], lhsT(kd),
                                        w[:, kd, half * 512:(half + 1) * 512], start=(kd == 0), stop=(kd == KD - 1))
                return ins

            def f_cT(f):
                pe.wait_ge(s["cn"], f + 1)
                after(pe, s["xTe"], f)
                for kd in range(KD):
                    ins = pe.transpose(cT_ps[:, kd, :], cx[0:SC, kd * P:(kd + 1) * P], ident[0:SC, 0:SC])
                ins.then_inc(s["cT"], 1)

            def f_v(f):
                pe.wait_ge(s["kn"], f + 1)
                rows(front, lambda kd: cT[:, kd, :], wv, SC).then_inc(s["v"], 1)

            def f_k(f):
                pe.wait_ge(s["cTe"], f + 1)
                rows(front, lambda kd: cT[:, kd, :], wk, SC).then_inc(s["k"], 1)

            def f_m(f):
                pe.wait_ge(s["ve"], f + 1)
                for c in range(IK):
                    cols = slice(c * P, (c + 1) * P)
                    ins = pe.matmul(front[:, cols], vv[0:SC, cols], kn[0:SC, cols], start=True, stop=True)
                ins.then_inc(s["M"], 1)

            def f_g(f, h):
                if h == 0:
                    pe.wait_ge(s["Me"], f + 1)
                else:
                    pe.wait_ge(s["Ge"], 2 * f + 1)
                for c in range(4):
                    ins = pe.matmul(front[:, c * D:(c + 1) * D], mT[:, 4 * h + c, :], wo[:, 4 * h + c, :],
                                    start=True, stop=True)
                ins.then_inc(s["G"], 1)

            def f_x(f):
                pe.wait_ge(s["xn"], f + 1)
                pe.wait_ge(s["Ge"], 2 * f + 2)
                transposes(xT_ps, xh).then_inc(s["xT"], 1)

            def b_q(i, tt):
                if tt == 0:
                    pe.wait_ge(s["xTl"], i + 1)
                    after(pe, s["ye"], TPB * i)
                else:
                    pe.wait_ge(s["qTe"], TPB * i + 1)
                for half in range(INNER // 512):
                    cols = slice(half * 512, (half + 1) * 512)
                    for kd in range(KD):
                        for m, (a, b) in enumerate(passes):
                            ins = pe.matmul(back[:, cols], xTs[a][:, kd, tt * P:(tt + 1) * P], wq[b][:, kd, cols],
                                            start=(kd == 0 and m == 0), stop=(kd == KD - 1 and m == 2))
                    ins.then_inc(s["q"], 1)

            def b_n(n):
                for c in range(IK):
                    if c % (IK // 2) == 0:
                        pe.wait_ge(s["qn"], 2 * n + 1 + c // (IK // 2))
                    ins = pe.transpose(back[:, c * P:(c + 1) * P], qn[:, c * P:(c + 1) * P], ident[:, :])
                ins.then_inc(s["qT"], 1)

            def b_o(i):
                pe.wait_ge(s["Ge"], 2 * i + 2)
                after(pe, s["ye"], TPB * i)
                for tt in range(TPB):
                    pe.wait_ge(s["qTe"], TPB * i + tt + 1)
                    for c in range(IK):
                        ins = pe.matmul(attended[tt], qT[:, tt, c, :], gm[:, c, :], start=(c == 0), stop=(c == IK - 1))
                    ins.then_inc(s["o"], 1)

            def b_x(i):
                for tt in range(TPB):
                    pe.wait_ge(s["x2"], TPB * i + tt + 1)
                    for kd in range(KD):
                        ins = pe.transpose(x2T_ps[:, kd, tt * P:(tt + 1) * P], xh2[:, tt, kd * P:(kd + 1) * P], ident[:, :])
                ins.then_inc(s["x2T"], 1)

            def b_h(i):
                pe.wait_ge(s["x2Te"], i + 1)
                for n in range(4):
                    if n >= 2:
                        pe.wait_ge(s["he"], 4 * i + n - 1)
                    for c in (2 * n, 2 * n + 1):
                        for kd in range(KD):
                            ins = pe.matmul(back[:, (c % 4) * S:(c % 4 + 1) * S], w1[:, kd, c * P:(c + 1) * P],
                                            xT2[:, kd, :], start=(kd == 0), stop=(kd == KD - 1))
                    ins.then_inc(s["h"], 1)

            def b_y(i, tt):
                pe.wait_ge(s["he"], 4 * i + 4)
                for c in range(FK):
                    ins = pe.matmul(attended[tt], hT[:, c, tt * P:(tt + 1) * P], w2[:, c, :],
                                    start=(c == 0), stop=(c == FK - 1))
                ins.then_inc(s["y"], 1)

            def t_h(n):
                pe.wait_ge(s["ti"], n + 1)
                after(pe, s["fin"], n)
                for kd in range(KD):
                    ins = pe.transpose(tT_ps[:, kd, :], ti[:, kd * P:(kd + 1) * P], ident16[:, :])
                ins.then_inc(s["tT"], 1)

            def t_g(n):
                pe.wait_ge(s["tTe"], n + 1)
                after(pe, s["ge"], n)
                for hf in range(FF // 512):
                    for kd in range(KD):
                        ins = pe.matmul(g_ps[:, hf * 512:(hf + 1) * 512], tT[:, kd, :],
                                        wb[0][:, kd, hf * 512:(hf + 1) * 512], start=(kd == 0), stop=(kd == KD - 1))
                ins.then_inc(s["g"], 1)

            def t_gT(n):
                pe.wait_ge(s["gi"], n + 1)
                for c in range(FK):
                    ins = pe.transpose(gT_ps[:, c, :], gi[:, c * P:(c + 1) * P], ident16[:, :])
                ins.then_inc(s["gT"], 1)

            def t_y(n):
                pe.wait_ge(s["gTe"], n + 1)
                for c in range(FK):
                    ins = pe.matmul(ty_ps, gT[:, c, :], wb[1][:, c, :], start=(c == 0), stop=(c == FK - 1))
                ins.then_inc(s["ty"], 1)

            def s_wq():
                pe.wait_ge(s["wql"], 1)

            def w_sum():
                pe.wait_ge(s["part"], 1)
                pe.matmul(sum_ps, ones[:, :], part[:, :], start=True, stop=True).then_inc(s["sum"], 1)

            parts = {
                "g_cT": f_cT, "f_v": f_v, "f_k": f_k, "f_m": f_m, "f_g0": lambda f: f_g(f, 0),
                "f_g1": lambda f: f_g(f, 1), "f_x": f_x,
                "b_q0": lambda i: b_q(i, 0), "b_q1": lambda i: b_q(i, 1),
                "b_n0": lambda i: b_n(TPB * i), "b_n1": lambda i: b_n(TPB * i + 1),
                "b_o": b_o, "b_x": b_x, "b_h": b_h, "b_y0": lambda i: b_y(i, 0), "b_y1": lambda i: b_y(i, 1),
                "t0_h": t_h, "t1_h": t_h, "t0_g": t_g, "t1_g": t_g, "t0_gT": t_gT, "t1_gT": t_gT,
                "t0_y": t_y, "t1_y": t_y, "w_sum": w_sum, "s_wq": s_wq,
            }
            pipeline(pe, parts)

        @block.sync
        def _(sp):
            with sp.Fori(0, NT) as i:
                sp.wait_ge(s["fin"], i + 1)
                sp.dma_start(ov[bass.ds(i, 1)].rearrange("a p d -> (a p) d"),
                             x[:, bass.ds(i, 1), :].rearrange("p a d -> p (a d)")).then_inc(s["store"], 16)
            sp.wait_ge(s["store"], 16 * NT)


def _spread(w, src, width, band, copies=3):
    import numpy as np
    w = np.asarray(w)
    o = np.zeros(w.shape[:-1] + (H * band,), w.dtype)
    for h in range(H):
        for c in range(copies):
            o[..., band * h + c * width:band * h + (c + 1) * width] = w[..., h * src:h * src + width]
    return o


def kernel(**inputs):
    import numpy as np
    import concourse.bacc as bacc
    from concourse.bass_utils import run_bass_kernel_spmd

    i = {n: np.ascontiguousarray(a) for n, a in inputs.items()}

    def columns(v):
        return np.ascontiguousarray(v.reshape(-1, P).T)

    def key_bias(v, src, width, band):
        o = _spread(v, src, width, band)
        for h in range(H):
            o[band * h + 3 * width] = 1.0
        return columns(o)

    def low_rows(width, band):
        o = np.zeros((P, 2), np.float32)
        for b in range(0, P, band):
            o[b + 2 * width:b + 3 * width, 0] = 1.0
            o[b + width:b + 2 * width, 1] = 1.0
        return o

    lat = D // 2
    ha, hb = D // H, lat // H
    arrays = {
        "x": i["x"], "ctx": i["ctx_1024"], "g_xattn": i["g_xattn"], "g_ffn": i["g_ffn"],
        "a_wq": _spread(i["L0_xattn_Wq"], ha, ha, 64), "a_bq": columns(_spread(i["L0_xattn_bq"], ha, ha, 64)),
        "a_wk": _spread(i["L0_xattn_Wk"], ha, ha, 64), "a_bk": key_bias(i["L0_xattn_bk"], ha, ha, 64),
        "a_wv": i["L0_xattn_Wv"], "a_bv": i["L0_xattn_bv"], "a_wo": i["L0_xattn_Wo"], "a_bo": i["L0_xattn_bo"],
        "a_low": low_rows(ha, 64), "b_low": low_rows(hb, 32),
        "b_wq": _spread(i["L0_ffn_q_w"], ha, hb, 32), "b_bq": columns(_spread(i["L0_ffn_q_b"], ha, hb, 32)),
        "b_wk": _spread(i["L0_ffn_k_w"], hb, hb, 32), "b_bk": key_bias(i["L0_ffn_k_b"], hb, hb, 32),
        "b_wv": _spread(i["L0_ffn_v_w"], hb, hb, 2 * hb, 2), "b_bv": _spread(i["L0_ffn_v_b"], hb, hb, 2 * hb, 2),
        "b_wo": np.ascontiguousarray(i["L0_ffn_o_w"][:lat]),
        "b_bo": i["L0_ffn_o_b"], "router_w": i["L0_ffn_router_w"], "router_b": i["L0_ffn_router_b"][:, None],
        "moe_w1": i["L0_ffn_w1"], "moe_b1": columns(i["L0_ffn_b1"]).reshape(P, E, -1), "moe_w2": i["L0_ffn_w2"], "moe_b2": i["L0_ffn_b2"],
        "l1_wq": i["L1_xattn_wq"], "l1_wk": i["L1_xattn_wk"], "l1_wv": i["L1_xattn_wv"], "l1_wo": i["L1_xattn_wo"],
        "l1_bo": i["L1_xattn_bo"], "l1_w1": i["L1_xattn_w1"], "l1_b1": columns(i["L1_xattn_b1"]),
        "l1_w2": i["L1_xattn_w2"], "l1_b2": i["L1_xattn_b2"],
        "l1_ln": np.ascontiguousarray(np.stack([i["L1_xattn_" + n].reshape(KD, P).T for n in
                                                ("ln1_g", "ln1_b", "ln2_g", "ln2_b")], axis=1)),
        "ff_w1t": np.ascontiguousarray(i["L1_ffn_w1"].T), "ff_w2t": np.ascontiguousarray(i["L1_ffn_w2"].T),
    }
    nc = bacc.Bacc("TRN2", target_bir_lowering=False, num_devices=1)
    t = {n: nc.dram_tensor(f"in_{n}", a.shape, mybir.dt.from_np(a.dtype), kind="ExternalInput").ap()
         for n, a in arrays.items()}
    out = nc.dram_tensor("out", (B, S, D), F32, kind="ExternalOutput").ap()
    program(nc, t, out)
    r = run_bass_kernel_spmd(nc, [{f"in_{n}": a for n, a in arrays.items()}], core_ids=[0])
    return r.results[0]["out"]
```
